# Optimizing a Trainium2 kernel written in Bass

```python
import numpy as np
import jax
import jax.numpy as jnp

def _softmax(x, axis=-1):
    return jax.nn.softmax(x, axis=axis)

def _gelu(x):
    return jax.nn.gelu(x, approximate=True)

def _silu(x):
    return jax.nn.silu(x)

def _sigmoid(x):
    return jax.nn.sigmoid(x)

def _layernorm(x, axis=-1, eps=1e-05):
    m = jnp.mean(x, axis=axis, keepdims=True)
    v = jnp.var(x, axis=axis, keepdims=True)
    return (x - m) / jnp.sqrt(v + eps)

def _scatter_add(tgt, idx, src, axis=0):
    return tgt.at[idx].add(src)

def _segment_sum(src, seg, n):
    return jax.ops.segment_sum(src, seg, n)
kernel_name = 'mk_decoder_postln_d1_seqx_r4_30d2fc'

def setup_inputs(seed: int=0):
    np.random.seed(seed)
    _w = jnp.asarray

    def _rec_inputs():
        import jax
        import jax.numpy as jnp
        _rk = jax.random.key(seed)
        x = -0.0003929 + 0.9999 * jax.random.normal(jax.random.fold_in(_rk, 1), (64, 128, 256), jnp.float32)
        _lenS = 128 - jax.random.randint(jax.random.fold_in(_rk, 7), (64,), 0, max(1, 128 // 4) + 1, jnp.int32)
        _lenS2 = 128 - jax.random.randint(jax.random.fold_in(_rk, 8), (64,), 0, max(1, 128 // 4) + 1, jnp.int32)
        _ctx_1024P = jax.random.normal(jax.random.fold_in(_rk, 11), (64, 16, 256), jnp.float32)
        _ctx_1024c = jax.random.dirichlet(jax.random.fold_in(_rk, 511), 0.3 * jnp.ones((16,), jnp.float32), (64, 128))
        _ctx_1024t = jnp.einsum('bsk,bkd->bsd', _ctx_1024c, _ctx_1024P)
        _ctx_1024t = _ctx_1024t * jax.lax.rsqrt(jnp.mean(jnp.square(_ctx_1024t)) + 1e-12) * 0.953939
        ctx_1024 = 4.13588e-05 + 0.999923 * (_ctx_1024t + 0.3 * jax.random.normal(jax.random.fold_in(_rk, 611), (64, 128, 256), jnp.float32))
        return (x, ctx_1024)
    x, ctx_1024 = _rec_inputs()

    def _L0_attn_setup():
        import jax, jax.numpy as jnp
        import numpy as np
        B, T, D = (4, 512, 256)
        N_HEADS = 16
        HEAD_DIM = D // N_HEADS

        def rope(x):
            t, dh = (x.shape[-2], x.shape[-1])
            half = dh // 2
            theta = 1.0 / 10000.0 ** (jnp.arange(half, dtype=jnp.float32) / half)
            ang = jnp.arange(t, dtype=jnp.float32)[:, None] * theta[None, :]
            sin, cos = (jnp.sin(ang), jnp.cos(ang))
            x1 = x[..., 0::2]
            x2 = x[..., 1::2]
            return jnp.concatenate([x1 * cos - x2 * sin, x1 * sin + x2 * cos], axis=-1)
        key = jax.random.key(seed)
        ks = jax.random.split(key, 9)
        s = 0.02
        return {'x': jax.random.normal(ks[0], (B, T, D), dtype=jnp.float32), 'W_q': jax.random.normal(ks[1], (D, D), dtype=jnp.float32) * s, 'b_q': jnp.zeros((D,), dtype=jnp.float32), 'W_k': jax.random.normal(ks[2], (D, D), dtype=jnp.float32) * s, 'b_k': jnp.zeros((D,), dtype=jnp.float32), 'W_v': jax.random.normal(ks[3], (D, D), dtype=jnp.float32) * s, 'b_v': jnp.zeros((D,), dtype=jnp.float32), 'W_o': jax.random.normal(ks[4], (D, D), dtype=jnp.float32) * s, 'b_o': jnp.zeros((D,), dtype=jnp.float32)}
    _L0_attn_all = _L0_attn_setup()
    _L0_attn_in = {k: v for k, v in _L0_attn_all.items() if k in ('W_q', 'b_q', 'W_k', 'b_k', 'W_v', 'b_v', 'W_o', 'b_o')}
    del _L0_attn_all

    def _L0_xattn_setup():
        import jax, jax.numpy as jnp
        import numpy as np
        H = 256
        B = 8
        L_CHAR = 512
        L_SUB = 256

        def _linear(x, W, b):
            return jnp.einsum('blh,oh->blo', x, W) + b

        def _interp_linear(x, out_len):
            L_in = x.shape[1]
            pos = (jnp.arange(out_len, dtype=x.dtype) + 0.5) * (L_in / out_len) - 0.5
            pos = jnp.clip(pos, 0.0, L_in - 1)
            lo = jnp.floor(pos).astype(jnp.int32)
            hi = jnp.minimum(lo + 1, L_in - 1)
            w = (pos - lo.astype(x.dtype))[None, :, None]
            return x[:, lo] * (1 - w) + x[:, hi] * w
        key = jax.random.key(seed)
        ks = jax.random.split(key, 18)
        s = 0.02
        inp = {'char_emb': jax.random.normal(ks[0], (B, L_CHAR, H), jnp.float32), 'subword_emb': jax.random.normal(ks[1], (B, L_SUB, H), jnp.float32)}
        names = ['Wq_c', 'Wk_s', 'Wv_s', 'Wq_s', 'Wk_c', 'Wv_c']
        for i, n in enumerate(names):
            inp[n] = jax.random.normal(ks[2 + 2 * i], (H, H), jnp.float32) * s
            inp['b' + n[1:]] = jax.random.normal(ks[3 + 2 * i], (H,), jnp.float32) * s
        inp['Wg'] = jax.random.normal(ks[14], (H, 2 * H), jnp.float32) * s
        inp['bg'] = jax.random.normal(ks[15], (H,), jnp.float32) * s
        return inp
    _L0_xattn_all = _L0_xattn_setup()
    _L0_xattn_in = {k: v for k, v in _L0_xattn_all.items() if k in ('Wq_c', 'bq_c', 'Wk_s', 'bk_s', 'Wv_s', 'bv_s', 'Wq_s', 'bq_s', 'Wk_c', 'bk_c', 'Wv_c', 'bv_c', 'Wg', 'bg')}
    del _L0_xattn_all

    def _L0_ffn_setup():
        import jax, jax.numpy as jnp
        import numpy as np
        import math
        B, L, D = (4, 1024, 256)
        F = 1024
        E = 16
        CAP_FACTOR = 1.0
        EPS = 1e-05
        key = jax.random.key(seed)
        ks = jax.random.split(key, 8)
        std = 0.02
        return {'x': jax.random.normal(ks[0], (B, L, D), dtype=jnp.float32), 'norm_weight': jnp.ones((D,), dtype=jnp.float32), 'router_weight': jax.random.normal(ks[1], (E, D), dtype=jnp.float32) * std, 'router_bias': jnp.zeros((E,), dtype=jnp.float32), 'fc1_weight': jax.random.normal(ks[2], (E, F, D), dtype=jnp.float32) * std, 'fc1_bias': jnp.zeros((E, F), dtype=jnp.float32), 'fc2_weight': jax.random.normal(ks[3], (E, D, F), dtype=jnp.float32) * std, 'fc2_bias': jnp.zeros((E, D), dtype=jnp.float32)}
    _L0_ffn_all = _L0_ffn_setup()
    _L0_ffn_in = {k: v for k, v in _L0_ffn_all.items() if k in ('norm_weight', 'router_weight', 'router_bias', 'fc1_weight', 'fc1_bias', 'fc2_weight', 'fc2_bias')}
    del _L0_ffn_all
    return {'x': x, 'ctx_1024': ctx_1024, 'L0_attn_W_q': _L0_attn_in['W_q'], 'L0_attn_b_q': _L0_attn_in['b_q'], 'L0_attn_W_k': _L0_attn_in['W_k'], 'L0_attn_b_k': _L0_attn_in['b_k'], 'L0_attn_W_v': _L0_attn_in['W_v'], 'L0_attn_b_v': _L0_attn_in['b_v'], 'L0_attn_W_o': _L0_attn_in['W_o'], 'L0_attn_b_o': _L0_attn_in['b_o'], 'L0_xattn_Wq_c': _L0_xattn_in['Wq_c'], 'L0_xattn_bq_c': _L0_xattn_in['bq_c'], 'L0_xattn_Wk_s': _L0_xattn_in['Wk_s'], 'L0_xattn_bk_s': _L0_xattn_in['bk_s'], 'L0_xattn_Wv_s': _L0_xattn_in['Wv_s'], 'L0_xattn_bv_s': _L0_xattn_in['bv_s'], 'L0_xattn_Wq_s': _L0_xattn_in['Wq_s'], 'L0_xattn_bq_s': _L0_xattn_in['bq_s'], 'L0_xattn_Wk_c': _L0_xattn_in['Wk_c'], 'L0_xattn_bk_c': _L0_xattn_in['bk_c'], 'L0_xattn_Wv_c': _L0_xattn_in['Wv_c'], 'L0_xattn_bv_c': _L0_xattn_in['bv_c'], 'L0_xattn_Wg': _L0_xattn_in['Wg'], 'L0_xattn_bg': _L0_xattn_in['bg'], 'L0_ffn_norm_weight': _L0_ffn_in['norm_weight'], 'L0_ffn_router_weight': _L0_ffn_in['router_weight'], 'L0_ffn_router_bias': _L0_ffn_in['router_bias'], 'L0_ffn_fc1_weight': _L0_ffn_in['fc1_weight'], 'L0_ffn_fc1_bias': _L0_ffn_in['fc1_bias'], 'L0_ffn_fc2_weight': _L0_ffn_in['fc2_weight'], 'L0_ffn_fc2_bias': _L0_ffn_in['fc2_bias']}

def reference(x, ctx_1024, L0_attn_W_q, L0_attn_b_q, L0_attn_W_k, L0_attn_b_k, L0_attn_W_v, L0_attn_b_v, L0_attn_W_o, L0_attn_b_o, L0_xattn_Wq_c, L0_xattn_bq_c, L0_xattn_Wk_s, L0_xattn_bk_s, L0_xattn_Wv_s, L0_xattn_bv_s, L0_xattn_Wq_s, L0_xattn_bq_s, L0_xattn_Wk_c, L0_xattn_bk_c, L0_xattn_Wv_c, L0_xattn_bv_c, L0_xattn_Wg, L0_xattn_bg, L0_ffn_norm_weight, L0_ffn_router_weight, L0_ffn_router_bias, L0_ffn_fc1_weight, L0_ffn_fc1_bias, L0_ffn_fc2_weight, L0_ffn_fc2_bias):
    import jax
    import jax.numpy as jnp

    def _L0_attn_ref(x, W_q, b_q, W_k, b_k, W_v, b_v, W_o, b_o):
        import jax, jax.numpy as jnp
        import numpy as np
        B, T, D = (4, 512, 256)
        N_HEADS = 16
        HEAD_DIM = D // N_HEADS

        def rope(x):
            t, dh = (x.shape[-2], x.shape[-1])
            half = dh // 2
            theta = 1.0 / 10000.0 ** (jnp.arange(half, dtype=jnp.float32) / half)
            ang = jnp.arange(t, dtype=jnp.float32)[:, None] * theta[None, :]
            sin, cos = (jnp.sin(ang), jnp.cos(ang))
            x1 = x[..., 0::2]
            x2 = x[..., 1::2]
            return jnp.concatenate([x1 * cos - x2 * sin, x1 * sin + x2 * cos], axis=-1)
        b, t, d = x.shape
        h, dh = (N_HEADS, d // N_HEADS)

        def heads(y):
            return y.reshape(b, t, h, dh).transpose(0, 2, 1, 3)
        q = rope(heads(x @ W_q.T + b_q))
        k = rope(heads(x @ W_k.T + b_k))
        v = heads(x @ W_v.T + b_v)
        scores = jnp.einsum('bhtd,bhsd->bhts', q, k)
        causal = jnp.tril(jnp.ones((t, t), dtype=bool))
        mask = jnp.where(causal, 0.0, -jnp.inf)
        probs = jax.nn.softmax((scores + mask) / jnp.sqrt(jnp.float32(dh)), axis=-1)
        out = jnp.einsum('bhts,bhsd->bhtd', probs, v)
        out = out.transpose(0, 2, 1, 3).reshape(b, t, d)
        return out @ W_o.T + b_o

    def _L0_xattn_ref(char_emb, subword_emb, Wq_c, bq_c, Wk_s, bk_s, Wv_s, bv_s, Wq_s, bq_s, Wk_c, bk_c, Wv_c, bv_c, Wg, bg):
        import jax, jax.numpy as jnp
        import numpy as np
        H = 256
        B = 8
        L_CHAR = 512
        L_SUB = 256

        def _linear(x, W, b):
            return jnp.einsum('blh,oh->blo', x, W) + b

        def _interp_linear(x, out_len):
            L_in = x.shape[1]
            pos = (jnp.arange(out_len, dtype=x.dtype) + 0.5) * (L_in / out_len) - 0.5
            pos = jnp.clip(pos, 0.0, L_in - 1)
            lo = jnp.floor(pos).astype(jnp.int32)
            hi = jnp.minimum(lo + 1, L_in - 1)
            w = (pos - lo.astype(x.dtype))[None, :, None]
            return x[:, lo] * (1 - w) + x[:, hi] * w
        h = char_emb.shape[-1]
        scale = 1.0 / jnp.sqrt(jnp.asarray(h, char_emb.dtype))
        Q_char = _linear(char_emb, Wq_c, bq_c)
        K_sub = _linear(subword_emb, Wk_s, bk_s)
        V_sub = _linear(subword_emb, Wv_s, bv_s)
        scores = jnp.einsum('bqh,bkh->bqk', Q_char, K_sub) * scale
        char2sub = jnp.einsum('bqk,bkh->bqh', jax.nn.softmax(scores, axis=-1), V_sub)
        Q_sub = _linear(subword_emb, Wq_s, bq_s)
        K_char = _linear(char_emb, Wk_c, bk_c)
        V_char = _linear(char_emb, Wv_c, bv_c)
        scores2 = jnp.einsum('bqh,bkh->bqk', Q_sub, K_char) * scale
        sub2char = jnp.einsum('bqk,bkh->bqh', jax.nn.softmax(scores2, axis=-1), V_char)
        L_char = char_emb.shape[1]
        if sub2char.shape[1] != L_char:
            sub2char = _interp_linear(sub2char, L_char)
        gate_in = jnp.concatenate([char2sub, sub2char], axis=-1)
        gate = jax.nn.sigmoid(jnp.einsum('blh,oh->blo', gate_in, Wg) + bg)
        return gate * char2sub + (1 - gate) * sub2char

    def _L0_ffn_ref(x, norm_weight, router_weight, router_bias, fc1_weight, fc1_bias, fc2_weight, fc2_bias):
        import jax, jax.numpy as jnp
        import numpy as np
        import math
        B, L, D = (4, 1024, 256)
        F = 1024
        E = 16
        CAP_FACTOR = 1.0
        EPS = 1e-05
        b, l, d = x.shape
        n_tokens = b * l
        n_experts = router_weight.shape[0]
        capacity = max(1, math.ceil(CAP_FACTOR * n_tokens / n_experts))
        top_k = min(capacity, n_tokens)
        xf = x.reshape(n_tokens, d)
        rms = jnp.sqrt(jnp.mean(xf * xf, axis=-1, keepdims=True) + EPS)
        xn = xf / rms * norm_weight
        logits = xn @ router_weight.T + router_bias
        probs = jax.nn.softmax(logits, axis=-1)
        _, idx = jax.lax.top_k(logits.T, top_k)
        xe = xn[idx]
        h = jnp.einsum('ecd,efd->ecf', xe, fc1_weight) + fc1_bias[:, None, :]
        h = jax.nn.gelu(h, approximate=False)
        y = jnp.einsum('ecf,edf->ecd', h, fc2_weight) + fc2_bias[:, None, :]
        gates = jnp.take_along_axis(probs.T, idx, axis=1)
        flat_idx = idx.reshape(-1)
        contrib = (y * gates[:, :, None]).reshape(-1, d)
        output = jnp.zeros((n_tokens, d), dtype=x.dtype).at[flat_idx].add(contrib)
        gate_sums = jnp.zeros((n_tokens, 1), dtype=x.dtype).at[flat_idx].add(gates.reshape(-1, 1))
        assigned = gate_sums > 0
        output = jnp.where(assigned, output / jnp.where(assigned, gate_sums, 1.0), output)
        return output.reshape(b, l, d)
    x = _layernorm(x + _L0_attn_ref(x, L0_attn_W_q, L0_attn_b_q, L0_attn_W_k, L0_attn_b_k, L0_attn_W_v, L0_attn_b_v, L0_attn_W_o, L0_attn_b_o), axis=-1)
    x = _layernorm(x + _L0_xattn_ref(x, ctx_1024, L0_xattn_Wq_c, L0_xattn_bq_c, L0_xattn_Wk_s, L0_xattn_bk_s, L0_xattn_Wv_s, L0_xattn_bv_s, L0_xattn_Wq_s, L0_xattn_bq_s, L0_xattn_Wk_c, L0_xattn_bk_c, L0_xattn_Wv_c, L0_xattn_bv_c, L0_xattn_Wg, L0_xattn_bg), axis=-1)
    x = _layernorm(x + _L0_ffn_ref(x, L0_ffn_norm_weight, L0_ffn_router_weight, L0_ffn_router_bias, L0_ffn_fc1_weight, L0_ffn_fc1_bias, L0_ffn_fc2_weight, L0_ffn_fc2_bias), axis=-1)
    return x

_drawn_inputs = setup_inputs


def setup_inputs(seed=0):
    import zlib

    import numpy as np

    out = dict(_drawn_inputs(seed))
    spreads = {'L0_attn_b_q': (0.0, 0.8),
     'L0_attn_b_k': (0.0, 0.8),
     'L0_attn_b_v': (0.0, 0.1),
     'L0_attn_b_o': (0.0, 0.1),
     'L0_ffn_norm_weight': (1.0, 0.2),
     'L0_ffn_router_bias': (0.0, 2.0),
     'L0_ffn_fc1_bias': (0.0, 0.322),
     'L0_ffn_fc2_bias': (0.0, 0.1)}
    factors = {'L0_attn_W_q': 8.0,
     'L0_attn_W_k': 8.0,
     'L0_xattn_Wq_c': 6.799,
     'L0_xattn_bq_c': 8.0,
     'L0_xattn_Wk_s': 6.925,
     'L0_xattn_bk_s': 64.0,
     'L0_xattn_bv_s': 5.092,
     'L0_xattn_Wq_s': 8.0,
     'L0_xattn_bq_s': 8.0,
     'L0_xattn_Wk_c': 8.0,
     'L0_xattn_bk_c': 64.0,
     'L0_xattn_bv_c': 5.005,
     'L0_xattn_Wg': 8.0,
     'L0_xattn_bg': 8.0}
    for name, (base, spread) in spreads.items():
        noise = np.random.default_rng([zlib.crc32(name.encode()), seed]).standard_normal(out[name].shape)
        drawn = base * np.exp(spread * noise) if base else spread * noise
        out[name] = jnp.asarray(drawn.astype(out[name].dtype))
    for name, factor in factors.items():
        out[name] = (out[name] * factor).astype(out[name].dtype)
    return out
```

```python
from contextlib import ExitStack

import concourse.bass as bass
from concourse import mybir

F32 = mybir.dt.float32
F32R = mybir.dt.float32r
BF16 = mybir.dt.bfloat16
I32 = mybir.dt.int32
ALU = mybir.AluOpType
ACT = mybir.ActivationFunctionType
AX_X = mybir.AxisListType.X

P = 128
B = 64
T = 128
D = 256
DC = D // P
H = 16
HD = D // H
N = B * T
G = 2
NG = B // G
GT = G * T
E = 16
F = 1024
FC = F // P
CAP = N // E
ROW = D + E
EPS = 1e-5
QT = CAP // P
SLOT_LO = 32
SLOT_HI = CAP // SLOT_LO
MASKED = -1e30
UNITS = 4
HU = H // UNITS
CHUNKS = P // E
CHUNK = N // CHUNKS
PASSES = ((0, 0), (0, 1), (1, 0))

QC, KC, KS, QS = 0, 1, 2, 3


def need(engine, semaphore, value):
    if isinstance(value, int) and value <= 0:
        return
    engine.wait_ge(semaphore, value)


def decoder_attention(nc, d, x2_dram, rows_dram, logits_dram, acc_dram, probs):
    with ExitStack() as ctx:
        def sb(name, shape, dt=F32):
            return ctx.enter_context(nc.sbuf_tensor(name, shape, dt))

        def sem(name):
            return ctx.enter_context(nc.semaphore(name))

        wqk = sb("wqk", [P, 2, DC, 2 * D], F32R)
        wv = sb("wv", [P, 2, DC, D], F32R)
        wo = sb("wo", [P, 2, DC, D], F32R)
        wx = sb("wx", [P, 2, 4, DC, D], F32R)
        wxv = sb("wxv", [P, 2, 2, DC, D], F32R)
        wg = sb("wg", [P, 2, 2 * DC, D], F32R)
        wr = sb("wr", [P, DC, E])
        WCOLS = DC * (2 * D + D + D + 4 * D + 2 * D + 2 * D)
        shared = sb("shared", [P, WCOLS])
        feat = shared[:, 0:8 * GT].rearrange("p (k c t) -> p k c t", k=4, c=DC)
        values = shared[:, 8 * GT:8 * GT + G * 2 * D].rearrange("p (g n) -> p g n", g=G)
        bqkv = sb("bqkv", [P, 3 * D])
        bo = sb("bo", [P, D])
        bxv = sb("bxv", [P, 2 * D])
        bg = sb("bg", [P, D])
        nw = sb("nw", [P, D])
        br = sb("br", [P, E])
        bx = sb("bx", [P, 4, DC])
        br_col = sb("br_col", [E, 1])
        rope_cos = sb("rope_cos", [P, 2 * H, HD // 2])
        rope_sin = sb("rope_sin", [P, 2 * H, HD // 2])
        ident = sb("ident", [P, P])
        ident_bf = sb("ident_bf", [P, P], BF16)
        mask = sb("mask", [P, HU, T], BF16)
        minus_half = sb("minus_half", [P, 1])
        eps_col = sb("eps_col", [P, 1])
        pool_pad = sb("pool_pad", [1, 1])
        dve_pad = sb("dve_pad", [1, 1])
        zero_tile = sb("zero_tile", [P, D])
        xT_raw = sb("xT_raw", [P, DC, GT])
        cT_raw = sb("cT_raw", [P, DC, GT])
        xT = sb("xT", [P, 2, DC, GT], F32R)
        cT = sb("cT", [P, 2, DC, GT], F32R)
        xb = sb("xb", [P, G, D])
        qkb = sb("qkb", [P, 2, 2 * D])
        by_cos = sb("by_cos", [P, 2 * H, 2, HD // 2])
        by_sin = sb("by_sin", [P, 2 * H, 2, HD // 2])
        roped = sb("roped", [P, 2, 2 * D])
        qkT = sb("qkT", [P, 2, 2, 2 * DC, T], F32R)
        kblock = sb("kblock", [P, 2, DC, H // DC, T], F32R)
        v_aug = sb("v_aug", [P, G, H, 2 * HD])
        nmax = sb("nmax", [P, 8, HU])
        probs_a = sb("probs_a", [P, 4, HU, T])
        probs_T = sb("probs_T", [P, 2, HU, T])
        outT = sb("outT", [P, 2, UNITS, T])
        rec = sb("rec", [P, 2, H])
        heads = sb("heads", [P, 2, D])
        headsT = sb("headsT", [P, 2, 2, DC, T], F32R)
        pre1 = sb("pre1", [P, 2, D])
        stats = sb("stats", [P, 2, 6])
        mv1 = sb("mv1", [P, 2, 2])
        rstd1 = sb("rstd1", [P, 2, 1])
        x1 = sb("x1", [P, G, D])
        x1T = sb("x1T", [P, 2, DC, GT], F32R)
        xnmax = sb("xnmax", [P, 2, 2])
        xbias = sb("xbias", [P, 2, 2])
        xsum = sb("xsum", [P, 2, 2])
        xrec = sb("xrec", [P, 2, 2])
        xprobs = sb("xprobs", [P, 2, 2, T])
        xprobs_T = sb("xprobs_T", [P, 2, 2, T])
        mixed = sb("mixed", [P, 2, 2, D])
        mixedT = sb("mixedT", [P, 2, 2, 2 * DC, T], F32R)
        diff = sb("diff", [P, 2, D])
        base = sb("base", [P, 2, D])
        gate_z = sb("gate_z", [P, 2, D])
        pre2 = sb("pre2", [P, 2, D])
        mv2 = sb("mv2", [P, 2, 2])
        rstd2 = sb("rstd2", [P, 2, 1])
        x2 = sb("x2", [P, 2, D])
        square = sb("square", [P, D], BF16)
        sumsq = sb("sumsq", [P, 2, 1])
        rrms = sb("rrms", [P, 2, 1])
        row = sb("row", [P, 2, ROW])
        xnT = sb("xnT", [P, DC, GT])
        lg = sb("lg", [P, E])
        lmax = sb("lmax", [P, 1])
        lexp = sb("lexp", [P, 2, E])
        lsum = sb("lsum", [P, 2, 1])
        lrec = sb("lrec", [P, 1])
        lgT = sb("lgT", [E, GT])

        bank = [ctx.enter_context(nc.psum_tensor(f"bank{k}", [P, 512], F32)) for k in range(8)]

        w_loaded = sem("w_loaded")
        w_high = sem("w_high")
        w_ready = sem("w_ready")
        consts = sem("consts")
        pool_step = sem("pool_step")
        xT_loaded = sem("xT_loaded")
        cT_loaded = sem("cT_loaded")
        x_loaded = sem("x_loaded")
        high_made = sem("high_made")
        xT_ready = sem("xT_ready")
        cT_ready = sem("cT_ready")
        xb_ready = sem("xb_ready")
        qk_done = sem("qk_done")
        v_done = sem("v_done")
        qkb_ready = sem("qkb_ready")
        v_ready = sem("v_ready")
        rope_products = sem("rope_products")
        rope_ready = sem("rope_ready")
        qkT_done = sem("qkT_done")
        qkT_high = sem("qkT_high")
        qkT_ready = sem("qkT_ready")
        kblock_ready = [sem(f"kblock_ready{c}") for c in range(DC)]
        scores_ready = sem("scores_ready")
        max_ready = sem("max_ready")
        probs_ready = sem("probs_ready")
        probsT_done = sem("probsT_done")
        probsT_ready = sem("probsT_ready")
        av_done = sem("av_done")
        outT_ready = sem("outT_ready")
        out_done = sem("out_done")
        rec_ready = sem("rec_ready")
        heads_ready = sem("heads_ready")
        headsT_done = sem("headsT_done")
        headsT_high = sem("headsT_high")
        headsT_ready = sem("headsT_ready")
        wo_done = sem("wo_done")
        pre1_ready = sem("pre1_ready")
        stats1 = sem("stats1")
        var1_ready = sem("var1_ready")
        pool1 = sem("pool1")
        rstd1_ready = sem("rstd1_ready")
        x1_ready = sem("x1_ready")
        x1T_done = sem("x1T_done")
        x1T_high = sem("x1T_high")
        x1T_ready = sem("x1T_ready")
        feat_done = sem("feat_done")
        feat_act = sem("feat_act")
        feat_dve = sem("feat_dve")
        xv_done = sem("xv_done")
        xv_ready = sem("xv_ready")
        xscores_done = sem("xscores_done")
        xmax_made = sem("xmax_made")
        xmax_ready = sem("xmax_ready")
        xprobs_ready = sem("xprobs_ready")
        xrec_ready = sem("xrec_ready")
        xprobsT_done = sem("xprobsT_done")
        xprobsT_ready = sem("xprobsT_ready")
        xav_done = sem("xav_done")
        mixed_ready = sem("mixed_ready")
        mixedT_done = sem("mixedT_done")
        mixedT_high = sem("mixedT_high")
        mixedT_ready = sem("mixedT_ready")
        base_ready = sem("base_ready")
        gate_done = sem("gate_done")
        gate_z_ready = sem("gate_z_ready")
        gate_t_ready = sem("gate_t_ready")
        dve_step = sem("dve_step")
        var2_ready = sem("var2_ready")
        pool2 = sem("pool2")
        rstd2_ready = sem("rstd2_ready")
        x2_ready = sem("x2_ready")
        sumsq_ready = sem("sumsq_ready")
        pool3 = sem("pool3")
        rrms_ready = sem("rrms_ready")
        xn_ready = sem("xn_ready")
        xnT_done = sem("xnT_done")
        xnT_ready = sem("xnT_ready")
        lg_done = sem("lg_done")
        lg_step = sem("lg_step")
        lexp_ready = sem("lexp_ready")
        row_ready = sem("row_ready")
        lgT_done = sem("lgT_done")
        lgT_ready = sem("lgT_ready")
        x2_stored = [sem(f"x2_stored{j}") for j in range(G)]
        row_stored = [sem(f"row_stored{j}") for j in range(G)]
        lgT_stored = sem("lgT_stored")
        acc_zeroed = sem("acc_zeroed")

        def loop(engine, group):
            group(0)
            with engine.Fori(1, NG) as i:
                group(i)

        def hold_dve(dve):
            dve.memset(dve_pad[:], 0.0)

        def hold_pool(pool):
            pool.tensor_tensor(pool_pad[:], eps_col[0:1, :], eps_col[0:1, :], ALU.add)

        block = ctx.enter_context(nc.Block())

        W_PARTS = ((wqk, d["wqk"]), (wv, d["wv"]), (wo, d["wo"]), (wx, d["wx"]), (wxv, d["wxv"]), (wg, d["wg"]))
        CONST_LOADS = ((bqkv, "bqkv"), (bo, "bo"), (bxv, "bxv"), (bg, "bg"), (nw, "nw"), (br, "br"), (bx, "bx"),
                       (br_col, "br_col"), (rope_cos, "rope_cos"), (rope_sin, "rope_sin"), (wr, "wr"))
        N_CONST = 16 * (len(W_PARTS) + len(CONST_LOADS))

        def weight_pieces():
            at = 0
            for tile, src in W_PARTS:
                cols = tile.shape
                width = 1
                for s in cols[2:]:
                    width *= s
                yield tile, src, at, width
                at += width

        def flat(ap):
            names = "abcd"[:len(ap.shape) - 1]
            if len(names) == 1:
                return ap
            return ap.rearrange(f"p {' '.join(names)} -> p ({' '.join(names)})")

        @block.sync
        def _(sp):
            for tile, src, at, width in weight_pieces():
                sp.dma_start(shared[:, at:at + width], src).then_inc(w_loaded, 16)
            for tile, name in CONST_LOADS:
                sp.dma_start(tile[:], d[name]).then_inc(w_loaded, 16)

            def group(i):
                need(sp, xT_ready, i)
                sp.dma_start(xT_raw[:], d["xT"][:, :, bass.ts(i, GT)]).then_inc(xT_loaded, 16)
                need(sp, cT_ready, i)
                sp.dma_start(cT_raw[:], d["cT"][:, :, bass.ts(i, GT)]).then_inc(cT_loaded, 16)
                need(sp, pre1_ready, G * i)
                sp.dma_start(xb[:], d["x"][:, bass.ts(i, G), :]).then_inc(x_loaded, 16)
                if isinstance(i, int):
                    sp.wait_ge(consts, 1)
                sp.dma_start(acc_dram[:, bass.ts(i, G), :], zero_tile[:].unsqueeze(1).to_broadcast([P, G, D])).then_inc(acc_zeroed, 16)
                for j in range(G):
                    n = G * i + j
                    need(sp, qkT_ready, n + 1)
                    for c in range(DC):
                        need(sp, scores_ready, UNITS * (n - 1) + UNITS // DC * (c + 1))
                        for h in range(H // DC):
                            rows = slice(HD * h, HD * (h + 1))
                            sp.dma_start(kblock[rows, :, c, h, :].bitcast(F32), qkT[rows, j, :, DC + c, :].bitcast(F32)).then_inc(kblock_ready[c], 16)
            loop(sp, group)
            sp.wait_ge(acc_zeroed, 16 * NG)

        @block.gpsimd
        def _(pool):
            pool.memset(zero_tile[:], 0.0).then_inc(consts, 1)
            pool.memset(minus_half[:], -0.5).then_inc(consts, 1)
            pool.memset(eps_col[:], EPS).then_inc(consts, 1)
            pool.memset(ident[:], 0.0).then_inc(pool_step, 1)
            pool.memset(ident_bf[:], 0.0).then_inc(pool_step, 1)
            pool.memset(mask[:], 0.0).then_inc(pool_step, 1)
            pool.memset(v_aug[:], 0.0).then_inc(pool_step, 1)
            pool.wait_ge(pool_step, 4)
            for t in (ident, ident_bf):
                pool.affine_select(out=t[:], in_=t[:], compare_op=ALU.not_equal, fill=1.0, base=0,
                                   pattern=[[-1, P]], channel_multiplier=1).then_inc(consts, 1)
            pool.affine_select(out=mask[:], in_=mask[:], compare_op=ALU.is_ge, fill=MASKED, base=0,
                               pattern=[[0, HU], [-1, T]], channel_multiplier=1).then_inc(consts, 1)
            pool.memset(v_aug[:, :, :, HD:HD + 1], 1.0).then_inc(consts, 1)
            pool.memset(kblock[:].bitcast(F32), 0.0).then_inc(consts, 1)
            pool.wait_ge(w_loaded, N_CONST)

            def group(i):
                need(pool, xT_loaded, 16 * (i + 1))
                need(pool, v_done, G * i)
                hold_pool(pool)
                pool.tensor_copy(xT[:, 0], xT_raw[:]).then_inc(high_made, 1)
                pool.wait_ge(high_made, 2 * i + 1)
                pool.tensor_tensor(xT[:, 1], xT_raw[:], xT[:, 0].bitcast(F32), ALU.subtract).then_inc(xT_ready, 1)
                need(pool, cT_loaded, 16 * (i + 1))
                need(pool, xv_done, G * i)
                hold_pool(pool)
                pool.tensor_copy(cT[:, 0], cT_raw[:]).then_inc(high_made, 1)
                pool.wait_ge(high_made, 2 * i + 2)
                pool.tensor_tensor(cT[:, 1], cT_raw[:], cT[:, 0].bitcast(F32), ALU.subtract).then_inc(cT_ready, 1)
                for j in range(G):
                    n = G * i + j
                    need(pool, qkb_ready, n + 1)
                    v = qkb[:, j].rearrange("p (h two k) -> p h two k", two=2, k=HD // 2)
                    both = [P, 2 * H, 2, HD // 2]
                    need(pool, rope_ready, n)
                    pool.tensor_tensor(by_cos[:], v, rope_cos[:].unsqueeze(2).to_broadcast(both), ALU.mult).then_inc(rope_products, 1)
                    pool.tensor_tensor(by_sin[:], v, rope_sin[:].unsqueeze(2).to_broadcast(both), ALU.mult).then_inc(rope_products, 1)
                    need(pool, qkT_done, n - 1)
                    pool.wait_ge(rope_products, 2 * n + 2)
                    r = roped[:, j].rearrange("p (h two k) -> p h two k", two=2, k=HD // 2)
                    pool.tensor_tensor(r[:, :, 0], by_cos[:, :, 0], by_sin[:, :, 1], ALU.subtract)
                    pool.tensor_tensor(r[:, :, 1], by_sin[:, :, 0], by_cos[:, :, 1], ALU.add).then_inc(rope_ready, 1)
                need(pool, x_loaded, 16 * (i + 1))
                for j in range(G):
                    pool.tensor_tensor(xb[:, j], xb[:, j], bo[:], ALU.add).then_inc(xb_ready, 1)
                for j in range(G):
                    n = G * i + j
                    need(pool, var1_ready, n + 1)
                    pool.tensor_tensor(rstd1[:, j], mv1[:, j, 1:2], eps_col[:], ALU.add).then_inc(pool1, 1)
                    pool.wait_ge(pool1, n + 1)
                    pool.tensor_tensor(rstd1[:, j], rstd1[:, j], minus_half[:], ALU.pow).then_inc(rstd1_ready, 1)
                for j in range(G):
                    n = G * i + j
                    need(pool, mixed_ready, n + 1)
                    need(pool, var2_ready, n - 1)
                    pool.tensor_tensor(diff[:, j], mixed[:, j, 0], mixed[:, j, 1], ALU.subtract)
                    pool.tensor_tensor(base[:, j], x1[:, j], mixed[:, j, 1], ALU.add).then_inc(base_ready, 1)
                for j in range(G):
                    n = G * i + j
                    need(pool, var2_ready, n + 1)
                    pool.tensor_tensor(rstd2[:, j], mv2[:, j, 1:2], eps_col[:], ALU.add).then_inc(pool2, 1)
                    pool.wait_ge(pool2, n + 1)
                    pool.tensor_tensor(rstd2[:, j], rstd2[:, j], minus_half[:], ALU.pow).then_inc(rstd2_ready, 1)
                    need(pool, sumsq_ready, n + 1)
                    pool.tensor_tensor(rrms[:, j], sumsq[:, j], eps_col[:], ALU.add).then_inc(pool3, 1)
                    pool.wait_ge(pool3, n + 1)
                    pool.tensor_tensor(rrms[:, j], rrms[:, j], minus_half[:], ALU.pow).then_inc(rrms_ready, 1)
                for j in range(G):
                    n = G * i + j
                    need(pool, x2_ready, n + 1)
                    pool.dma_start(x2_dram[:, bass.ts(n, 1), :], x2[:, j:j + 1, :]).then_inc(x2_stored[j], 16)
                    need(pool, row_ready, n + 1)
                    pool.dma_start(rows_dram[:, bass.ts(n, 1), :], row[:, j:j + 1, :]).then_inc(row_stored[j], 16)
                need(pool, lgT_ready, i + 1)
                pool.dma_start(logits_dram[:, bass.ts(i, GT)], lgT[:]).then_inc(lgT_stored, 16)
            loop(pool, group)
            for j in range(G):
                pool.wait_ge(x2_stored[j], 16 * NG)
                pool.wait_ge(row_stored[j], 16 * NG)
            pool.wait_ge(lgT_stored, 16 * NG)

        @block.tensor
        def _(pe):
            pe.wait_ge(w_ready, 2 * len(W_PARTS))
            pe.wait_ge(consts, 8)

            def split_product(out, stationary, moving, chunks):
                last = None
                for k, (a, b) in enumerate(PASSES):
                    for c in range(chunks):
                        last = pe.matmul(out, stationary(a, c), moving(b, c), start=(k == 0 and c == 0),
                                         stop=(k == len(PASSES) - 1 and c == chunks - 1))
                return last

            def qkv(i, j):
                n = G * i + j
                tok = slice(j * T, (j + 1) * T)
                need(pe, xT_ready, i + 1)
                need(pe, probs_ready, UNITS * G * i)
                split_product(bank[j][:], lambda a, c: xT[:, a, c, tok], lambda b, c: wqk[:, b, c, :], DC).then_inc(qk_done, 1)
                split_product(bank[2 + j][:, 0:D], lambda a, c: xT[:, a, c, tok], lambda b, c: wv[:, b, c, :], DC).then_inc(v_done, 1)

            def transpose_qk(i, j):
                n = G * i + j
                need(pe, rope_ready, n + 1)
                need(pe, xnT_ready, G * i)
                last = None
                for k in range(2 * DC):
                    last = pe.transpose(bank[4 + j][:, k * P:(k + 1) * P], roped[:, j, k * P:(k + 1) * P], ident[:])
                last.then_inc(qkT_done, 1)

            def scores(i, j, t):
                n = G * i + j
                u = UNITS * n + t
                c = t // (UNITS // DC)
                h0 = HU * (t % (UNITS // DC))
                if t % (UNITS // DC) == 0:
                    need(pe, kblock_ready[c], 16 * (H // DC) * (n + 1))
                need(pe, probs_ready, u - 3)
                if j == 0:
                    need(pe, qkb_ready, G * (i + 1))
                    need(pe, v_ready, G * (i + 1))
                pe.matmul(bank[t][:], ident_bf[:], mask[:].rearrange("p h k -> p (h k)"), start=True, stop=False)
                last = None
                for k, (a, b) in enumerate(PASSES):
                    last = pe.matmul(bank[t][:], qkT[:, j, a, c, :], kblock[:, b, c, h0:h0 + HU, :].rearrange("p h k -> p (h k)"),
                                     start=False, stop=(k == len(PASSES) - 1))
                last.then_inc(scores_ready, 1)

            def transpose_probs(i, j, t):
                n = G * i + j
                u = UNITS * n + t
                need(pe, probs_ready, u + 1)
                need(pe, probsT_ready, u - 1)
                if j == 0:
                    need(pe, qkT_ready, G * (i + 1))
                last = None
                for h in range(HU):
                    last = pe.transpose(bank[4 + t % 2][:, h * T:(h + 1) * T], probs_a[:, t, h], ident[:])
                last.then_inc(probsT_done, 1)

            def weigh_values(i, j, t):
                n = G * i + j
                u = UNITS * n + t
                need(pe, probsT_ready, u + 1)
                if t == 0:
                    need(pe, v_ready, n + 1)
                    need(pe, lexp_ready, G * i)
                    need(pe, lgT_ready, i)
                last = None
                for h in range(HU):
                    last = pe.matmul(bank[6 + j][2 * HD * h:2 * HD * (h + 1), t * T:(t + 1) * T], v_aug[:, j, HU * t + h, :],
                                     probs_T[:, t % 2, h], start=True, stop=True)
                last.then_inc(av_done, 1)

            def transpose_out(i, j):
                n = G * i + j
                need(pe, outT_ready, n + 1)
                last = None
                for t in range(UNITS):
                    last = pe.transpose(bank[6 + j][:, t * P:(t + 1) * P], outT[:, j, t], ident[:])
                last.then_inc(out_done, 1)

            def transpose_heads(i, j):
                n = G * i + j
                need(pe, heads_ready, n + 1)
                last = None
                for c in range(DC):
                    last = pe.transpose(bank[6 + j][:, c * P:(c + 1) * P], heads[:, j, c * P:(c + 1) * P], ident[:])
                last.then_inc(headsT_done, 1)

            def project_out(i, j):
                n = G * i + j
                need(pe, headsT_ready, n + 1)
                split_product(bank[6 + j][:, 0:D], lambda a, c: headsT[:, j, a, c, :], lambda b, c: wo[:, b, c, :], DC).then_inc(wo_done, 1)

            def transpose_x1(i, j):
                n = G * i + j
                need(pe, x1_ready, n + 1)
                need(pe, probsT_ready, UNITS * G * (i + 1))
                last = None
                for c in range(DC):
                    last = pe.transpose(bank[4 + j][:, c * P:(c + 1) * P], x1[:, j, c * P:(c + 1) * P], ident[:])
                last.then_inc(x1T_done, 1)

            def features(i, k):
                kind = (KS, QS, QC, KC)[k]
                src = cT if k < 2 else x1T
                need(pe, cT_ready, i + 1)
                if k >= 2:
                    need(pe, x1T_ready, G * (i + 1))
                need(pe, probs_ready, UNITS * G * (i + 1))
                for m in range(DC):
                    last = split_product(bank[k][:, m * GT:(m + 1) * GT], lambda a, c: wx[:, a, kind, c, m * P:(m + 1) * P],
                                         lambda b, c: src[:, b, c, :], DC)
                last.then_inc(feat_done, 1)

            def cross_values(i, j):
                n = G * i + j
                tok = slice(j * T, (j + 1) * T)
                need(pe, pre1_ready, n + 1)
                split_product(bank[6 + j][:, 0:D], lambda a, c: cT[:, a, c, tok], lambda b, c: wxv[:, b, 0, c, :], DC)
                split_product(bank[6 + j][:, D:2 * D], lambda a, c: x1T[:, a, c, tok], lambda b, c: wxv[:, b, 1, c, :], DC).then_inc(xv_done, 1)

            def cross_scores(i, j):
                n = G * i + j
                tok = slice(j * T, (j + 1) * T)
                need(pe, feat_act, DC * (i + 1))
                need(pe, feat_dve, DC * (i + 1))
                last = None
                for s, (q, k) in enumerate(((QC, KS), (QS, KC))):
                    for c in range(DC):
                        last = pe.matmul(bank[j][:, s * T:(s + 1) * T], feat[:, q, c, tok], feat[:, k, c, tok],
                                         start=(c == 0), stop=(c == DC - 1))
                last.then_inc(xscores_done, 1)

            def transpose_cross(i, j):
                n = G * i + j
                need(pe, xprobs_ready, n + 1)
                need(pe, x1T_ready, n + 1)
                last = None
                for s in range(2):
                    last = pe.transpose(bank[4 + j][:, s * T:(s + 1) * T], xprobs[:, j, s], ident[:])
                last.then_inc(xprobsT_done, 1)

            def cross_weigh(i, j):
                n = G * i + j
                need(pe, xprobsT_ready, n + 1)
                need(pe, xv_ready, n + 1)
                last = None
                for s in range(2):
                    last = pe.matmul(bank[6 + j][:, s * D:(s + 1) * D], xprobs_T[:, j, s], values[:, j, s * D:(s + 1) * D],
                                     start=True, stop=True)
                last.then_inc(xav_done, 1)

            def transpose_mixed(i, j):
                n = G * i + j
                need(pe, mixed_ready, n + 1)
                last = None
                for k in range(2 * DC):
                    last = pe.transpose(bank[4 + j][:, k * P:(k + 1) * P], mixed[:, j, k // DC, (k % DC) * P:(k % DC + 1) * P], ident[:])
                last.then_inc(mixedT_done, 1)

            def gate(i, j):
                n = G * i + j
                need(pe, mixedT_ready, n + 1)
                split_product(bank[6 + j][:, 0:D], lambda a, c: mixedT[:, j, a, c, :], lambda b, c: wg[:, b, c, :], 2 * DC).then_inc(gate_done, 1)

            def transpose_xn(i, j):
                n = G * i + j
                need(pe, xn_ready, n + 1)
                last = None
                for c in range(DC):
                    last = pe.transpose(bank[4 + j][:, c * P:(c + 1) * P], row[:, j, c * P:(c + 1) * P], ident[:])
                last.then_inc(xnT_done, 1)

            def router(i, j):
                n = G * i + j
                tok = slice(j * T, (j + 1) * T)
                need(pe, xnT_ready, n + 1)
                need(pe, gate_z_ready, n + 1)
                last = None
                for c in range(DC):
                    last = pe.matmul(bank[6 + j][:, 0:E], xnT[:, c, tok], wr[:, c, :], start=(c == 0), stop=(c == DC - 1))
                last.then_inc(lg_done, 1)

            def router_T(i):
                need(pe, lexp_ready, G * (i + 1))
                last = None
                for c in range(DC):
                    last = pe.matmul(bank[7][0:E, 0:GT], wr[:, c, :], xnT[:, c, :], start=(c == 0), stop=(c == DC - 1))
                last.then_inc(lgT_done, 1)

            def group(i):
                for j in range(G):
                    qkv(i, j)
                for j in range(G):
                    transpose_qk(i, j)
                units = [(j, t) for j in range(G) for t in range(UNITS)]
                ahead = 3
                for u in range(ahead):
                    scores(i, *units[u])
                for u, (j, t) in enumerate(units):
                    transpose_probs(i, j, t)
                    if u + ahead < len(units):
                        scores(i, *units[u + ahead])
                    weigh_values(i, j, t)
                    if u == UNITS + 1:
                        transpose_out(i, 0)
                    if u == UNITS + 2:
                        transpose_heads(i, 0)
                    if u == UNITS + 3:
                        project_out(i, 0)
                for k in range(2):
                    features(i, k)
                transpose_out(i, 1)
                transpose_x1(i, 0)
                transpose_heads(i, 1)
                project_out(i, 1)
                transpose_x1(i, 1)
                for k in range(2, 4):
                    features(i, k)
                for j in range(G):
                    cross_values(i, j)
                for step in (cross_scores, transpose_cross, cross_weigh, transpose_mixed, gate, transpose_xn, router):
                    for j in range(G):
                        step(i, j)
                router_T(i)
            loop(pe, group)

        @block.scalar
        def _(act):
            act.wait_ge(w_loaded, N_CONST)
            for tile, src, at, width in weight_pieces():
                act.activation(flat(tile[:, 0]), shared[:, at:at + width], ACT.Copy).then_inc(w_high, 1)

            def attend(i, j):
                for t in range(UNITS):
                    n = G * i + j
                    u = UNITS * n + t
                    need(act, max_ready, u + 1)
                    need(act, probsT_done, u - 3)
                    last = None
                    for h in range(HU):
                        last = act.activation(probs_a[:, t, h], bank[t][:, h * T:(h + 1) * T], ACT.Exp, bias=nmax[:, u8(j, t), h:h + 1])
                    last.then_inc(probs_ready, 1)

            def u8(j, t):
                return (UNITS * j + t) % 8

            def out_evacuate(i, j):
                n = G * i + j
                need(act, av_done, UNITS * (n + 1))
                act.activation(outT[:, j].rearrange("p u t -> p (u t)"), bank[6 + j][:], ACT.Copy).then_inc(outT_ready, 1)

            def heads_high(i, j):
                n = G * i + j
                need(act, headsT_done, n + 1)
                need(act, wo_done, n - 1)
                act.activation(headsT[:, j, 0].rearrange("p c t -> p (c t)"), bank[6 + j][:, 0:D], ACT.Copy).then_inc(headsT_high, 1)

            def group(i):
                for j in range(G):
                    n = G * i + j
                    need(act, qkT_done, n + 1)
                    need(act, scores_ready, UNITS * G * i)
                    act.activation(qkT[:, j, 0].rearrange("p c t -> p (c t)"), bank[4 + j][:], ACT.Copy).then_inc(qkT_high, 1)
                attend(i, 0)
                out_evacuate(i, 0)
                attend(i, 1)
                heads_high(i, 0)
                out_evacuate(i, 1)
                for k in (0,):
                    features_out(act, i, k)
                x1_high(i, 0)
                heads_high(i, 1)
                x1_high(i, 1)
                features_out(act, i, 2)
                for j in range(G):
                    n = G * i + j
                    need(act, xmax_ready, n + 1)
                    need(act, xprobsT_done, n - 1)
                    for s in range(2):
                        last = act.activation(xprobs[:, j, s], bank[j][:, s * T:(s + 1) * T], ACT.Exp, scale=float(D) ** -0.5,
                                              bias=xbias[:, j, s:s + 1], accum_out=xsum[:, j, s:s + 1])
                    last.then_inc(xprobs_ready, 1)
                for j in range(G):
                    n = G * i + j
                    need(act, xprobsT_done, n + 1)
                    act.activation(xprobs_T[:, j].rearrange("p s t -> p (s t)"), bank[4 + j][:, 0:2 * T], ACT.Copy).then_inc(xprobsT_ready, 1)
                for j in range(G):
                    n = G * i + j
                    need(act, xav_done, n + 1)
                    need(act, xrec_ready, n + 1)
                    need(act, base_ready, n - 1)
                    need(act, mixedT_done, n - 1)
                    for s in range(2):
                        last = act.activation(mixed[:, j, s], bank[6 + j][:, s * D:(s + 1) * D], ACT.Copy, scale=xrec[:, j, s:s + 1])
                    last.then_inc(mixed_ready, 1)
                for j in range(G):
                    n = G * i + j
                    need(act, mixedT_done, n + 1)
                    need(act, gate_done, n - 1)
                    act.activation(mixedT[:, j, 0].rearrange("p c t -> p (c t)"), bank[4 + j][:], ACT.Copy).then_inc(mixedT_high, 1)
                for j in range(G):
                    n = G * i + j
                    need(act, gate_z_ready, n + 1)
                    need(act, var2_ready, n - 1)
                    act.activation(gate_z[:, j], gate_z[:, j], ACT.Tanh, scale=0.5).then_inc(gate_t_ready, 1)
                for j in range(G):
                    n = G * i + j
                    need(act, x2_ready, n + 1)
                    need(act, rrms_ready, n - 1)
                    need(act, sumsq_ready, n)
                    act.activation(square[:], x2[:, j], ACT.Square, scale=float(D) ** -0.5, accum_out=sumsq[:, j]).then_inc(sumsq_ready, 1)
                for j in range(G):
                    n = G * i + j
                    need(act, xnT_done, n + 1)
                    need(act, lgT_done, i)
                    act.activation(xnT[:, :, j * T:(j + 1) * T], bank[4 + j][:, 0:D].rearrange("p (c t) -> p c t", c=DC), ACT.Copy).then_inc(xnT_ready, 1)
                for j in range(G):
                    n = G * i + j
                    need(act, lg_step, 3 * n + 2)
                    act.activation(lexp[:, j], lg[:], ACT.Exp, bias=lmax[:], accum_out=lsum[:, j]).then_inc(lexp_ready, 1)
                need(act, lgT_done, i + 1)
                need(act, lgT_stored, 16 * i)
                act.activation(lgT[:], bank[7][0:E, 0:GT], ACT.Identity, bias=br_col[:]).then_inc(lgT_ready, 1)

            def x1_high(i, j):
                n = G * i + j
                need(act, x1T_done, n + 1)
                need(act, xv_done, G * i)
                act.activation(x1T[:, 0, :, j * T:(j + 1) * T], bank[4 + j][:, 0:D].rearrange("p (c t) -> p c t", c=DC), ACT.Copy).then_inc(x1T_high, 1)

            def features_out(act, i, k):
                kind = (KS, QS, QC, KC)[k]
                need(act, feat_done, 4 * i + k + 1)
                need(act, xscores_done, G * i)
                for m in range(DC):
                    last = act.activation(feat[:, kind, m, :], bank[k][:, m * GT:(m + 1) * GT], ACT.Identity, bias=bx[:, kind, m:m + 1])
                last.then_inc(feat_act, 1)

            loop(act, group)

        @block.vector
        def _(dve):
            for k, (tile, src, at, width) in enumerate(weight_pieces()):
                dve.wait_ge(w_high, k + 1)
                dve.tensor_tensor(flat(tile[:, 1]), shared[:, at:at + width], flat(tile[:, 0]).bitcast(F32), ALU.subtract).then_inc(w_ready, 2)

            def max_unit(i, j, t):
                u = UNITS * (G * i + j) + t
                need(dve, scores_ready, u + 1)
                need(dve, probs_ready, u - 7)
                dve.tensor_reduce(out=nmax[:, (UNITS * j + t) % 8], in_=bank[t][:].rearrange("p (h k) -> p h k", h=HU),
                                  axis=AX_X, op=ALU.max, negate=True).then_inc(max_ready, 1)

            def probs_evacuate(i, j, t):
                u = UNITS * (G * i + j) + t
                need(dve, probsT_done, u + 1)
                need(dve, av_done, u - 1)
                dve.tensor_copy(probs_T[:, t % 2].rearrange("p h t -> p (h t)"), bank[4 + t % 2][:]).then_inc(probsT_ready, 1)

            def normalise_heads(i, j):
                n = G * i + j
                need(dve, out_done, n + 1)
                need(dve, headsT_done, n - 1)
                o = bank[6 + j][:].rearrange("p (h k) -> p h k", h=H)
                dve.reciprocal(rec[:, j].unsqueeze(2), o[:, :, HD:HD + 1]).then_inc(rec_ready, 1)
                need(dve, rec_ready, n + 1)
                dve.tensor_tensor(heads[:, j].rearrange("p (h k) -> p h k", h=H), o[:, :, 0:HD],
                                  rec[:, j].unsqueeze(2).to_broadcast([P, H, HD]), ALU.mult).then_inc(heads_ready, 1)

            def heads_low(i, j):
                n = G * i + j
                need(dve, headsT_high, n + 1)
                dve.tensor_tensor(headsT[:, j, 1].rearrange("p c t -> p (c t)"), bank[6 + j][:, 0:D],
                                  headsT[:, j, 0].rearrange("p c t -> p (c t)").bitcast(F32), ALU.subtract).then_inc(headsT_ready, 1)

            def norm1_stats(i, j):
                n = G * i + j
                need(dve, wo_done, n + 1)
                need(dve, xb_ready, n + 1)
                need(dve, x1_ready, n - 1)
                dve.tensor_tensor(pre1[:, j], bank[6 + j][:, 0:D], xb[:, j], ALU.add).then_inc(pre1_ready, 1)
                need(dve, pre1_ready, n + 1)
                need(dve, var1_ready, n)
                dve.bn_stats(stats[:, 0], pre1[:, j]).then_inc(stats1, 1)
                need(dve, stats1, n + 1)
                need(dve, rstd1_ready, n - 1)
                hold_dve(dve)
                dve.bn_aggr(mv1[:, j], stats[:, 0]).then_inc(var1_ready, 1)

            def norm1(i, j):
                n = G * i + j
                need(dve, rstd1_ready, n + 1)
                need(dve, base_ready, G * i)
                dve.tensor_scalar(x1[:, j], pre1[:, j], mv1[:, j, 0:1], rstd1[:, j], ALU.subtract, ALU.mult).then_inc(x1_ready, 1)

            def x1_low(i, j):
                n = G * i + j
                need(dve, x1T_high, n + 1)
                dve.tensor_tensor(x1T[:, 1, :, j * T:(j + 1) * T], bank[4 + j][:, 0:D].rearrange("p (c t) -> p c t", c=DC),
                                  x1T[:, 0, :, j * T:(j + 1) * T].bitcast(F32), ALU.subtract).then_inc(x1T_ready, 1)

            def features_out(i, k):
                kind = (KS, QS, QC, KC)[k]
                need(dve, feat_done, 4 * i + k + 1)
                need(dve, xscores_done, G * i)
                for m in range(DC):
                    last = dve.tensor_scalar(feat[:, kind, m, :], bank[k][:, m * GT:(m + 1) * GT], bx[:, kind, m:m + 1], None, ALU.add)
                last.then_inc(feat_dve, 1)

            def group(i):
                for j in range(G):
                    n = G * i + j
                    need(dve, qk_done, n + 1)
                    need(dve, rope_ready, n - 1)
                    dve.tensor_tensor(qkb[:, j], bank[j][:], bqkv[:, 0:2 * D], ALU.add).then_inc(qkb_ready, 1)
                    need(dve, v_done, n + 1)
                    need(dve, av_done, UNITS * G * i)
                    dve.tensor_tensor(v_aug[:, j, :, 0:HD], bank[2 + j][:, 0:D].rearrange("p (h k) -> p h k", h=H),
                                      bqkv[:, 2 * D:3 * D].rearrange("p (h k) -> p h k", h=H), ALU.add).then_inc(v_ready, 1)
                for j in range(G):
                    n = G * i + j
                    need(dve, qkT_high, n + 1)
                    dve.tensor_tensor(qkT[:, j, 1].rearrange("p c t -> p (c t)"), bank[4 + j][:],
                                      qkT[:, j, 0].rearrange("p c t -> p (c t)").bitcast(F32), ALU.subtract).then_inc(qkT_ready, 1)
                units = [(j, t) for j in range(G) for t in range(UNITS)]
                ahead = 2
                for u in range(ahead):
                    max_unit(i, *units[u])
                for u, (j, t) in enumerate(units):
                    if u + ahead < len(units):
                        max_unit(i, *units[u + ahead])
                    probs_evacuate(i, j, t)
                    if u == UNITS + 1:
                        normalise_heads(i, 0)
                    if u == UNITS + 2:
                        heads_low(i, 0)
                norm1_stats(i, 0)
                features_out(i, 1)
                normalise_heads(i, 1)
                norm1(i, 0)
                x1_low(i, 0)
                heads_low(i, 1)
                norm1_stats(i, 1)
                norm1(i, 1)
                x1_low(i, 1)
                features_out(i, 3)
                for j in range(G):
                    n = G * i + j
                    need(dve, xv_done, n + 1)
                    need(dve, xav_done, G * i)
                    dve.tensor_tensor(values[:, j], bank[6 + j][:], bxv[:], ALU.add).then_inc(xv_ready, 1)
                for j in range(G):
                    n = G * i + j
                    need(dve, xscores_done, n + 1)
                    dve.tensor_reduce(out=xnmax[:, j], in_=bank[j][:, 0:2 * T].rearrange("p (s k) -> p s k", s=2),
                                      axis=AX_X, op=ALU.max, negate=True).then_inc(xmax_made, 1)
                    need(dve, xmax_made, n + 1)
                    need(dve, xprobs_ready, n - 1)
                    dve.tensor_scalar(xbias[:, j], xnmax[:, j], float(D) ** -0.5, None, ALU.mult).then_inc(xmax_ready, 1)
                for j in range(G):
                    n = G * i + j
                    need(dve, xprobs_ready, n + 1)
                    need(dve, mixed_ready, n - 1)
                    dve.reciprocal(xrec[:, j], xsum[:, j]).then_inc(xrec_ready, 1)
                for j in range(G):
                    n = G * i + j
                    need(dve, mixedT_high, n + 1)
                    dve.tensor_tensor(mixedT[:, j, 1].rearrange("p c t -> p (c t)"), bank[4 + j][:],
                                      mixedT[:, j, 0].rearrange("p c t -> p (c t)").bitcast(F32), ALU.subtract).then_inc(mixedT_ready, 1)
                for j in range(G):
                    n = G * i + j
                    need(dve, gate_done, n + 1)
                    need(dve, gate_t_ready, n - 1)
                    dve.tensor_tensor(gate_z[:, j], bank[6 + j][:, 0:D], bg[:], ALU.add).then_inc(gate_z_ready, 1)
                for j in range(G):
                    n = G * i + j
                    need(dve, gate_t_ready, n + 1)
                    need(dve, base_ready, n + 1)
                    need(dve, dve_step, 3 * n)
                    dve.scalar_tensor_tensor(diff[:, j], gate_z[:, j], 1.0, diff[:, j], ALU.add, ALU.mult).then_inc(dve_step, 1)
                    need(dve, dve_step, 3 * n + 1)
                    need(dve, x2_ready, n - 1)
                    dve.scalar_tensor_tensor(pre2[:, j], diff[:, j], 0.5, base[:, j], ALU.mult, ALU.add).then_inc(dve_step, 1)
                    need(dve, dve_step, 3 * n + 2)
                    need(dve, var2_ready, n)
                    dve.bn_stats(stats[:, 1], pre2[:, j]).then_inc(dve_step, 1)
                    need(dve, dve_step, 3 * n + 3)
                    need(dve, rstd2_ready, n - 1)
                    hold_dve(dve)
                    dve.bn_aggr(mv2[:, j], stats[:, 1]).then_inc(var2_ready, 1)
                for j in range(G):
                    n = G * i + j
                    need(dve, rstd2_ready, n + 1)
                    need(dve, x2_stored[j], 16 * i)
                    need(dve, sumsq_ready, n - 1)
                    dve.tensor_scalar(x2[:, j], pre2[:, j], mv2[:, j, 0:1], rstd2[:, j], ALU.subtract, ALU.mult).then_inc(x2_ready, 1)
                for j in range(G):
                    n = G * i + j
                    need(dve, rrms_ready, n + 1)
                    need(dve, row_stored[j], 16 * i)
                    dve.scalar_tensor_tensor(row[:, j, 0:D], x2[:, j], rrms[:, j], nw[:], ALU.mult, ALU.mult).then_inc(xn_ready, 1)
                for j in range(G):
                    n = G * i + j
                    need(dve, lg_done, n + 1)
                    need(dve, lexp_ready, n)
                    dve.tensor_tensor(lg[:], bank[6 + j][:, 0:E], br[:], ALU.add).then_inc(lg_step, 1)
                    need(dve, lg_step, 3 * n + 1)
                    dve.tensor_reduce(out=lmax[:], in_=lg[:], axis=AX_X, op=ALU.max, negate=True).then_inc(lg_step, 1)
                    need(dve, lexp_ready, n + 1)
                    dve.reciprocal(lrec[:], lsum[:, j]).then_inc(lg_step, 1)
                    need(dve, lg_step, 3 * n + 3)
                    dve.tensor_scalar(row[:, j, D:ROW], lexp[:, j], lrec[:], None, ALU.mult)
                    dve.tensor_scalar(probs[:, bass.ts(n, 1), :].rearrange("p o e -> p (o e)"), lexp[:, j], lrec[:], None, ALU.mult).then_inc(row_ready, 1)
            loop(dve, group)


def choose_tokens(nc, d, logits_dram, slots_dram, probs, slot_rows, gate_scale):
    with ExitStack() as ctx:
        def sb(name, shape, dt=F32):
            return ctx.enter_context(nc.sbuf_tensor(name, shape, dt))

        def sem(name):
            return ctx.enter_context(nc.semaphore(name))

        keys = sb("keys", [P, CHUNK])
        ones = sb("ones_bf", [P, CHUNK], BF16)
        hits = sb("hits", [P, CHUNK])
        same = sb("same", [P, CHUNK])
        place = sb("place", [P, CHUNK])
        same_expert = sb("same_expert", [P, P])
        earlier_chunk = sb("earlier_chunk", [P, P])
        ident = sb("ident_b", [P, P])
        digits_hi = sb("digits_hi", [P, SLOT_HI])
        digits_lo = sb("digits_lo", [P, SLOT_LO])
        token_no = sb("token_no", [P, 1])
        batch_no = sb("batch_no", [P, B])
        combine = sb("combine", [2 * SLOT_HI, SLOT_HI])
        zeros = sb("zeros_bf", [P, E * SLOT_LO], BF16)
        thr = sb("thr", [P, 1], I32)
        cand = sb("cand", [P, 1], I32)
        bit = sb("bit", [P, 1], I32)
        accept = sb("accept", [P, 1], I32)
        neg = sb("neg", [P, 1])
        pad = sb("pad_b", [1, 1])
        neg_i = sb("neg_i", [P, 1], I32)
        count = sb("count", [P, 1])
        counts = sb("counts", [P, 2])
        left = sb("left", [P, 1])
        before = sb("before", [P, 2])
        slot = sb("slot", [P, CHUNKS, CHUNK // P, E], I32)
        slot_hi = sb("slot_hi", [P, CHUNKS, CHUNK // P * E], I32)
        slot_lo = sb("slot_lo", [P, CHUNKS, CHUNK // P * E], I32)
        gated = sb("gated", [P, B, E])
        gate_sum = sb("gate_sum", [P, B])
        empty = sb("empty", [P, B])
        KB = CHUNK // P
        hot_hi = sb("hot_hi", [P, 2, KB * E, SLOT_HI], BF16)
        hot_ids = sb("hot_ids", [P, 2, KB * E, 2, SLOT_HI], BF16)
        hot_lo = sb("hot_lo", [P, 2, KB * E, SLOT_LO], BF16)
        ids_two = sb("ids_two", [2 * SLOT_HI, E * SLOT_LO])
        ids = sb("ids", [SLOT_HI, E * SLOT_LO], I32)
        total = ctx.enter_context(nc.psum_tensor("total", [P, 512], F32))
        placeT = ctx.enter_context(nc.psum_tensor("placeT", [P, KB, P], F32))
        table = ctx.enter_context(nc.psum_tensor("table", [P, 512], F32))
        table2 = ctx.enter_context(nc.psum_tensor("table2", [P, 512], F32))

        loaded = sem("b_loaded")
        ready = sem("b_consts")
        counted = sem("counted")
        totalled = sem("totalled")
        step = sem("b_step")
        placed = sem("placed")
        transposed = sem("transposed")
        hot_ready = sem("hot_ready")
        table_used = sem("table_used")
        table_done = sem("table_done")
        ids_two_ready = sem("ids_two_ready")
        ids_done = sem("ids_done")
        ids_ready = sem("ids_ready")
        slots_stored = sem("slots_stored")
        slots_loaded = sem("slots_loaded")

        consts = ((same_expert, "same_expert"), (earlier_chunk, "earlier_chunk"), (ident, "ident"), (digits_hi, "digits_hi"),
                  (digits_lo, "digits_lo"), (token_no, "token_no"), (batch_no, "batch_no"), (combine, "combine"))
        block = ctx.enter_context(nc.Block())

        @block.sync
        def _(sp):
            sp.dma_start(keys[:], logits_dram.rearrange("e (c k) -> (e c) k", c=CHUNKS)).then_inc(loaded, 16)
            for tile, name in consts:
                sp.dma_start(tile[:], d[name]).then_inc(loaded, 16)
            sp.wait_ge(ids_ready, 1)
            sp.dma_start(slots_dram.rearrange("e (h l) -> h e l", h=SLOT_HI), ids[:].rearrange("h (e l) -> h e l", e=E)).then_inc(slots_stored, 16)
            sp.wait_ge(slots_stored, 16)
            sp.dma_start(slot_rows[:], slots_dram.rearrange("e (p q) -> p e q", p=P)).then_inc(slots_loaded, 16)
            sp.wait_ge(slots_loaded, 16)

        @block.tensor
        def _(pe):
            pe.wait_ge(loaded, 16 * (1 + len(consts)))
            pe.wait_ge(counted, 1)
            pe.matmul(total[:, 0:1], same_expert[:], count[:], start=True, stop=True).then_inc(totalled, 1)
            with pe.Fori(0, 31) as k:
                pe.wait_ge(counted, k + 2)
                pe.matmul(total[:, 0:1], same_expert[:], count[:], start=True, stop=True).then_inc(totalled, 1)
            pe.wait_ge(counted, 33)
            pe.matmul(total[:, 0:1], same_expert[:], counts[:, 0:1], start=True, stop=True)
            pe.matmul(total[:, 1:2], earlier_chunk[:], counts[:, 1:2], start=True, stop=True).then_inc(totalled, 1)
            pe.wait_ge(counted, 34)
            pe.matmul(total[:, 0:1], earlier_chunk[:], count[:], start=True, stop=True).then_inc(totalled, 1)
            pe.wait_ge(placed, 1)
            last = None
            for k in range(KB):
                last = pe.transpose(placeT[:, k], place[:, k * P:(k + 1) * P], ident[:])
            last.then_inc(transposed, 1)
            pe.wait_ge(ready, 2)
            pe.matmul(table[0:2 * SLOT_HI, :], zeros[:, 0:2 * SLOT_HI], zeros[:], start=True, stop=False)

            def chunk_pair(i):
                last = None
                for b in range(2):
                    pe.wait_ge(hot_ready, 2 * i + b + 1)
                    for k in range(KB * E):
                        e = k % E
                        last = pe.matmul(table[0:2 * SLOT_HI, e * SLOT_LO:(e + 1) * SLOT_LO],
                                         hot_ids[:, b, k].rearrange("p two h -> p (two h)"), hot_lo[:, b, k],
                                         start=False, stop=False, skip_group_check=True)
                    last.then_inc(table_used, 1)
            with pe.Fori(0, CHUNKS // 2) as i:
                chunk_pair(i)
            pe.matmul(table[0:2 * SLOT_HI, :], zeros[:, 0:2 * SLOT_HI], zeros[:], start=False, stop=True).then_inc(table_done, 1)
            pe.wait_ge(ids_two_ready, 1)
            pe.matmul(table2[0:SLOT_HI, :], combine[:], ids_two[:], start=True, stop=True).then_inc(ids_done, 1)

        @block.vector
        def _(dve):
            dve.memset(ones[:], 1.0).then_inc(ready, 1)
            dve.memset(zeros[:], 0.0).then_inc(ready, 1)
            dve.memset(cand[:], 0).then_inc(step, 1)
            dve.memset(bit[:], 1 << 30).then_inc(step, 1)
            dve.wait_ge(loaded, 16 * (1 + len(consts)))
            dve.wait_ge(step, 2)
            cand_f = cand[:].bitcast(F32)

            def count_at_least():
                dve.tensor_scalar(hits[:], keys[:], cand_f, None, ALU.is_ge, ALU.add, accum_out=count[:]).then_inc(counted, 1)

            count_at_least()
            dve.wait_ge(totalled, 1)
            dve.tensor_scalar(neg[:], total[:, 0:1], float(CAP), None, ALU.is_lt).then_inc(step, 1)
            dve.tensor_scalar(neg_i[:], total[:, 0:1], float(CAP), None, ALU.is_lt).then_inc(step, 1)
            dve.wait_ge(step, 4)
            dve.tensor_scalar(thr[:], neg_i[:], 31, None, ALU.logical_shift_left).then_inc(step, 1)
            dve.wait_ge(step, 5)
            dve.tensor_tensor(cand[:], thr[:], bit[:], ALU.bitwise_or).then_inc(step, 1)
            with dve.Fori(0, 31) as k:
                dve.wait_ge(step, 4 * k + 6)
                count_at_least()
                dve.tensor_scalar(bit[:], bit[:], 1, None, ALU.logical_shift_right).then_inc(step, 1)
                dve.wait_ge(totalled, k + 2)
                dve.tensor_scalar(accept[:], total[:, 0:1], float(CAP), neg[:], ALU.is_ge, ALU.not_equal).then_inc(step, 1)
                dve.wait_ge(step, 4 * k + 8)
                dve.memset(pad[:], 0.0)
                dve.copy_predicated(thr[:], accept[:], cand[:]).then_inc(step, 1)
                dve.wait_ge(step, 4 * k + 9)
                dve.tensor_tensor(cand[:], thr[:], bit[:], ALU.bitwise_or).then_inc(step, 1)
            s = 4 * 31 + 6
            dve.wait_ge(step, s)
            dve.tensor_tensor(thr[:], thr[:], neg_i[:], ALU.add).then_inc(step, 1)
            dve.wait_ge(step, s + 1)
            thr_f = thr[:].bitcast(F32)
            dve.tensor_scalar(hits[:], keys[:], thr_f, None, ALU.is_gt, ALU.add, accum_out=counts[:, 0:1])
            dve.tensor_scalar(same[:], keys[:], thr_f, None, ALU.is_equal, ALU.add, accum_out=counts[:, 1:2]).then_inc(counted, 1)
            dve.wait_ge(totalled, 33)
            dve.tensor_scalar(left[:], total[:, 0:1], -1.0, float(CAP), ALU.mult, ALU.add).then_inc(step, 1)
            dve.tensor_copy(before[:, 0:1], total[:, 1:2]).then_inc(step, 1)
            dve.wait_ge(step, s + 3)
            dve.tensor_tensor_scan(place[:], ones[:], same[:], before[:, 0:1], ALU.mult, ALU.add).then_inc(step, 1)
            dve.wait_ge(step, s + 4)
            dve.scalar_tensor_tensor(same[:], place[:], left[:], same[:], ALU.is_le, ALU.mult).then_inc(step, 1)
            dve.wait_ge(step, s + 5)
            dve.scalar_tensor_tensor(hits[:], same[:], 1.0, hits[:], ALU.mult, ALU.add, accum_out=count[:]).then_inc(counted, 1)
            dve.wait_ge(totalled, 34)
            dve.tensor_copy(before[:, 1:2], total[:, 0:1]).then_inc(step, 1)
            dve.wait_ge(step, s + 6)
            dve.tensor_tensor_scan(place[:], ones[:], hits[:], before[:, 1:2], ALU.mult, ALU.add).then_inc(step, 1)
            dve.wait_ge(step, s + 7)
            dve.tensor_tensor(place[:], place[:], hits[:], ALU.mult).then_inc(placed, 1)
            dve.wait_ge(transposed, 1)
            for k in range(KB):
                last = dve.tensor_scalar(slot[:, :, k, :], placeT[:, k].rearrange("p (e c) -> p c e", e=E), -1.0, None, ALU.add)
            last.then_inc(step, 1)
            dve.wait_ge(step, s + 8)
            flat = slot[:].rearrange("p c k e -> p c (k e)")
            dve.tensor_scalar(slot_hi[:], flat, SLOT_LO.bit_length() - 1, None, ALU.arith_shift_right).then_inc(step, 1)
            dve.tensor_scalar(slot_lo[:], flat, SLOT_LO - 1, None, ALU.bitwise_and).then_inc(step, 1)
            dve.scalar_tensor_tensor(gated[:].rearrange("p b e -> p (b e)"), slot[:].rearrange("p c k e -> p (c k e)"), 0.0,
                                     probs[:].rearrange("p b e -> p (b e)"), ALU.is_ge, ALU.mult).then_inc(step, 1)
            dve.wait_ge(step, s + 11)
            dve.tensor_reduce(out=gate_sum[:], in_=gated[:], axis=AX_X, op=ALU.add).then_inc(step, 1)
            dve.wait_ge(step, s + 12)
            dve.tensor_scalar(empty[:], gate_sum[:], 0.0, None, ALU.is_le).then_inc(step, 1)
            dve.wait_ge(step, s + 13)
            dve.tensor_tensor(gate_sum[:], gate_sum[:], empty[:], ALU.add).then_inc(step, 1)
            dve.wait_ge(step, s + 14)
            dve.reciprocal(gate_scale[:], gate_sum[:]).then_inc(step, 1)
            s += 15

            def chunk(c, b, first):
                hi_all = [P, KB * E, SLOT_HI]
                lo_all = [P, KB * E, SLOT_LO]
                dve.tensor_tensor(hot_hi[:, b], slot_hi[:, bass.ts(c, 1)].rearrange("p o n -> p (o n)").unsqueeze(2).to_broadcast(hi_all),
                                  digits_hi[:].unsqueeze(1).to_broadcast(hi_all), ALU.is_equal).then_inc(step, 1)
                if not first:
                    dve.wait_ge(table_used, c - 1)
                dve.tensor_tensor(hot_lo[:, b], slot_lo[:, bass.ts(c, 1)].rearrange("p o n -> p (o n)").unsqueeze(2).to_broadcast(lo_all),
                                  digits_lo[:].unsqueeze(1).to_broadcast(lo_all), ALU.is_equal)
                dve.wait_ge(step, s + c + 1)
                dve.tensor_scalar(hot_ids[:, b, :, 0], hot_hi[:, b], token_no[:], None, ALU.mult)
                dve.tensor_tensor(hot_ids[:, b, :, 1].rearrange("p (k e) h -> p k e h", e=E),
                                  hot_hi[:, b].rearrange("p (k e) h -> p k e h", e=E),
                                  batch_no[:, bass.ts(c, KB)].unsqueeze(2).unsqueeze(3).to_broadcast([P, KB, E, SLOT_HI]), ALU.mult).then_inc(hot_ready, 1)
            for b in range(2):
                chunk(b, b, True)
            with dve.Fori(1, CHUNKS // 2) as i:
                for b in range(2):
                    chunk(2 * i + b, b, False)
            dve.wait_ge(table_done, 1)
            dve.tensor_copy(ids_two[:], table[0:2 * SLOT_HI, :]).then_inc(ids_two_ready, 1)
            dve.wait_ge(ids_done, 1)
            dve.tensor_copy(ids[:], table2[0:SLOT_HI, :]).then_inc(ids_ready, 1)


def run_experts(nc, d, rows_dram, acc_dram, slot_rows):
    with ExitStack() as ctx:
        def sb(name, shape, dt=F32):
            return ctx.enter_context(nc.sbuf_tensor(name, shape, dt))

        def sem(name):
            return ctx.enter_context(nc.semaphore(name))

        ident = sb("ident_c", [P, P])
        w1_raw = sb("w1_raw", [P, DC * F])
        w2_raw = sb("w2_raw", [P, FC * D])
        w1 = sb("w1", [P, 2, 2, DC, F], F32R)
        w2 = sb("w2", [P, 2, 2, FC, D], F32R)
        b1 = sb("b1", [P, 2, FC])
        b2 = sb("b2", [P, 2, D])
        rows_now = sb("rows_now", [P, 2, QT], I32)
        xe = sb("xe", [P, 2, QT, ROW])
        xeT = sb("xeT", [P, 2, DC, CAP], F32R)
        h_full = sb("h_full", [P, 2, CAP])
        h = sb("h", [P, 2, 2, FC, CAP], F32R)
        y = sb("y", [P, 2, QT, D])
        pool_pad = sb("pool_pad_c", [1, 6])
        pool_one = sb("pool_one_c", [1, 1])
        bank = [ctx.enter_context(nc.psum_tensor(f"cbank{k}", [P, 512], F32)) for k in range(7)]

        ident_loaded = sem("ident_loaded")
        w_loaded = sem("ew_loaded")
        w_high = sem("ew_high")
        w1_ready = sem("w1_ready")
        w2_ready = sem("w2_ready")
        b_loaded = [sem(f"eb_loaded{k}") for k in range(2)]
        one_ready = sem("one_ready")
        idx_ready = sem("idx_ready")
        gathered = [sem(f"gathered{k}") for k in range(2)]
        xT_done = sem("exT_done")
        xT_high = sem("exT_high")
        xT_ready = sem("exT_ready")
        fc1_done = sem("fc1_done")
        gelu_ready = sem("gelu_ready")
        h_high = sem("h_high")
        h_ready = sem("h_ready")
        fc2_done = sem("fc2_done")
        y_step = sem("y_step")
        y_ready = sem("y_ready")
        scattered = [sem(f"scattered{k}") for k in range(2)]

        def loop(engine, pair):
            pair(0)
            with engine.Fori(1, E // 2) as i:
                pair(i)

        block = ctx.enter_context(nc.Block())

        @block.sync
        def _(sp):
            sp.dma_start(ident[:], d["ident"]).then_inc(ident_loaded, 16)

            def pair(i):
                experts = [sp.snap(2 * i + k) if not isinstance(i, int) else 2 * i + k for k in range(2)]
                for k, e in enumerate(experts):
                    need(sp, w1_ready, e)
                    sp.dma_start(w1_raw[:], d["w1"][bass.ts(e, 1)].rearrange("o p n -> p (o n)")).then_inc(w_loaded, 16)
                    need(sp, w2_ready, e)
                    sp.dma_start(w2_raw[:], d["w2"][bass.ts(e, 1)].rearrange("o p n -> p (o n)")).then_inc(w_loaded, 16)
                    need(sp, y_step, QT * (e - 1))
                    sp.dma_start(b1[:, k], d["b1"][bass.ts(e, 1)].rearrange("o p n -> p (o n)")).then_inc(b_loaded[k], 16)
                    sp.dma_start(b2[:, k], d["b2"][bass.ts(e, 1)].rearrange("o n -> (o n)").partition_broadcast(P)).then_inc(b_loaded[k], 16)
            loop(sp, pair)

        @block.gpsimd
        def _(pool):
            pool.memset(pool_one[:], 1.0).then_inc(one_ready, 1)
            pool.wait_ge(one_ready, 1)
            rows_all = rows_dram.rearrange("p b n -> (p b) n")
            acc_all = acc_dram.rearrange("p b n -> (p b) n")

            def hold(place):
                pool.tensor_tensor(pool_pad[:, place:place + 1], pool_one[:], pool_one[:], ALU.add)

            def scatter(i, k):
                e = 2 * i + k
                need(pool, y_ready, QT * (e + 1))
                need(pool, scattered[1 - k], 16 * QT * (i + k))
                hold(4 + k)
                for q in range(QT):
                    pool.indirect_dma_start(acc_all, bass.IndirectOffsetOnAxis(ap=rows_now[:, k, q:q + 1], axis=0), y[:, k, q], None,
                                            compute_op=ALU.add).then_inc(scattered[k], 16)

            def pair(i):
                for k in range(2):
                    e = 2 * i + k
                    need(pool, scattered[k], 16 * QT * i)
                    need(pool, y_ready, QT * (e - 1))
                    need(pool, xT_done, e - 1)
                    hold(k)
                    pool.tensor_copy(rows_now[:, k], slot_rows[:, bass.ts(e, 1)].rearrange("p o q -> p (o q)")).then_inc(idx_ready, 1)
                    pool.wait_ge(idx_ready, e + 1)
                    hold(2 + k)
                    for q in range(QT):
                        pool.indirect_dma_start(xe[:, k, q], None, rows_all, bass.IndirectOffsetOnAxis(ap=rows_now[:, k, q:q + 1], axis=0)
                                                ).then_inc(gathered[k], 16)
                    need(pool, w_high, 2 * e + 2)
                    pool.tensor_tensor(w2[:, k, 1].rearrange("p c n -> p (c n)"), w2_raw[:], w2[:, k, 0].rearrange("p c n -> p (c n)").bitcast(F32),
                                       ALU.subtract).then_inc(w2_ready, 1)
                    if k == 1:
                        scatter(i, 0)
                    elif not isinstance(i, int):
                        scatter(i - 1, 1)
            loop(pool, pair)
            scatter(E // 2 - 1, 1)
            for k in range(2):
                pool.wait_ge(scattered[k], 16 * QT * (E // 2))

        @block.tensor
        def _(pe):
            pe.wait_ge(ident_loaded, 16)

            def transpose_rows(i, k):
                e = 2 * i + k
                need(pe, gathered[k], 16 * QT * (i + 1))
                need(pe, xT_ready, e)
                last = None
                for c in range(DC):
                    for q in range(QT):
                        last = pe.transpose(bank[3 + c][:, q * P:(q + 1) * P], xe[:, k, q, c * P:(c + 1) * P], ident[:])
                last.then_inc(xT_done, 1)

            def fc1(i, k):
                e = 2 * i + k
                need(pe, xT_ready, e + 1)
                need(pe, w1_ready, e + 1)
                for m in range(FC):
                    u = FC * e + m
                    need(pe, gelu_ready, u - 1)
                    last = None
                    for s, (a, b) in enumerate(PASSES):
                        for c in range(DC):
                            last = pe.matmul(bank[m % 2][:], w1[:, k, a, c, m * P:(m + 1) * P], xeT[:, b, c, :],
                                             start=(s == 0 and c == 0), stop=(s == 2 and c == DC - 1))
                    last.then_inc(fc1_done, 1)

            def fc2(i, k):
                e = 2 * i + k
                need(pe, h_ready, FC * (e + 1))
                need(pe, w2_ready, e + 1)
                for q in range(QT):
                    u = QT * e + q
                    need(pe, y_step, u - 1)
                    last = None
                    for s, (a, b) in enumerate(PASSES):
                        for m in range(FC):
                            last = pe.matmul(bank[5 + q % 2][:, 0:D], h[:, k, a, m, q * P:(q + 1) * P], w2[:, k, b, m, :],
                                             start=(s == 0 and m == 0), stop=(s == 2 and m == FC - 1))
                    last.then_inc(fc2_done, 1)

            def pair(i):
                for k in range(2):
                    transpose_rows(i, k)
                    if k == 1:
                        fc2(i, 0)
                    elif not isinstance(i, int):
                        fc2(i - 1, 1)
                    fc1(i, k)
            loop(pe, pair)
            fc2(E // 2 - 1, 1)

        @block.scalar
        def _(act):
            def pair(i):
                for k in range(2):
                    e = 2 * i + k
                    need(act, w_loaded, 32 * e + 32)
                    need(act, fc1_done, FC * (e - 1))
                    act.activation(w1[:, k, 0].rearrange("p c n -> p (c n)"), w1_raw[:], ACT.Copy).then_inc(w_high, 1)
                    need(act, fc2_done, QT * (e - 1))
                    act.activation(w2[:, k, 0].rearrange("p c n -> p (c n)"), w2_raw[:], ACT.Copy).then_inc(w_high, 1)
                    need(act, xT_done, e + 1)
                    need(act, fc1_done, FC * e)
                    last = None
                    for c in range(DC):
                        last = act.activation(xeT[:, 0, c], bank[3 + c][:], ACT.Copy)
                    last.then_inc(xT_high, 1)
                    need(act, b_loaded[k], 32 * (i + 1))
                    for m in range(FC):
                        u = FC * e + m
                        need(act, fc1_done, u + 1)
                        need(act, h_ready, u - 1)
                        act.activation(h_full[:, m % 2], bank[m % 2][:], ACT.Gelu, bias=b1[:, k, m:m + 1]).then_inc(gelu_ready, 1)
            loop(act, pair)

        @block.vector
        def _(dve):
            def outputs(i, k):
                e = 2 * i + k
                need(dve, b_loaded[k], 32 * (i + 1))
                need(dve, scattered[k], 16 * QT * i)
                for q in range(QT):
                    u = QT * e + q
                    need(dve, fc2_done, u + 1)
                    dve.tensor_tensor(y[:, k, q], bank[5 + q % 2][:, 0:D], b2[:, k], ALU.add).then_inc(y_step, 1)
                    need(dve, y_step, u + 1)
                    dve.tensor_scalar(y[:, k, q], y[:, k, q], xe[:, k, q, bass.ds(D + e, 1)], None, ALU.mult).then_inc(y_ready, 1)

            def pair(i):
                for k in range(2):
                    e = 2 * i + k
                    need(dve, w_high, 2 * e + 1)
                    dve.tensor_tensor(w1[:, k, 1].rearrange("p c n -> p (c n)"), w1_raw[:], w1[:, k, 0].rearrange("p c n -> p (c n)").bitcast(F32),
                                      ALU.subtract).then_inc(w1_ready, 1)
                    need(dve, xT_high, e + 1)
                    last = None
                    for c in range(DC):
                        last = dve.tensor_tensor(xeT[:, 1, c], bank[3 + c][:], xeT[:, 0, c].bitcast(F32), ALU.subtract)
                    last.then_inc(xT_ready, 1)
                    if k == 1:
                        outputs(i, 0)
                    elif not isinstance(i, int):
                        outputs(i - 1, 1)
                    need(dve, fc2_done, QT * (e - 1))
                    for m in range(FC):
                        u = FC * e + m
                        need(dve, gelu_ready, u + 1)
                        dve.tensor_copy(h[:, k, 0, m], h_full[:, m % 2]).then_inc(h_high, 1)
                        need(dve, h_high, u + 1)
                        dve.tensor_tensor(h[:, k, 1, m], h_full[:, m % 2], h[:, k, 0, m].bitcast(F32), ALU.subtract).then_inc(h_ready, 1)
            loop(dve, pair)
            outputs(E // 2 - 1, 1)


def finish(nc, x2_dram, acc_dram, out_dram, gate_scale):
    with ExitStack() as ctx:
        def sb(name, shape, dt=F32):
            return ctx.enter_context(nc.sbuf_tensor(name, shape, dt))

        def sem(name):
            return ctx.enter_context(nc.semaphore(name))

        S = 4
        x2 = sb("x2_d", [P, 2, S, D])
        acc = sb("acc_d", [P, 2, S, D])
        res = sb("res_d", [P, 2, S, D])
        stats = sb("stats_d", [P, 2, S, 6])
        mv = sb("mv_d", [P, 2, S, 2])
        rstd = sb("rstd_d", [P, 2, S, 1])
        eps_col = sb("eps_d", [P, S, 1])
        minus_half = sb("minus_half_d", [P, S, 1])
        pad = sb("pad_d", [1, 1])
        loaded = [sem(f"d_loaded{k}") for k in range(2)]
        consts = sem("d_consts")
        summed = sem("d_summed")
        stats_made = sem("d_stats")
        var_ready = sem("d_var")
        var_eps = sem("d_var_eps")
        rstd_ready = sem("d_rstd")
        res_ready = sem("d_res")
        stored = [sem(f"d_stored{k}") for k in range(2)]
        STEPS = B // S

        def loop(engine, pair):
            pair(0)
            with engine.Fori(1, STEPS // 2) as i:
                pair(i)

        block = ctx.enter_context(nc.Block())

        @block.sync
        def _(sp):
            def pair(i):
                for k in range(2):
                    n = 2 * i + k
                    need(sp, res_ready, S * (n - 1))
                    sp.dma_start(x2[:, k], x2_dram[:, bass.ts(n, S), :]).then_inc(loaded[k], 16)
                    sp.dma_start(acc[:, k], acc_dram[:, bass.ts(n, S), :]).then_inc(loaded[k], 16)
            loop(sp, pair)

        @block.gpsimd
        def _(pool):
            pool.memset(eps_col[:], EPS).then_inc(consts, 1)
            pool.memset(minus_half[:], -0.5).then_inc(consts, 1)
            pool.wait_ge(consts, 2)

            def pair(i):
                for k in range(2):
                    n = 2 * i + k
                    need(pool, var_ready, S * (n + 1))
                    pool.tensor_tensor(rstd[:, k], mv[:, k, :, 1:2], eps_col[:], ALU.add).then_inc(var_eps, 1)
                    pool.wait_ge(var_eps, n + 1)
                    pool.tensor_tensor(rstd[:, k], rstd[:, k], minus_half[:], ALU.pow).then_inc(rstd_ready, 1)
            loop(pool, pair)

        @block.scalar
        def _(act):
            def pair(i):
                for k in range(2):
                    n = 2 * i + k
                    need(act, res_ready, S * (n + 1))
                    act.dma_start(out_dram[:, bass.ts(n, S), :], res[:, k]).then_inc(stored[k], 16)
            loop(act, pair)
            for k in range(2):
                act.wait_ge(stored[k], 16 * (STEPS // 2))

        @block.vector
        def _(dve):
            def normalise(i, k):
                n = 2 * i + k
                need(dve, rstd_ready, n + 1)
                need(dve, stored[k], 16 * i)
                for s in range(S):
                    dve.tensor_scalar(res[:, k, s], acc[:, k, s], mv[:, k, s, 0:1], rstd[:, k, s], ALU.subtract, ALU.mult).then_inc(res_ready, 1)

            def pair(i):
                for k in range(2):
                    n = 2 * i + k
                    need(dve, loaded[k], 32 * (i + 1))
                    for s in range(S):
                        u = S * n + s
                        dve.scalar_tensor_tensor(acc[:, k, s], acc[:, k, s], gate_scale[:, bass.ts(u, 1)], x2[:, k, s],
                                                 ALU.mult, ALU.add).then_inc(summed, 1)
                    for s in range(S):
                        u = S * n + s
                        need(dve, summed, u + 1)
                        dve.bn_stats(stats[:, k, s], acc[:, k, s]).then_inc(stats_made, 1)
                    need(dve, stats_made, S * (n + 1))
                    dve.memset(pad[:], 0.0)
                    for s in range(S):
                        dve.bn_aggr(mv[:, k, s], stats[:, k, s]).then_inc(var_ready, 1)
                    if k == 1:
                        normalise(i, 0)
                    elif not isinstance(i, int):
                        normalise(i - 1, 1)
            loop(dve, pair)
            normalise(STEPS // 2 - 1, 1)


def decoder_layer(nc, d, x2_dram, rows_dram, logits_dram, acc_dram, slots_dram, out_dram):
    with ExitStack() as ctx:
        probs = ctx.enter_context(nc.sbuf_tensor("probs", [P, B, E], F32))
        slot_rows = ctx.enter_context(nc.sbuf_tensor("slot_rows", [P, E, QT], I32))
        gate_scale = ctx.enter_context(nc.sbuf_tensor("gate_scale", [P, B], F32))
        decoder_attention(nc, d, x2_dram, rows_dram, logits_dram, acc_dram, probs)
        choose_tokens(nc, d, logits_dram, slots_dram, probs, slot_rows, gate_scale)
        run_experts(nc, d, rows_dram, acc_dram, slot_rows)
        finish(nc, x2_dram, acc_dram, out_dram, gate_scale)


def _by_row_chunk(w):
    import numpy as np
    rows, cols = w.shape
    return np.ascontiguousarray(w.reshape(rows // P, P, cols).transpose(1, 0, 2))


def _in_every_partition(v):
    import numpy as np
    return np.ascontiguousarray(np.broadcast_to(v, (P, v.shape[-1])))


def _rope_tables():
    import numpy as np
    half = HD // 2
    theta = (1.0 / 10000.0 ** (np.arange(half, dtype=np.float32) / half)).astype(np.float32)
    ang = np.arange(T, dtype=np.float32)[:, None] * theta[None, :]
    scale = np.repeat(np.array([HD ** -0.5, 1.0], np.float32), H)
    return [np.ascontiguousarray(f(ang).astype(np.float32)[:, None, :] * scale[None, :, None]) for f in (np.cos, np.sin)]


def _layout(v):
    import numpy as np

    def flat(a):
        return np.ascontiguousarray(a.reshape(a.shape[0], -1))

    order = np.arange(D).reshape(H, HD // 2, 2).transpose(0, 2, 1).reshape(-1)
    wt = {k: _by_row_chunk(v[k].T) for k in v if "_W" in k and k != "L0_xattn_Wg"}
    cross = ["Wq_c", "Wk_c", "Wk_s", "Wq_s"]
    cos, sin = _rope_tables()
    a = {
        "x": np.ascontiguousarray(v["x"].transpose(1, 0, 2)),
        "xT": _by_row_chunk(v["x"].reshape(-1, D).T),
        "cT": _by_row_chunk(v["ctx_1024"].reshape(-1, D).T),
        "wqk": flat(np.concatenate([wt["L0_attn_W_q"][:, :, order], wt["L0_attn_W_k"][:, :, order]], axis=2)),
        "wv": flat(wt["L0_attn_W_v"]),
        "wo": flat(wt["L0_attn_W_o"]),
        "wx": flat(np.stack([wt["L0_xattn_" + n] for n in cross], axis=1)),
        "wxv": flat(np.stack([wt["L0_xattn_Wv_s"], wt["L0_xattn_Wv_c"]], axis=1)),
        "wg": flat(_by_row_chunk(v["L0_xattn_Wg"].T)),
        "wr": _by_row_chunk(v["L0_ffn_router_weight"].T),
        "bqkv": _in_every_partition(np.concatenate([v["L0_attn_b_q"][order], v["L0_attn_b_k"][order], v["L0_attn_b_v"]])),
        "bo": _in_every_partition(v["L0_attn_b_o"]),
        "bx": np.ascontiguousarray(np.stack([v["L0_xattn_b" + n[1:]].reshape(DC, P).T for n in cross], axis=1)),
        "bxv": _in_every_partition(np.concatenate([v["L0_xattn_bv_s"], v["L0_xattn_bv_c"]])),
        "bg": _in_every_partition(v["L0_xattn_bg"]),
        "nw": _in_every_partition(v["L0_ffn_norm_weight"]),
        "br": _in_every_partition(v["L0_ffn_router_bias"]),
        "br_col": np.ascontiguousarray(v["L0_ffn_router_bias"].reshape(E, 1)),
        "rope_cos": cos,
        "rope_sin": sin,
        "w1": np.stack([flat(_by_row_chunk(w.T)) for w in v["L0_ffn_fc1_weight"]]),
        "w2": np.stack([flat(_by_row_chunk(w.T)) for w in v["L0_ffn_fc2_weight"]]),
        "b1": np.ascontiguousarray(v["L0_ffn_fc1_bias"].reshape(E, FC, P).transpose(0, 2, 1)),
        "b2": np.ascontiguousarray(v["L0_ffn_fc2_bias"]),
    }
    expert, chunk = np.divmod(np.arange(P), CHUNKS)
    like = expert[:, None] == expert[None, :]
    a["ident"] = np.eye(P, dtype=np.float32)
    a["same_expert"] = like.astype(np.float32)
    a["earlier_chunk"] = (like & (chunk[:, None] < chunk[None, :])).astype(np.float32)
    a["digits_hi"] = _in_every_partition(np.arange(SLOT_HI, dtype=np.float32))
    a["digits_lo"] = _in_every_partition(np.arange(SLOT_LO, dtype=np.float32))
    a["token_no"] = np.arange(P, dtype=np.float32)[:, None]
    a["batch_no"] = _in_every_partition(np.arange(B, dtype=np.float32))
    a["combine"] = np.concatenate([B * np.eye(SLOT_HI), np.eye(SLOT_HI)]).astype(np.float32)
    return a


def kernel(**inputs):
    import numpy as np
    import concourse.bacc as bacc
    from concourse.bass_utils import run_bass_kernel_spmd as run

    arrays = _layout({name: np.asarray(a) for name, a in inputs.items()})
    nc = bacc.Bacc("TRN2", target_bir_lowering=False, num_devices=1)
    d = {name: nc.dram_tensor(f"in_{name}", a.shape, mybir.dt.from_np(a.dtype), kind="ExternalInput").ap()
         for name, a in arrays.items()}
    x2 = nc.dram_tensor("x2_rows", (P, B, D), F32).ap()
    rows = nc.dram_tensor("normed_rows", (P, B, ROW), F32).ap()
    logits = nc.dram_tensor("logits", (E, N), F32).ap()
    acc = nc.dram_tensor("expert_sum", (P, B, D), F32).ap()
    slots = nc.dram_tensor("slots", (E, CAP), I32).ap()
    out = nc.dram_tensor("out_0", (P, B, D), F32, kind="ExternalOutput").ap()
    decoder_layer(nc, d, x2, rows, logits, acc, slots, out)
    r = run(nc, [{f"in_{name}": a for name, a in arrays.items()}], core_ids=[0])
    return np.ascontiguousarray(r.results[0]["out_0"].transpose(1, 0, 2))
```

```python
from contextlib import ExitStack

import concourse.bass as bass
from concourse import mybir

F32 = mybir.dt.float32
F32R = mybir.dt.float32r
BF16 = mybir.dt.bfloat16
I32 = mybir.dt.int32
ALU = mybir.AluOpType
ACT = mybir.ActivationFunctionType
AX_X = mybir.AxisListType.X

P = 128
B = 64
T = 128
D = 256
DC = D // P
H = 16
HD = D // H
N = B * T
G = 2
NG = B // G
GT = G * T
E = 16
F = 1024
FC = F // P
CAP = N // E
ROW = D + E
EPS = 1e-5
QT = CAP // P
SLOT_LO = 32
SLOT_HI = CAP // SLOT_LO
MASKED = -1e30
UNITS = 4
HU = H // UNITS
CHUNKS = P // E
CHUNK = N // CHUNKS
PASSES = ((0, 0), (0, 1), (1, 0))

QC, KC, KS, QS = 0, 1, 2, 3


def need(engine, semaphore, value):
    if isinstance(value, int) and value <= 0:
        return
    engine.wait_ge(semaphore, value)


def decoder_attention(nc, d, x2_dram, rows_dram, logits_dram, acc_dram, probs):
    with ExitStack() as ctx:
        def sb(name, shape, dt=F32):
            return ctx.enter_context(nc.sbuf_tensor(name, shape, dt))

        def sem(name):
            return ctx.enter_context(nc.semaphore(name))

        wqk = sb("wqk", [P, 2, DC, 2 * D], F32R)
        wv = sb("wv", [P, 2, DC, D], F32R)
        wo = sb("wo", [P, 2, DC, D], F32R)
        wx = sb("wx", [P, 2, 4, DC, D], F32R)
        wxv = sb("wxv", [P, 2, 2, DC, D], F32R)
        wg = sb("wg", [P, 2, 2 * DC, D], F32R)
        wr = sb("wr", [P, DC, E])
        WCOLS = DC * (2 * D + D + D + 4 * D + 2 * D + 2 * D)
        shared = sb("shared", [P, WCOLS])
        feat = shared[:, 0:8 * GT].rearrange("p (k c t) -> p k c t", k=4, c=DC)
        values = shared[:, 8 * GT:8 * GT + G * 2 * D].rearrange("p (g n) -> p g n", g=G)
        bqkv = sb("bqkv", [P, 3 * D])
        bo = sb("bo", [P, D])
        bxv = sb("bxv", [P, 2 * D])
        bg = sb("bg", [P, D])
        nw = sb("nw", [P, D])
        br = sb("br", [P, E])
        bx = sb("bx", [P, 4, DC])
        br_col = sb("br_col", [E, 1])
        rope_cos = sb("rope_cos", [P, 2 * H, HD // 2])
        rope_sin = sb("rope_sin", [P, 2 * H, HD // 2])
        ident = sb("ident", [P, P])
        ident_bf = sb("ident_bf", [P, P], BF16)
        mask = sb("mask", [P, HU, T], BF16)
        minus_half = sb("minus_half", [P, 1])
        eps_col = sb("eps_col", [P, 1])
        pool_pad = sb("pool_pad", [1, 1])
        dve_pad = sb("dve_pad", [1, 1])
        zero_tile = sb("zero_tile", [P, D])
        xT_raw = sb("xT_raw", [P, DC, GT])
        cT_raw = sb("cT_raw", [P, DC, GT])
        xT = sb("xT", [P, 2, DC, GT], F32R)
        cT = sb("cT", [P, 2, DC, GT], F32R)
        xb = sb("xb", [P, G, D])
        qkb = sb("qkb", [P, 2, 2 * D])
        by_cos = sb("by_cos", [P, 2 * H, 2, HD // 2])
        by_sin = sb("by_sin", [P, 2 * H, 2, HD // 2])
        roped = sb("roped", [P, 2, 2 * D])
        qkT = sb("qkT", [P, 2, 2, 2 * DC, T], F32R)
        kblock = sb("kblock", [P, 2, DC, H // DC, T], F32R)
        v_aug = sb("v_aug", [P, G, H, 2 * HD])
        nmax = sb("nmax", [P, 8, HU])
        probs_a = sb("probs_a", [P, 4, HU, T])
        probs_T = sb("probs_T", [P, 2, HU, T])
        outT = sb("outT", [P, 2, UNITS, T])
        rec = sb("rec", [P, 2, H])
        heads = sb("heads", [P, 2, D])
        headsT = sb("headsT", [P, 2, 2, DC, T], F32R)
        pre1 = sb("pre1", [P, 2, D])
        stats = sb("stats", [P, 2, 6])
        mv1 = sb("mv1", [P, 2, 2])
        rstd1 = sb("rstd1", [P, 2, 1])
        x1 = sb("x1", [P, G, D])
        x1T = sb("x1T", [P, 2, DC, GT], F32R)
        xnmax = sb("xnmax", [P, 2, 2])
        xbias = sb("xbias", [P, 2, 2])
        xsum = sb("xsum", [P, 2, 2])
        xrec = sb("xrec", [P, 2, 2])
        xprobs = sb("xprobs", [P, 2, 2, T])
        xprobs_T = sb("xprobs_T", [P, 2, 2, T])
        mixed = sb("mixed", [P, 2, 2, D])
        mixedT = sb("mixedT", [P, 2, 2, 2 * DC, T], F32R)
        diff = sb("diff", [P, 2, D])
        base = sb("base", [P, 2, D])
        gate_z = sb("gate_z", [P, 2, D])
        pre2 = sb("pre2", [P, 2, D])
        mv2 = sb("mv2", [P, 2, 2])
        rstd2 = sb("rstd2", [P, 2, 1])
        rrms2 = sb("rrms2", [P, 2, 1])
        x2 = sb("x2", [P, 2, D])
        row = sb("row", [P, 2, ROW])
        xnT = sb("xnT", [P, DC, GT])
        lg = sb("lg", [P, 2, E])
        lmax = sb("lmax", [P, 2, 1])
        lexp = sb("lexp", [P, 2, E])
        lsum = sb("lsum", [P, 2, 1])
        lrec = sb("lrec", [P, 2, 1])
        lgT = sb("lgT", [E, GT])

        bank = [ctx.enter_context(nc.psum_tensor(f"bank{k}", [P, 512], F32)) for k in range(8)]

        w_loaded = sem("w_loaded")
        w_high = sem("w_high")
        w_ready = sem("w_ready")
        consts = sem("consts")
        pool_step = sem("pool_step")
        xT_loaded = [sem(f"xT_loaded{j}") for j in range(G)]
        cT_loaded = sem("cT_loaded")
        x_loaded = sem("x_loaded")
        xT_high = sem("xT_high")
        cT_high = sem("cT_high")
        xT_ready = sem("xT_ready")
        cT_ready = sem("cT_ready")
        xb_ready = sem("xb_ready")
        qk_done = sem("qk_done")
        v_done = sem("v_done")
        qkb_ready = sem("qkb_ready")
        v_ready = sem("v_ready")
        rope_products = sem("rope_products")
        rope_ready = sem("rope_ready")
        qkT_done = sem("qkT_done")
        qkT_high = sem("qkT_high")
        qkT_ready = sem("qkT_ready")
        kblock_ready = [sem(f"kblock_ready{c}") for c in range(DC)]
        scores_ready = sem("scores_ready")
        max_ready = sem("max_ready")
        probs_ready = sem("probs_ready")
        probsT_done = sem("probsT_done")
        probsT_ready = sem("probsT_ready")
        av_done = sem("av_done")
        outT_ready = sem("outT_ready")
        out_done = sem("out_done")
        rec_ready = sem("rec_ready")
        heads_ready = sem("heads_ready")
        headsT_done = sem("headsT_done")
        headsT_high = sem("headsT_high")
        headsT_ready = sem("headsT_ready")
        wo_done = sem("wo_done")
        pre1_ready = sem("pre1_ready")
        stats1 = sem("stats1")
        var1_ready = sem("var1_ready")
        pool1 = sem("pool1")
        rstd1_ready = sem("rstd1_ready")
        x1_ready = sem("x1_ready")
        x1T_done = sem("x1T_done")
        x1T_high = sem("x1T_high")
        x1T_ready = sem("x1T_ready")
        feat_done = sem("feat_done")
        feat_act = sem("feat_act")
        feat_dve = sem("feat_dve")
        xv_done = sem("xv_done")
        xv_ready = sem("xv_ready")
        xscores_done = sem("xscores_done")
        xmax_made = sem("xmax_made")
        xmax_ready = sem("xmax_ready")
        xprobs_ready = sem("xprobs_ready")
        xrec_ready = sem("xrec_ready")
        xprobsT_done = sem("xprobsT_done")
        xprobsT_ready = sem("xprobsT_ready")
        xav_done = sem("xav_done")
        mixed_ready = sem("mixed_ready")
        mixedT_done = sem("mixedT_done")
        mixedT_high = sem("mixedT_high")
        mixedT_ready = sem("mixedT_ready")
        base_ready = sem("base_ready")
        gate_done = sem("gate_done")
        gate_z_ready = sem("gate_z_ready")
        gate_t_ready = sem("gate_t_ready")
        dve_step = sem("dve_step")
        var2_ready = sem("var2_ready")
        pool2 = sem("pool2")
        rstd2_ready = sem("rstd2_ready")
        rrms_ready = sem("rrms_ready")
        x2_ready = sem("x2_ready")
        xn_ready = sem("xn_ready")
        xnT_done = sem("xnT_done")
        xnT_ready = sem("xnT_ready")
        lg_done = sem("lg_done")
        lg_step = sem("lg_step")
        lmax_ready = sem("lmax_ready")
        lrec_ready = sem("lrec_ready")
        lexp_ready = sem("lexp_ready")
        row_ready = sem("row_ready")
        lgT_done = sem("lgT_done")
        lgT_ready = sem("lgT_ready")
        x2_stored = [sem(f"x2_stored{j}") for j in range(G)]
        row_stored = [sem(f"row_stored{j}") for j in range(G)]
        lgT_stored = sem("lgT_stored")
        acc_zeroed = sem("acc_zeroed")

        def hold_dve(dve):
            dve.memset(dve_pad[:], 0.0)

        def hold_pool(pool):
            pool.tensor_tensor(pool_pad[:], eps_col[0:1, :], eps_col[0:1, :], ALU.add)

        block = ctx.enter_context(nc.Block())

        W_PARTS = ((wqk, d["wqk"]), (wv, d["wv"]), (wo, d["wo"]), (wx, d["wx"]), (wxv, d["wxv"]), (wg, d["wg"]))
        CONST_LOADS = ((bqkv, "bqkv"), (bo, "bo"), (bxv, "bxv"), (bg, "bg"), (nw, "nw"), (br, "br"), (bx, "bx"),
                       (br_col, "br_col"), (rope_cos, "rope_cos"), (rope_sin, "rope_sin"), (wr, "wr"))
        N_CONST = 16 * (len(W_PARTS) + len(CONST_LOADS))

        def weight_pieces():
            at = 0
            for tile, src in W_PARTS:
                cols = tile.shape
                width = 1
                for s in cols[2:]:
                    width *= s
                yield tile, src, at, width
                at += width

        def flat(ap):
            names = "abcd"[:len(ap.shape) - 1]
            if len(names) == 1:
                return ap
            return ap.rearrange(f"p {' '.join(names)} -> p ({' '.join(names)})")

        FIRST_FULL, LAST_FULL = 3, NG - 3

        def exists(g):
            return not isinstance(g, int) or 0 <= g < NG

        def passes(engine, body):
            for i in range(-1, FIRST_FULL):
                body(i)
            with engine.Fori(FIRST_FULL, LAST_FULL + 1) as i:
                body(i)
            for i in range(LAST_FULL + 1, NG + 2):
                body(i)

        def units(i):
            for s in range(G * UNITS):
                ahead = (i, (s + 1) // UNITS, (s + 1) % UNITS) if s + 1 < G * UNITS else (i + 1, 0, 0)
                yield s, (i, s // UNITS, s % UNITS), ahead

        @block.sync
        def _(sp):
            def load_x(sp, g, j):
                if not exists(g):
                    return
                n = G * g + j
                need(sp, xT_ready, n - 1)
                sp.dma_start(xT_raw[:, :, j * T:(j + 1) * T], d["xT"][:, :, bass.ts(n, T)]).then_inc(xT_loaded[j], 16)

            for tile, src, at, width in weight_pieces():
                sp.dma_start(shared[:, at:at + width], src).then_inc(w_loaded, 16)
            for tile, name in CONST_LOADS:
                sp.dma_start(tile[:], d[name]).then_inc(w_loaded, 16)
            load_x(sp, 0, 0)
            load_x(sp, 0, 1)

            def kblocks(g, j):
                if not exists(g):
                    return
                n = G * g + j
                need(sp, qkT_ready, n + 1)
                for c in range(DC):
                    need(sp, scores_ready, UNITS * (n - 1) + UNITS // DC * (c + 1))
                    for h in range(H // DC):
                        rows = slice(HD * h, HD * (h + 1))
                        sp.dma_start(kblock[rows, :, c, h, :].bitcast(F32), qkT[rows, j, :, DC + c, :].bitcast(F32)).then_inc(kblock_ready[c], 16)

            def body(i):
                load_x(sp, i + 2, 0)
                kblocks(i, 1)
                if exists(i):
                    need(sp, cT_ready, i)
                    sp.dma_start(cT_raw[:], d["cT"][:, :, bass.ts(i, GT)]).then_inc(cT_loaded, 16)
                    need(sp, pre1_ready, G * i)
                    sp.dma_start(xb[:], d["x"][:, bass.ts(i, G), :]).then_inc(x_loaded, 16)
                    if isinstance(i, int):
                        sp.wait_ge(consts, 1)
                    sp.dma_start(acc_dram[:, bass.ts(i, G), :], zero_tile[:].unsqueeze(1).to_broadcast([P, G, D])).then_inc(acc_zeroed, 16)
                load_x(sp, i + 2, 1)
                kblocks(i + 1, 0)
                if exists(i - 2):
                    for j in range(G):
                        n = G * (i - 2) + j
                        need(sp, x2_ready, n + 1)
                        sp.dma_start(x2_dram[:, bass.ts(n, 1), :], x2[:, j:j + 1, :]).then_inc(x2_stored[j], 16)
                    for j in range(G):
                        n = G * (i - 2) + j
                        need(sp, row_ready, n + 1)
                        sp.dma_start(rows_dram[:, bass.ts(n, 1), :], row[:, j:j + 1, :]).then_inc(row_stored[j], 16)
                    need(sp, lgT_ready, i - 1)
                    sp.dma_start(logits_dram[:, bass.ts(i - 2, GT)], lgT[:]).then_inc(lgT_stored, 16)
            passes(sp, body)
            sp.wait_ge(acc_zeroed, 16 * NG)
            sp.wait_ge(lgT_stored, 16 * NG)
            for j in range(G):
                sp.wait_ge(x2_stored[j], 16 * NG)
                sp.wait_ge(row_stored[j], 16 * NG)

        @block.gpsimd
        def _(pool):
            pool.memset(zero_tile[:], 0.0).then_inc(consts, 1)
            pool.memset(minus_half[:], -0.5).then_inc(consts, 1)
            pool.memset(eps_col[:], EPS).then_inc(consts, 1)
            pool.memset(ident[:], 0.0).then_inc(pool_step, 1)
            pool.memset(ident_bf[:], 0.0).then_inc(pool_step, 1)
            pool.memset(mask[:], 0.0).then_inc(pool_step, 1)
            pool.memset(v_aug[:], 0.0).then_inc(pool_step, 1)
            pool.wait_ge(pool_step, 4)
            for t in (ident, ident_bf):
                pool.affine_select(out=t[:], in_=t[:], compare_op=ALU.not_equal, fill=1.0, base=0,
                                   pattern=[[-1, P]], channel_multiplier=1).then_inc(consts, 1)
            pool.affine_select(out=mask[:], in_=mask[:], compare_op=ALU.is_ge, fill=MASKED, base=0,
                               pattern=[[0, HU], [-1, T]], channel_multiplier=1).then_inc(consts, 1)
            pool.memset(v_aug[:, :, :, HD:HD + 1], 1.0).then_inc(consts, 1)
            pool.memset(kblock[:].bitcast(F32), 0.0).then_inc(consts, 1)
            pool.wait_ge(w_loaded, N_CONST)

            def split_x(g, j):
                if not exists(g):
                    return
                n = G * g + j
                tok = slice(j * T, (j + 1) * T)
                need(pool, xT_loaded[j], 16 * (g + 1))
                need(pool, v_done, n - 1)
                hold_pool(pool)
                pool.tensor_copy(xT[:, 0, :, tok], xT_raw[:, :, tok]).then_inc(xT_high, 1)
                need(pool, xT_high, n + 1)
                pool.tensor_tensor(xT[:, 1, :, tok], xT_raw[:, :, tok], xT[:, 0, :, tok].bitcast(F32), ALU.subtract).then_inc(xT_ready, 1)

            def split_context(g):
                if not exists(g):
                    return
                need(pool, cT_loaded, 16 * (g + 1))
                need(pool, xv_done, G * g)
                hold_pool(pool)
                pool.tensor_copy(cT[:, 0], cT_raw[:]).then_inc(cT_high, 1)
                pool.wait_ge(cT_high, g + 1)
                pool.tensor_tensor(cT[:, 1], cT_raw[:], cT[:, 0].bitcast(F32), ALU.subtract).then_inc(cT_ready, 1)

            def rope_products_of(g, j):
                if not exists(g):
                    return
                n = G * g + j
                v = qkb[:, j].rearrange("p (h two k) -> p h two k", two=2, k=HD // 2)
                both = [P, 2 * H, 2, HD // 2]
                need(pool, rope_ready, n)
                need(pool, qkb_ready, n + 1)
                pool.tensor_tensor(by_cos[:], v, rope_cos[:].unsqueeze(2).to_broadcast(both), ALU.mult).then_inc(rope_products, 1)
                pool.tensor_tensor(by_sin[:], v, rope_sin[:].unsqueeze(2).to_broadcast(both), ALU.mult).then_inc(rope_products, 1)

            def rope_sums(g, j):
                if not exists(g):
                    return
                n = G * g + j
                need(pool, qkT_done, n - 1)
                need(pool, rope_products, 2 * n + 2)
                r = roped[:, j].rearrange("p (h two k) -> p h two k", two=2, k=HD // 2)
                pool.tensor_tensor(r[:, :, 0], by_cos[:, :, 0], by_sin[:, :, 1], ALU.subtract)
                pool.tensor_tensor(r[:, :, 1], by_sin[:, :, 0], by_cos[:, :, 1], ALU.add).then_inc(rope_ready, 1)

            def gate_ends(g, j):
                if not exists(g):
                    return
                n = G * g + j
                need(pool, var2_ready, n - 1)
                need(pool, mixed_ready, n + 1)
                pool.tensor_tensor(diff[:, j], mixed[:, j, 0], mixed[:, j, 1], ALU.subtract)
                pool.tensor_tensor(base[:, j], x1[:, j], mixed[:, j, 1], ALU.add).then_inc(base_ready, 1)

            def norm1_root(g, j):
                if not exists(g):
                    return
                n = G * g + j
                need(pool, x1_ready, n - 1)
                need(pool, var1_ready, n + 1)
                pool.tensor_tensor(rstd1[:, j], mv1[:, j, 1:2], eps_col[:], ALU.add).then_inc(pool1, 1)
                need(pool, pool1, n + 1)
                pool.tensor_tensor(rstd1[:, j], rstd1[:, j], minus_half[:], ALU.pow).then_inc(rstd1_ready, 1)

            def norm2_roots(g, j):
                if not exists(g):
                    return
                n = G * g + j
                var, rstd, rrms = mv2[:, j, 1:2], rstd2[:, j], rrms2[:, j]
                need(pool, xn_ready, n - 1)
                need(pool, var2_ready, n + 1)
                pool.tensor_tensor(rrms, var, eps_col[:], ALU.add).then_inc(pool2, 1)
                need(pool, pool2, 4 * n + 1)
                pool.tensor_tensor(rstd, rrms, minus_half[:], ALU.pow).then_inc(rstd2_ready, 1)
                need(pool, rstd2_ready, n + 1)
                pool.tensor_tensor(rrms, var, rstd, ALU.mult).then_inc(pool2, 1)
                need(pool, pool2, 4 * n + 2)
                pool.tensor_tensor(rrms, rrms, rstd, ALU.mult).then_inc(pool2, 1)
                need(pool, pool2, 4 * n + 3)
                pool.tensor_tensor(rrms, rrms, eps_col[:], ALU.add).then_inc(pool2, 1)
                need(pool, pool2, 4 * n + 4)
                pool.tensor_tensor(rrms, rrms, minus_half[:], ALU.pow).then_inc(rrms_ready, 1)

            def add_bias(g):
                if not exists(g):
                    return
                need(pool, x_loaded, 16 * (g + 1))
                for j in range(G):
                    pool.tensor_tensor(xb[:, j], xb[:, j], bo[:], ALU.add).then_inc(xb_ready, 1)

            def body(i):
                for j in range(G):
                    gate_ends(i - 2, j)
                split_x(i + 1, 1)
                rope_products_of(i + 1, 0)
                norm1_root(i - 1, 1)
                rope_sums(i + 1, 0)
                for j in range(G):
                    norm2_roots(i - 2, j)
                add_bias(i)
                split_x(i + 2, 0)
                rope_products_of(i + 1, 1)
                rope_sums(i + 1, 1)
                norm1_root(i, 0)
                split_context(i)
            split_x(0, 0)
            passes(pool, body)

        @block.tensor
        def _(pe):
            pe.wait_ge(w_ready, 2 * len(W_PARTS))
            pe.wait_ge(consts, 8)

            def split_product(out, stationary, moving, chunks):
                last = None
                for k, (a, b) in enumerate(PASSES):
                    for c in range(chunks):
                        last = pe.matmul(out, stationary(a, c), moving(b, c), start=(k == 0 and c == 0),
                                         stop=(k == len(PASSES) - 1 and c == chunks - 1))
                return last


            def project_qk(g, j):
                if not exists(g):
                    return
                tok = slice(j * T, (j + 1) * T)
                need(pe, xT_ready, G * g + j + 1)
                need(pe, v_ready, G * g + j)
                split_product(bank[5][:], lambda a, c: xT[:, a, c, tok], lambda b, c: wqk[:, b, c, :], DC).then_inc(qk_done, 1)

            def project_v(g, j):
                if not exists(g):
                    return
                tok = slice(j * T, (j + 1) * T)
                need(pe, qkT_ready, G * g + j + 1)
                split_product(bank[5][:, 0:D], lambda a, c: xT[:, a, c, tok], lambda b, c: wv[:, b, c, :], DC).then_inc(v_done, 1)

            def transpose_qk(g, j):
                if not exists(g):
                    return
                n = G * g + j
                if j == 0:
                    need(pe, x1T_ready, g - 1)
                need(pe, rope_ready, n + 1)
                last = None
                for k in range(2 * DC):
                    last = pe.transpose(bank[5][:, k * P:(k + 1) * P], roped[:, j, k * P:(k + 1) * P], ident[:])
                last.then_inc(qkT_done, 1)

            def scores(g, j, t):
                if not exists(g):
                    return
                n = G * g + j
                u = UNITS * n + t
                c = t // (UNITS // DC)
                h0 = HU * (t % (UNITS // DC))
                need(pe, probs_ready, u - 1)
                if t % (UNITS // DC) == 0:
                    need(pe, kblock_ready[c], 16 * (H // DC) * (n + 1))
                pe.matmul(bank[t % 2][:], ident_bf[:], mask[:].rearrange("p h k -> p (h k)"), start=True, stop=False)
                last = None
                for k, (a, b) in enumerate(PASSES):
                    last = pe.matmul(bank[t % 2][:], qkT[:, j, a, c, :], kblock[:, b, c, h0:h0 + HU, :].rearrange("p h k -> p (h k)"),
                                     start=False, stop=(k == len(PASSES) - 1))
                last.then_inc(scores_ready, 1)

            def transpose_probs(g, j, t):
                if not exists(g):
                    return
                u = UNITS * (G * g + j) + t
                if (j, t) == (1, UNITS - 2):
                    need(pe, xnT_ready, G * (g - 1))
                elif (j, t) == (1, UNITS - 1):
                    need(pe, lg_step, G * (g - 1))
                elif (j, t) == (0, 0):
                    need(pe, lgT_ready, g - 2)
                need(pe, probsT_ready, u)
                need(pe, probs_ready, u + 1)
                last = None
                for h in range(HU):
                    last = pe.transpose(bank[2][:, h * T:(h + 1) * T], probs_a[:, t, h], ident[:])
                last.then_inc(probsT_done, 1)

            def weigh_values(g, j, t):
                if not exists(g):
                    return
                n = G * g + j
                if t == 0:
                    need(pe, v_ready, n + 1)
                    need(pe, pre1_ready, n - 1)
                need(pe, probsT_ready, UNITS * n + t + 1)
                last = None
                for h in range(HU):
                    last = pe.matmul(bank[3 + j][2 * HD * h:2 * HD * (h + 1), t * T:(t + 1) * T], v_aug[:, j, HU * t + h, :],
                                     probs_T[:, t % 2, h], start=True, stop=True)
                last.then_inc(av_done, 1)

            def transpose_out(g, j):
                if not exists(g):
                    return
                need(pe, outT_ready, G * g + j + 1)
                last = None
                for t in range(UNITS):
                    last = pe.transpose(bank[3 + j][:, t * P:(t + 1) * P], outT[:, j, t], ident[:])
                last.then_inc(out_done, 1)

            def transpose_heads(g, j):
                if not exists(g):
                    return
                need(pe, heads_ready, G * g + j + 1)
                last = None
                for c in range(DC):
                    last = pe.transpose(bank[3 + j][:, c * P:(c + 1) * P], heads[:, j, c * P:(c + 1) * P], ident[:])
                last.then_inc(headsT_done, 1)

            def project_out(g, j):
                if not exists(g):
                    return
                need(pe, headsT_ready, G * g + j + 1)
                split_product(bank[3 + j][:, 0:D], lambda a, c: headsT[:, j, a, c, :], lambda b, c: wo[:, b, c, :], DC).then_inc(wo_done, 1)

            def transpose_x1(g):
                if not exists(g):
                    return
                need(pe, x1_ready, G * (g + 1))
                if exists(g + 2):
                    need(pe, qkb_ready, G * (g + 2) + 1)
                elif exists(g + 1):
                    need(pe, v_ready, G * (g + 2))
                last = None
                for j in range(G):
                    for c in range(DC):
                        last = pe.transpose(bank[5][:, (DC * j + c) * P:(DC * j + c + 1) * P], x1[:, j, c * P:(c + 1) * P], ident[:])
                last.then_inc(x1T_done, 1)

            def features(g, k):
                if not exists(g):
                    return
                kind = (KS, QS, QC, KC)[k]
                src = cT if k < 2 else x1T
                if k == 0:
                    need(pe, cT_ready, g + 1)
                    need(pe, gate_z_ready, G * g - 1)
                elif k == 1:
                    need(pe, gate_z_ready, G * g)
                elif k == 2:
                    need(pe, x1T_ready, g + 1)
                    need(pe, feat_act, 2 * g + 1)
                else:
                    need(pe, feat_dve, 2 * g + 1)
                last = None
                for m in range(DC):
                    last = split_product(bank[6 + k % 2][:, m * GT:(m + 1) * GT], lambda a, c: wx[:, a, kind, c, m * P:(m + 1) * P],
                                         lambda b, c: src[:, b, c, :], DC)
                last.then_inc(feat_done, 1)

            def cross_values(g, j):
                if not exists(g):
                    return
                tok = slice(j * T, (j + 1) * T)
                need(pe, (feat_act, feat_dve)[j], 2 * g + 2)
                split_product(bank[6 + j][:, 0:D], lambda a, c: cT[:, a, c, tok], lambda b, c: wxv[:, b, 0, c, :], DC)
                split_product(bank[6 + j][:, D:2 * D], lambda a, c: x1T[:, a, c, tok], lambda b, c: wxv[:, b, 1, c, :], DC).then_inc(xv_done, 1)

            def cross_scores(g, j):
                if not exists(g):
                    return
                tok = slice(j * T, (j + 1) * T)
                if j == 0:
                    need(pe, feat_dve, 2 * g + 2)
                need(pe, xv_ready, G * g + j + 1)
                last = None
                for s, (q, k) in enumerate(((QC, KS), (QS, KC))):
                    for c in range(DC):
                        last = pe.matmul(bank[6 + j][:, s * T:(s + 1) * T], feat[:, q, c, tok], feat[:, k, c, tok],
                                         start=(c == 0), stop=(c == DC - 1))
                last.then_inc(xscores_done, 1)

            def transpose_cross(g, j):
                if not exists(g):
                    return
                need(pe, xprobs_ready, G * g + j + 1)
                last = None
                for s in range(2):
                    last = pe.transpose(bank[6 + j][:, s * T:(s + 1) * T], xprobs[:, j, s], ident[:])
                last.then_inc(xprobsT_done, 1)

            def cross_weigh(g, j):
                if not exists(g):
                    return
                need(pe, xprobsT_ready, G * g + j + 1)
                last = None
                for s in range(2):
                    last = pe.matmul(bank[6 + j][:, s * D:(s + 1) * D], xprobs_T[:, j, s], values[:, j, s * D:(s + 1) * D],
                                     start=True, stop=True)
                last.then_inc(xav_done, 1)

            def transpose_mixed(g, j):
                if not exists(g):
                    return
                need(pe, mixed_ready, G * g + j + 1)
                last = None
                for k in range(2 * DC):
                    last = pe.transpose(bank[6 + j][:, k * P:(k + 1) * P], mixed[:, j, k // DC, (k % DC) * P:(k % DC + 1) * P], ident[:])
                last.then_inc(mixedT_done, 1)

            def gate(g, j):
                if not exists(g):
                    return
                need(pe, mixedT_ready, G * g + j + 1)
                split_product(bank[6 + j][:, 0:D], lambda a, c: mixedT[:, j, a, c, :], lambda b, c: wg[:, b, c, :], 2 * DC).then_inc(gate_done, 1)


            def transpose_xn(g, j):
                if not exists(g):
                    return
                need(pe, lgT_ready, g)
                need(pe, xn_ready, G * g + j + 1)
                last = None
                for c in range(DC):
                    last = pe.transpose(bank[2][:, (j * DC + c) * P:(j * DC + c + 1) * P], row[:, j, c * P:(c + 1) * P], ident[:])
                last.then_inc(xnT_done, 1)

            def router(g, j):
                if not exists(g):
                    return
                tok = slice(j * T, (j + 1) * T)
                need(pe, xnT_ready, G * (g + 1))
                last = None
                for c in range(DC):
                    last = pe.matmul(bank[2][:, j * E:(j + 1) * E], xnT[:, c, tok], wr[:, c, :], start=(c == 0), stop=(c == DC - 1))
                last.then_inc(lg_done, 1)

            def router_T(g):
                if not exists(g):
                    return
                need(pe, lmax_ready, G * (g + 1))
                last = None
                for c in range(DC):
                    last = pe.matmul(bank[2][0:E, 0:GT], wr[:, c, :], xnT[:, c, :], start=(c == 0), stop=(c == DC - 1))
                last.then_inc(lgT_done, 1)

            def body(i):
                for s, unit, ahead in units(i):
                    if s == 1:
                        transpose_heads(i - 1, 1)
                    if s == 5:
                        transpose_heads(i, 0)
                    scores(*ahead)
                    transpose_probs(*unit)
                    if s == 0:
                        transpose_out(i - 1, 1)
                        transpose_mixed(i - 2, 0)
                        transpose_mixed(i - 2, 1)
                        transpose_qk(i, 1)
                    if s == 1:
                        gate(i - 2, 0)
                        project_v(i, 1)
                        gate(i - 2, 1)
                    if s == 2:
                        project_qk(i + 1, 0)
                        project_out(i - 1, 1)
                    if s == 3:
                        features(i - 1, 1)
                    if s == 4:
                        transpose_out(i, 0)
                        transpose_qk(i + 1, 0)
                        features(i - 1, 2)
                    if s == 5:
                        project_v(i + 1, 0)
                        features(i - 1, 3)
                    if s == 6:
                        cross_values(i - 1, 1)
                        project_qk(i + 1, 1)
                        project_out(i, 0)
                    if s == 7:
                        transpose_cross(i - 1, 0)
                        transpose_cross(i - 1, 1)
                    weigh_values(*unit)
                    if s == 2:
                        features(i - 1, 0)
                    if s == 3:
                        transpose_x1(i - 1)
                    if s == 5:
                        transpose_xn(i - 2, 0)
                        transpose_xn(i - 2, 1)
                        cross_values(i - 1, 0)
                    if s == 6:
                        router(i - 2, 0)
                        router(i - 2, 1)
                        cross_scores(i - 1, 0)
                        cross_scores(i - 1, 1)
                    if s == 7:
                        router_T(i - 2)
                        cross_weigh(i - 1, 0)
                        cross_weigh(i - 1, 1)
            passes(pe, body)

        @block.scalar
        def _(act):
            act.wait_ge(w_loaded, N_CONST)
            for tile, src, at, width in weight_pieces():
                act.activation(flat(tile[:, 0]), shared[:, at:at + width], ACT.Copy).then_inc(w_high, 1)

            def exponentials(g, j, t):
                if not exists(g):
                    return
                u = UNITS * (G * g + j) + t
                need(act, probsT_done, u - 3)
                need(act, max_ready, u + 1)
                last = None
                for h in range(HU):
                    last = act.activation(probs_a[:, t, h], bank[t % 2][:, h * T:(h + 1) * T], ACT.Exp,
                                          bias=nmax[:, UNITS * j + t, h:h + 1])
                last.then_inc(probs_ready, 1)

            def qkT_out(g, j):
                if not exists(g):
                    return
                n = G * g + j
                need(act, scores_ready, UNITS * (n - 1))
                need(act, qkT_done, n + 1)
                act.activation(qkT[:, j, 0].rearrange("p c t -> p (c t)"), bank[5][:], ACT.Copy).then_inc(qkT_high, 1)

            def out_evacuate(g, j):
                if not exists(g):
                    return
                n = G * g + j
                need(act, out_done, n - 1)
                need(act, av_done, UNITS * (n + 1))
                act.activation(outT[:, j].rearrange("p u t -> p (u t)"), bank[3 + j][:], ACT.Copy).then_inc(outT_ready, 1)

            def heads_out(g, j):
                if not exists(g):
                    return
                n = G * g + j
                need(act, wo_done, n - 1)
                need(act, headsT_done, n + 1)
                act.activation(headsT[:, j, 0].rearrange("p c t -> p (c t)"), bank[3 + j][:, 0:D], ACT.Copy).then_inc(headsT_high, 1)

            def x1T_out(g):
                if not exists(g):
                    return
                need(act, xv_done, G * g)
                need(act, x1T_done, g + 1)
                act.activation(x1T[:, 0].rearrange("p c (j t) -> p j c t", j=G), bank[5][:].rearrange("p (j c t) -> p j c t", j=G, c=DC),
                               ACT.Copy).then_inc(x1T_high, 1)

            def features_out(g, k):
                if not exists(g):
                    return
                kind = (KS, QS, QC, KC)[k]
                need(act, xscores_done, G * g)
                need(act, feat_done, 4 * g + k + 1)
                last = None
                for m in range(DC):
                    last = act.activation(feat[:, kind, m, :], bank[6 + k % 2][:, m * GT:(m + 1) * GT], ACT.Identity, bias=bx[:, kind, m:m + 1])
                last.then_inc(feat_act, 1)

            def cross_exponentials(g, j):
                if not exists(g):
                    return
                n = G * g + j
                need(act, xprobsT_done, n - 1)
                need(act, xmax_ready, n + 1)
                last = None
                for s in range(2):
                    last = act.activation(xprobs[:, j, s], bank[6 + j][:, s * T:(s + 1) * T], ACT.Exp, scale=float(D) ** -0.5,
                                          bias=xbias[:, j, s:s + 1], accum_out=xsum[:, j, s:s + 1])
                last.then_inc(xprobs_ready, 1)

            def cross_probs_out(g, j):
                if not exists(g):
                    return
                n = G * g + j
                need(act, xav_done, n - 1)
                need(act, xprobsT_done, n + 1)
                act.activation(xprobs_T[:, j].rearrange("p s t -> p (s t)"), bank[6 + j][:, 0:2 * T], ACT.Copy).then_inc(xprobsT_ready, 1)

            def mixed_out(g, j):
                if not exists(g):
                    return
                n = G * g + j
                need(act, base_ready, n - 1)
                need(act, mixedT_done, n - 1)
                need(act, xrec_ready, n + 1)
                need(act, xav_done, n + 1)
                last = None
                for s in range(2):
                    last = act.activation(mixed[:, j, s], bank[6 + j][:, s * D:(s + 1) * D], ACT.Copy, scale=xrec[:, j, s:s + 1])
                last.then_inc(mixed_ready, 1)

            def mixedT_out(g, j):
                if not exists(g):
                    return
                n = G * g + j
                need(act, gate_done, n - 1)
                need(act, mixedT_done, n + 1)
                act.activation(mixedT[:, j, 0].rearrange("p c t -> p (c t)"), bank[6 + j][:], ACT.Copy).then_inc(mixedT_high, 1)

            def gate_tanh(g, j):
                if not exists(g):
                    return
                n = G * g + j
                need(act, gate_z_ready, n + 1)
                act.activation(gate_z[:, j], gate_z[:, j], ACT.Tanh, scale=0.5).then_inc(gate_t_ready, 1)

            def xnT_out(g, j):
                if not exists(g):
                    return
                need(act, lgT_done, g)
                need(act, xnT_done, G * (g + 1))
                act.activation(xnT[:, :, j * T:(j + 1) * T], bank[2][:, j * D:(j + 1) * D].rearrange("p (c t) -> p c t", c=DC), ACT.Copy).then_inc(xnT_ready, 1)

            def router_exponentials(g, j):
                if not exists(g):
                    return
                n = G * g + j
                need(act, row_ready, n - 1)
                need(act, lmax_ready, n + 1)
                act.activation(lexp[:, j], lg[:, j], ACT.Exp, bias=lmax[:, j], accum_out=lsum[:, j]).then_inc(lexp_ready, 1)

            def logitsT_out(g):
                if not exists(g):
                    return
                need(act, lgT_stored, 16 * g)
                need(act, lgT_done, g + 1)
                act.activation(lgT[:], bank[2][0:E, 0:GT], ACT.Identity, bias=br_col[:]).then_inc(lgT_ready, 1)

            def body(i):
                for s, unit, ahead in units(i):
                    if s == 0:
                        mixed_out(i - 2, 0)
                        mixed_out(i - 2, 1)
                        out_evacuate(i - 1, 1)
                    if s == 1:
                        heads_out(i - 1, 1)
                    if s == 3:
                        features_out(i - 1, 0)
                    if s == 4:
                        out_evacuate(i, 0)
                    if s == 5:
                        heads_out(i, 0)
                        features_out(i - 1, 2)
                    if s == 7:
                        router_exponentials(i - 2, 0)
                        router_exponentials(i - 2, 1)
                    exponentials(*ahead)
                    if s == 0:
                        mixedT_out(i - 2, 0)
                        mixedT_out(i - 2, 1)
                        qkT_out(i, 1)
                    if s == 2:
                        gate_tanh(i - 2, 0)
                        gate_tanh(i - 2, 1)
                    if s == 3:
                        x1T_out(i - 1)
                    if s == 4:
                        qkT_out(i + 1, 0)
                    if s == 5:
                        xnT_out(i - 2, 0)
                        xnT_out(i - 2, 1)
                    if s == 6:
                        cross_exponentials(i - 1, 0)
                        cross_exponentials(i - 1, 1)
                    if s == 7:
                        cross_probs_out(i - 1, 0)
                        cross_probs_out(i - 1, 1)
                        logitsT_out(i - 2)
            passes(act, body)

        @block.vector
        def _(dve):
            for k, (tile, src, at, width) in enumerate(weight_pieces()):
                dve.wait_ge(w_high, k + 1)
                dve.tensor_tensor(flat(tile[:, 1]), shared[:, at:at + width], flat(tile[:, 0]).bitcast(F32), ALU.subtract).then_inc(w_ready, 2)

            def qk_out(g, j):
                if not exists(g):
                    return
                n = G * g + j
                need(dve, rope_ready, n - 1)
                need(dve, qk_done, n + 1)
                dve.tensor_tensor(qkb[:, j], bank[5][:], bqkv[:, 0:2 * D], ALU.add).then_inc(qkb_ready, 1)

            def v_out(g, j):
                if not exists(g):
                    return
                n = G * g + j
                need(dve, av_done, UNITS * (n - 1))
                need(dve, v_done, n + 1)
                dve.tensor_tensor(v_aug[:, j, :, 0:HD], bank[5][:, 0:D].rearrange("p (h k) -> p h k", h=H),
                                  bqkv[:, 2 * D:3 * D].rearrange("p (h k) -> p h k", h=H), ALU.add).then_inc(v_ready, 1)

            def qkT_low(g, j):
                if not exists(g):
                    return
                need(dve, qkT_high, G * g + j + 1)
                dve.tensor_tensor(qkT[:, j, 1].rearrange("p c t -> p (c t)"), bank[5][:],
                                  qkT[:, j, 0].rearrange("p c t -> p (c t)").bitcast(F32), ALU.subtract).then_inc(qkT_ready, 1)

            def maxima(g, j, t):
                if not exists(g):
                    return
                u = UNITS * (G * g + j) + t
                need(dve, probs_ready, u - 7)
                need(dve, scores_ready, u + 1)
                dve.tensor_reduce(out=nmax[:, UNITS * j + t], in_=bank[t % 2][:].rearrange("p (h k) -> p h k", h=HU),
                                  axis=AX_X, op=ALU.max, negate=True).then_inc(max_ready, 1)

            def probs_out(g, j, t):
                if not exists(g):
                    return
                u = UNITS * (G * g + j) + t
                need(dve, av_done, u - 1)
                need(dve, probsT_done, u + 1)
                dve.tensor_copy(probs_T[:, t % 2].rearrange("p h t -> p (h t)"), bank[2][:]).then_inc(probsT_ready, 1)

            def normalise_heads(g, j):
                if not exists(g):
                    return
                n = G * g + j
                need(dve, headsT_done, n - 1)
                need(dve, out_done, n + 1)
                o = bank[3 + j][:].rearrange("p (h k) -> p h k", h=H)
                dve.reciprocal(rec[:, j].unsqueeze(2), o[:, :, HD:HD + 1]).then_inc(rec_ready, 1)
                need(dve, rec_ready, n + 1)
                dve.tensor_tensor(heads[:, j].rearrange("p (h k) -> p h k", h=H), o[:, :, 0:HD],
                                  rec[:, j].unsqueeze(2).to_broadcast([P, H, HD]), ALU.mult).then_inc(heads_ready, 1)

            def heads_low(g, j):
                if not exists(g):
                    return
                need(dve, headsT_high, G * g + j + 1)
                dve.tensor_tensor(headsT[:, j, 1].rearrange("p c t -> p (c t)"), bank[3 + j][:, 0:D],
                                  headsT[:, j, 0].rearrange("p c t -> p (c t)").bitcast(F32), ALU.subtract).then_inc(headsT_ready, 1)

            def norm1_stats(g, j):
                if not exists(g):
                    return
                n = G * g + j
                need(dve, x1_ready, n - 1)
                need(dve, xb_ready, n + 1)
                need(dve, wo_done, n + 1)
                dve.tensor_tensor(pre1[:, j], bank[3 + j][:, 0:D], xb[:, j], ALU.add).then_inc(pre1_ready, 1)
                need(dve, pre1_ready, n + 1)
                dve.bn_stats(stats[:, 0], pre1[:, j]).then_inc(stats1, 1)
                need(dve, rstd1_ready, n - 1)
                need(dve, stats1, n + 1)
                hold_dve(dve)
                dve.bn_aggr(mv1[:, j], stats[:, 0]).then_inc(var1_ready, 1)

            def norm1(g, j):
                if not exists(g):
                    return
                n = G * g + j
                need(dve, base_ready, n - 1)
                need(dve, x1T_done, g)
                need(dve, rstd1_ready, n + 1)
                dve.tensor_scalar(x1[:, j], pre1[:, j], mv1[:, j, 0:1], rstd1[:, j], ALU.subtract, ALU.mult).then_inc(x1_ready, 1)

            def x1T_low(g):
                if not exists(g):
                    return
                need(dve, x1T_high, g + 1)
                for j in range(G):
                    last = dve.tensor_tensor(x1T[:, 1, :, j * T:(j + 1) * T], bank[5][:, j * D:(j + 1) * D].rearrange("p (c t) -> p c t", c=DC),
                                             x1T[:, 0, :, j * T:(j + 1) * T].bitcast(F32), ALU.subtract)
                last.then_inc(x1T_ready, 1)

            def features_out(g, k):
                if not exists(g):
                    return
                kind = (KS, QS, QC, KC)[k]
                need(dve, xscores_done, G * g)
                need(dve, feat_done, 4 * g + k + 1)
                last = None
                for m in range(DC):
                    last = dve.tensor_scalar(feat[:, kind, m, :], bank[6 + k % 2][:, m * GT:(m + 1) * GT], bx[:, kind, m:m + 1], None, ALU.add)
                last.then_inc(feat_dve, 1)

            def values_out(g, j):
                if not exists(g):
                    return
                n = G * g + j
                need(dve, xav_done, n - 1)
                need(dve, xv_done, n + 1)
                dve.tensor_tensor(values[:, j], bank[6 + j][:], bxv[:], ALU.add).then_inc(xv_ready, 1)

            def cross_maxima(g, j):
                if not exists(g):
                    return
                n = G * g + j
                need(dve, xscores_done, n + 1)
                dve.tensor_reduce(out=xnmax[:, j], in_=bank[6 + j][:, 0:2 * T].rearrange("p (s k) -> p s k", s=2),
                                  axis=AX_X, op=ALU.max, negate=True).then_inc(xmax_made, 1)
                need(dve, xprobs_ready, n - 1)
                need(dve, xmax_made, n + 1)
                dve.tensor_scalar(xbias[:, j], xnmax[:, j], float(D) ** -0.5, None, ALU.mult).then_inc(xmax_ready, 1)

            def cross_reciprocal(g, j):
                if not exists(g):
                    return
                n = G * g + j
                need(dve, mixed_ready, n - 1)
                need(dve, xprobs_ready, n + 1)
                dve.reciprocal(xrec[:, j], xsum[:, j]).then_inc(xrec_ready, 1)

            def mixedT_low(g, j):
                if not exists(g):
                    return
                need(dve, mixedT_high, G * g + j + 1)
                dve.tensor_tensor(mixedT[:, j, 1].rearrange("p c t -> p (c t)"), bank[6 + j][:],
                                  mixedT[:, j, 0].rearrange("p c t -> p (c t)").bitcast(F32), ALU.subtract).then_inc(mixedT_ready, 1)

            def gate_out(g, j):
                if not exists(g):
                    return
                n = G * g + j
                need(dve, gate_done, n + 1)
                dve.tensor_tensor(gate_z[:, j], bank[6 + j][:, 0:D], bg[:], ALU.add).then_inc(gate_z_ready, 1)

            def gate_and_stats(g, j):
                if not exists(g):
                    return
                n = G * g + j
                need(dve, base_ready, n + 1)
                need(dve, gate_t_ready, n + 1)
                dve.scalar_tensor_tensor(diff[:, j], gate_z[:, j], 1.0, diff[:, j], ALU.add, ALU.mult).then_inc(dve_step, 1)
                need(dve, x2_ready, n - 1)
                need(dve, dve_step, 3 * n + 1)
                dve.scalar_tensor_tensor(pre2[:, j], diff[:, j], 0.5, base[:, j], ALU.mult, ALU.add).then_inc(dve_step, 1)
                need(dve, dve_step, 3 * n + 2)
                dve.bn_stats(stats[:, 1], pre2[:, j]).then_inc(dve_step, 1)
                need(dve, rrms_ready, n - 1)
                need(dve, dve_step, 3 * n + 3)
                hold_dve(dve)
                dve.bn_aggr(mv2[:, j], stats[:, 1]).then_inc(var2_ready, 1)

            def norm2(g, j):
                if not exists(g):
                    return
                n = G * g + j
                need(dve, x2_stored[j], 16 * g)
                need(dve, rstd2_ready, n + 1)
                dve.tensor_scalar(x2[:, j], pre2[:, j], mv2[:, j, 0:1], rstd2[:, j], ALU.subtract, ALU.mult).then_inc(x2_ready, 1)

            def rms_norm(g, j):
                if not exists(g):
                    return
                n = G * g + j
                need(dve, row_stored[j], 16 * g)
                need(dve, x2_ready, n + 1)
                need(dve, rrms_ready, n + 1)
                dve.scalar_tensor_tensor(row[:, j, 0:D], x2[:, j], rrms2[:, j], nw[:], ALU.mult, ALU.mult).then_inc(xn_ready, 1)

            def router_maximum(g, j):
                if not exists(g):
                    return
                n = G * g + j
                need(dve, lexp_ready, n - 1)
                need(dve, lg_done, G * (g + 1))
                dve.tensor_tensor(lg[:, j], bank[2][:, j * E:(j + 1) * E], br[:], ALU.add).then_inc(lg_step, 1)
                need(dve, lg_step, n + 1)
                dve.tensor_reduce(out=lmax[:, j], in_=lg[:, j], axis=AX_X, op=ALU.max, negate=True).then_inc(lmax_ready, 1)

            def router_probs(g, j):
                if not exists(g):
                    return
                n = G * g + j
                need(dve, lexp_ready, n + 1)
                dve.reciprocal(lrec[:, j], lsum[:, j]).then_inc(lrec_ready, 1)
                need(dve, lrec_ready, n + 1)
                dve.tensor_scalar(row[:, j, D:ROW], lexp[:, j], lrec[:, j], None, ALU.mult)
                dve.tensor_scalar(probs[:, bass.ts(n, 1), :].rearrange("p o e -> p (o e)"), lexp[:, j], lrec[:, j], None, ALU.mult).then_inc(row_ready, 1)

            def body(i):
                for s, unit, ahead in units(i):
                    if s == 1:
                        heads_low(i - 1, 1)
                    if s == 4:
                        features_out(i - 1, 1)
                    if s == 5:
                        heads_low(i, 0)
                    if s == 6:
                        values_out(i - 1, 0)
                    maxima(*ahead)
                    probs_out(*unit)
                    if s == 0:
                        normalise_heads(i - 1, 1)
                        mixedT_low(i - 2, 0)
                        mixedT_low(i - 2, 1)
                        qkT_low(i, 1)
                    if s == 1:
                        norm1(i - 1, 0)
                        gate_out(i - 2, 0)
                        v_out(i, 1)
                        gate_out(i - 2, 1)
                    if s == 2:
                        qk_out(i + 1, 0)
                        norm1_stats(i - 1, 1)
                    if s == 3:
                        norm1(i - 1, 1)
                        gate_and_stats(i - 2, 0)
                        gate_and_stats(i - 2, 1)
                        x1T_low(i - 1)
                    if s == 4:
                        normalise_heads(i, 0)
                        qkT_low(i + 1, 0)
                        norm2(i - 2, 0)
                        norm2(i - 2, 1)
                        rms_norm(i - 2, 0)
                        rms_norm(i - 2, 1)
                    if s == 5:
                        v_out(i + 1, 0)
                        features_out(i - 1, 3)
                    if s == 6:
                        values_out(i - 1, 1)
                        qk_out(i + 1, 1)
                        norm1_stats(i, 0)
                        router_maximum(i - 2, 0)
                        router_maximum(i - 2, 1)
                        cross_maxima(i - 1, 0)
                        cross_maxima(i - 1, 1)
                    if s == 7:
                        cross_reciprocal(i - 1, 0)
                        cross_reciprocal(i - 1, 1)
                        router_probs(i - 2, 0)
                        router_probs(i - 2, 1)
            passes(dve, body)


def choose_tokens(nc, d, logits_dram, slots_dram, probs, slot_rows, gate_scale):
    with ExitStack() as ctx:
        def sb(name, shape, dt=F32):
            return ctx.enter_context(nc.sbuf_tensor(name, shape, dt))

        def sem(name):
            return ctx.enter_context(nc.semaphore(name))

        keys = sb("keys", [P, CHUNK])
        ones = sb("ones_bf", [P, CHUNK], BF16)
        hits = sb("hits", [P, CHUNK])
        same = sb("same", [P, CHUNK])
        place = sb("place", [P, CHUNK])
        same_expert = sb("same_expert", [P, P])
        earlier_chunk = sb("earlier_chunk", [P, P])
        ident = sb("ident_b", [P, P])
        digits_hi = sb("digits_hi", [P, SLOT_HI])
        digits_lo = sb("digits_lo", [P, SLOT_LO])
        token_no = sb("token_no", [P, 1])
        batch_no = sb("batch_no", [P, B])
        combine = sb("combine", [2 * SLOT_HI, SLOT_HI])
        zeros = sb("zeros_bf", [P, E * SLOT_LO], BF16)
        thr = sb("thr", [P, 1], I32)
        cand = sb("cand", [P, 1], I32)
        bit = sb("bit", [P, 1], I32)
        accept = sb("accept", [P, 1], I32)
        neg = sb("neg", [P, 1])
        pad = sb("pad_b", [1, 1])
        neg_i = sb("neg_i", [P, 1], I32)
        count = sb("count", [P, 1])
        counts = sb("counts", [P, 2])
        left = sb("left", [P, 1])
        before = sb("before", [P, 2])
        slot = sb("slot", [P, CHUNKS, CHUNK // P, E], I32)
        slot_hi = sb("slot_hi", [P, CHUNKS, CHUNK // P * E], I32)
        slot_lo = sb("slot_lo", [P, CHUNKS, CHUNK // P * E], I32)
        gated = sb("gated", [P, B, E])
        gate_sum = sb("gate_sum", [P, B])
        empty = sb("empty", [P, B])
        KB = CHUNK // P
        hot_hi = sb("hot_hi", [P, 2, KB * E, SLOT_HI], BF16)
        hot_ids = sb("hot_ids", [P, 2, KB * E, 2, SLOT_HI], BF16)
        hot_lo = sb("hot_lo", [P, 2, KB * E, SLOT_LO], BF16)
        ids_two = sb("ids_two", [2 * SLOT_HI, E * SLOT_LO])
        ids = sb("ids", [SLOT_HI, E * SLOT_LO], I32)
        total = ctx.enter_context(nc.psum_tensor("total", [P, 512], F32))
        placeT = ctx.enter_context(nc.psum_tensor("placeT", [P, KB, P], F32))
        table = ctx.enter_context(nc.psum_tensor("table", [P, 512], F32))
        table2 = ctx.enter_context(nc.psum_tensor("table2", [P, 512], F32))

        loaded = sem("b_loaded")
        ready = sem("b_consts")
        counted = sem("counted")
        totalled = sem("totalled")
        step = sem("b_step")
        placed = sem("placed")
        transposed = sem("transposed")
        hot_ready = sem("hot_ready")
        table_used = sem("table_used")
        table_done = sem("table_done")
        ids_two_ready = sem("ids_two_ready")
        ids_done = sem("ids_done")
        ids_ready = sem("ids_ready")
        slots_stored = sem("slots_stored")
        slots_loaded = sem("slots_loaded")

        consts = ((same_expert, "same_expert"), (earlier_chunk, "earlier_chunk"), (ident, "ident"), (digits_hi, "digits_hi"),
                  (digits_lo, "digits_lo"), (token_no, "token_no"), (batch_no, "batch_no"), (combine, "combine"))
        block = ctx.enter_context(nc.Block())

        @block.sync
        def _(sp):
            sp.dma_start(keys[:], logits_dram.rearrange("e (c k) -> (e c) k", c=CHUNKS)).then_inc(loaded, 16)
            for tile, name in consts:
                sp.dma_start(tile[:], d[name]).then_inc(loaded, 16)
            sp.wait_ge(ids_ready, 1)
            sp.dma_start(slots_dram.rearrange("e (h l) -> h e l", h=SLOT_HI), ids[:].rearrange("h (e l) -> h e l", e=E)).then_inc(slots_stored, 16)
            sp.wait_ge(slots_stored, 16)
            sp.dma_start(slot_rows[:], slots_dram.rearrange("e (p q) -> p e q", p=P)).then_inc(slots_loaded, 16)
            sp.wait_ge(slots_loaded, 16)

        @block.tensor
        def _(pe):
            pe.wait_ge(loaded, 16 * (1 + len(consts)))
            pe.wait_ge(counted, 1)
            pe.matmul(total[:, 0:1], same_expert[:], count[:], start=True, stop=True).then_inc(totalled, 1)
            with pe.Fori(0, 31) as k:
                pe.wait_ge(counted, k + 2)
                pe.matmul(total[:, 0:1], same_expert[:], count[:], start=True, stop=True).then_inc(totalled, 1)
            pe.wait_ge(counted, 33)
            pe.matmul(total[:, 0:1], same_expert[:], counts[:, 0:1], start=True, stop=True)
            pe.matmul(total[:, 1:2], earlier_chunk[:], counts[:, 1:2], start=True, stop=True).then_inc(totalled, 1)
            pe.wait_ge(counted, 34)
            pe.matmul(total[:, 0:1], earlier_chunk[:], count[:], start=True, stop=True).then_inc(totalled, 1)
            pe.wait_ge(placed, 1)
            last = None
            for k in range(KB):
                last = pe.transpose(placeT[:, k], place[:, k * P:(k + 1) * P], ident[:])
            last.then_inc(transposed, 1)
            pe.wait_ge(ready, 2)
            pe.matmul(table[0:2 * SLOT_HI, :], zeros[:, 0:2 * SLOT_HI], zeros[:], start=True, stop=False)

            def chunk_pair(i):
                last = None
                for b in range(2):
                    pe.wait_ge(hot_ready, 2 * i + b + 1)
                    for k in range(KB * E):
                        e = k % E
                        last = pe.matmul(table[0:2 * SLOT_HI, e * SLOT_LO:(e + 1) * SLOT_LO],
                                         hot_ids[:, b, k].rearrange("p two h -> p (two h)"), hot_lo[:, b, k],
                                         start=False, stop=False, skip_group_check=True)
                    last.then_inc(table_used, 1)
            with pe.Fori(0, CHUNKS // 2) as i:
                chunk_pair(i)
            pe.matmul(table[0:2 * SLOT_HI, :], zeros[:, 0:2 * SLOT_HI], zeros[:], start=False, stop=True).then_inc(table_done, 1)
            pe.wait_ge(ids_two_ready, 1)
            pe.matmul(table2[0:SLOT_HI, :], combine[:], ids_two[:], start=True, stop=True).then_inc(ids_done, 1)

        @block.vector
        def _(dve):
            dve.memset(ones[:], 1.0).then_inc(ready, 1)
            dve.memset(zeros[:], 0.0).then_inc(ready, 1)
            dve.memset(cand[:], 0).then_inc(step, 1)
            dve.memset(bit[:], 1 << 30).then_inc(step, 1)
            dve.wait_ge(loaded, 16 * (1 + len(consts)))
            dve.wait_ge(step, 2)
            cand_f = cand[:].bitcast(F32)

            def count_at_least():
                dve.tensor_scalar(hits[:], keys[:], cand_f, None, ALU.is_ge, ALU.add, accum_out=count[:]).then_inc(counted, 1)

            count_at_least()
            dve.wait_ge(totalled, 1)
            dve.tensor_scalar(neg[:], total[:, 0:1], float(CAP), None, ALU.is_lt).then_inc(step, 1)
            dve.tensor_scalar(neg_i[:], total[:, 0:1], float(CAP), None, ALU.is_lt).then_inc(step, 1)
            dve.wait_ge(step, 4)
            dve.tensor_scalar(thr[:], neg_i[:], 31, None, ALU.logical_shift_left).then_inc(step, 1)
            dve.wait_ge(step, 5)
            dve.tensor_tensor(cand[:], thr[:], bit[:], ALU.bitwise_or).then_inc(step, 1)
            with dve.Fori(0, 31) as k:
                dve.wait_ge(step, 4 * k + 6)
                count_at_least()
                dve.tensor_scalar(bit[:], bit[:], 1, None, ALU.logical_shift_right).then_inc(step, 1)
                dve.wait_ge(totalled, k + 2)
                dve.tensor_scalar(accept[:], total[:, 0:1], float(CAP), neg[:], ALU.is_ge, ALU.not_equal).then_inc(step, 1)
                dve.wait_ge(step, 4 * k + 8)
                dve.memset(pad[:], 0.0)
                dve.copy_predicated(thr[:], accept[:], cand[:]).then_inc(step, 1)
                dve.wait_ge(step, 4 * k + 9)
                dve.tensor_tensor(cand[:], thr[:], bit[:], ALU.bitwise_or).then_inc(step, 1)
            s = 4 * 31 + 6
            dve.wait_ge(step, s)
            dve.tensor_tensor(thr[:], thr[:], neg_i[:], ALU.add).then_inc(step, 1)
            dve.wait_ge(step, s + 1)
            thr_f = thr[:].bitcast(F32)
            dve.tensor_scalar(hits[:], keys[:], thr_f, None, ALU.is_gt, ALU.add, accum_out=counts[:, 0:1])
            dve.tensor_scalar(same[:], keys[:], thr_f, None, ALU.is_equal, ALU.add, accum_out=counts[:, 1:2]).then_inc(counted, 1)
            dve.wait_ge(totalled, 33)
            dve.tensor_scalar(left[:], total[:, 0:1], -1.0, float(CAP), ALU.mult, ALU.add).then_inc(step, 1)
            dve.tensor_copy(before[:, 0:1], total[:, 1:2]).then_inc(step, 1)
            dve.wait_ge(step, s + 3)
            dve.tensor_tensor_scan(place[:], ones[:], same[:], before[:, 0:1], ALU.mult, ALU.add).then_inc(step, 1)
            dve.wait_ge(step, s + 4)
            dve.scalar_tensor_tensor(same[:], place[:], left[:], same[:], ALU.is_le, ALU.mult).then_inc(step, 1)
            dve.wait_ge(step, s + 5)
            dve.scalar_tensor_tensor(hits[:], same[:], 1.0, hits[:], ALU.mult, ALU.add, accum_out=count[:]).then_inc(counted, 1)
            dve.wait_ge(totalled, 34)
            dve.tensor_copy(before[:, 1:2], total[:, 0:1]).then_inc(step, 1)
            dve.wait_ge(step, s + 6)
            dve.tensor_tensor_scan(place[:], ones[:], hits[:], before[:, 1:2], ALU.mult, ALU.add).then_inc(step, 1)
            dve.wait_ge(step, s + 7)
            dve.tensor_tensor(place[:], place[:], hits[:], ALU.mult).then_inc(placed, 1)
            dve.wait_ge(transposed, 1)
            for k in range(KB):
                last = dve.tensor_scalar(slot[:, :, k, :], placeT[:, k].rearrange("p (e c) -> p c e", e=E), -1.0, None, ALU.add)
            last.then_inc(step, 1)
            dve.wait_ge(step, s + 8)
            flat = slot[:].rearrange("p c k e -> p c (k e)")
            dve.tensor_scalar(slot_hi[:], flat, SLOT_LO.bit_length() - 1, None, ALU.arith_shift_right).then_inc(step, 1)
            dve.tensor_scalar(slot_lo[:], flat, SLOT_LO - 1, None, ALU.bitwise_and).then_inc(step, 1)
            dve.scalar_tensor_tensor(gated[:].rearrange("p b e -> p (b e)"), slot[:].rearrange("p c k e -> p (c k e)"), 0.0,
                                     probs[:].rearrange("p b e -> p (b e)"), ALU.is_ge, ALU.mult).then_inc(step, 1)
            dve.wait_ge(step, s + 11)
            dve.tensor_reduce(out=gate_sum[:], in_=gated[:], axis=AX_X, op=ALU.add).then_inc(step, 1)
            dve.wait_ge(step, s + 12)
            dve.tensor_scalar(empty[:], gate_sum[:], 0.0, None, ALU.is_le).then_inc(step, 1)
            dve.wait_ge(step, s + 13)
            dve.tensor_tensor(gate_sum[:], gate_sum[:], empty[:], ALU.add).then_inc(step, 1)
            dve.wait_ge(step, s + 14)
            dve.reciprocal(gate_scale[:], gate_sum[:]).then_inc(step, 1)
            s += 15

            def chunk(c, b, first):
                hi_all = [P, KB * E, SLOT_HI]
                lo_all = [P, KB * E, SLOT_LO]
                dve.tensor_tensor(hot_hi[:, b], slot_hi[:, bass.ts(c, 1)].rearrange("p o n -> p (o n)").unsqueeze(2).to_broadcast(hi_all),
                                  digits_hi[:].unsqueeze(1).to_broadcast(hi_all), ALU.is_equal).then_inc(step, 1)
                if not first:
                    dve.wait_ge(table_used, c - 1)
                dve.tensor_tensor(hot_lo[:, b], slot_lo[:, bass.ts(c, 1)].rearrange("p o n -> p (o n)").unsqueeze(2).to_broadcast(lo_all),
                                  digits_lo[:].unsqueeze(1).to_broadcast(lo_all), ALU.is_equal)
                dve.wait_ge(step, s + c + 1)
                dve.tensor_scalar(hot_ids[:, b, :, 0], hot_hi[:, b], token_no[:], None, ALU.mult)
                dve.tensor_tensor(hot_ids[:, b, :, 1].rearrange("p (k e) h -> p k e h", e=E),
                                  hot_hi[:, b].rearrange("p (k e) h -> p k e h", e=E),
                                  batch_no[:, bass.ts(c, KB)].unsqueeze(2).unsqueeze(3).to_broadcast([P, KB, E, SLOT_HI]), ALU.mult).then_inc(hot_ready, 1)
            for b in range(2):
                chunk(b, b, True)
            with dve.Fori(1, CHUNKS // 2) as i:
                for b in range(2):
                    chunk(2 * i + b, b, False)
            dve.wait_ge(table_done, 1)
            dve.tensor_copy(ids_two[:], table[0:2 * SLOT_HI, :]).then_inc(ids_two_ready, 1)
            dve.wait_ge(ids_done, 1)
            dve.tensor_copy(ids[:], table2[0:SLOT_HI, :]).then_inc(ids_ready, 1)


def run_experts(nc, d, rows_dram, acc_dram, slot_rows):
    with ExitStack() as ctx:
        def sb(name, shape, dt=F32):
            return ctx.enter_context(nc.sbuf_tensor(name, shape, dt))

        def sem(name):
            return ctx.enter_context(nc.semaphore(name))

        ident = sb("ident_c", [P, P])
        w1_raw = sb("w1_raw", [P, DC * F])
        w2_raw = sb("w2_raw", [P, FC * D])
        w1 = sb("w1", [P, 2, 2, DC, F], F32R)
        w2 = sb("w2", [P, 2, 2, FC, D], F32R)
        b1 = sb("b1", [P, 2, FC])
        b2 = sb("b2", [P, 2, D])
        gather_rows = sb("gather_rows", [P, 2, QT], I32)
        scatter_rows = sb("scatter_rows", [P, 2, QT], I32)
        gates = sb("gates", [P, 2, QT])
        xe = sb("xe", [P, 2, QT, ROW])
        xeT = sb("xeT", [P, 2, DC, CAP], F32R)
        h_full = sb("h_full", [P, 2, CAP])
        h = sb("h", [P, 2, 2, FC, CAP], F32R)
        y = sb("y", [P, 2, QT, D])
        pool_pad = sb("pool_pad_c", [1, 10])
        pool_one = sb("pool_one_c", [1, 1])
        bank = [ctx.enter_context(nc.psum_tensor(f"cbank{k}", [P, 512], F32)) for k in range(7)]

        ident_loaded = sem("ident_loaded")
        w_loaded = sem("ew_loaded")
        w_high = sem("ew_high")
        w1_ready = sem("w1_ready")
        w2_ready = sem("w2_ready")
        b_loaded = [sem(f"eb_loaded{k}") for k in range(2)]
        one_ready = sem("one_ready")
        gather_rows_ready = sem("gather_rows_ready")
        scatter_rows_ready = sem("scatter_rows_ready")
        gathered = [sem(f"gathered{k}") for k in range(2)]
        xT_done = sem("exT_done")
        xT_high = sem("exT_high")
        xT_ready = sem("exT_ready")
        fc1_done = sem("fc1_done")
        gelu_ready = sem("gelu_ready")
        h_high = sem("h_high")
        h_ready = sem("h_ready")
        fc2_done = sem("fc2_done")
        y_step = sem("y_step")
        gates_ready = sem("gates_ready")
        y_ready = sem("y_ready")
        scattered = [sem(f"scattered{k}") for k in range(2)]

        def loop(engine, pair):
            pair(0)
            with engine.Fori(1, E // 2) as i:
                pair(i)

        block = ctx.enter_context(nc.Block())

        @block.sync
        def _(sp):
            sp.dma_start(ident[:], d["ident"]).then_inc(ident_loaded, 16)

            def pair(i):
                experts = [sp.snap(2 * i + k) if not isinstance(i, int) else 2 * i + k for k in range(2)]
                for k, e in enumerate(experts):
                    need(sp, w1_ready, e)
                    sp.dma_start(w1_raw[:], d["w1"][bass.ts(e, 1)].rearrange("o p n -> p (o n)")).then_inc(w_loaded, 16)
                    need(sp, w2_ready, e)
                    sp.dma_start(w2_raw[:], d["w2"][bass.ts(e, 1)].rearrange("o p n -> p (o n)")).then_inc(w_loaded, 16)
                    need(sp, y_step, QT * (e - 1))
                    sp.dma_start(b1[:, k], d["b1"][bass.ts(e, 1)].rearrange("o p n -> p (o n)")).then_inc(b_loaded[k], 16)
                    sp.dma_start(b2[:, k], d["b2"][bass.ts(e, 1)].rearrange("o n -> (o n)").partition_broadcast(P)).then_inc(b_loaded[k], 16)
            loop(sp, pair)

        @block.gpsimd
        def _(pool):
            pool.memset(pool_one[:], 1.0).then_inc(one_ready, 1)
            pool.wait_ge(one_ready, 1)
            rows_all = rows_dram.rearrange("p b n -> (p b) n")
            acc_all = acc_dram.rearrange("p b n -> (p b) n")

            def hold(place):
                pool.tensor_tensor(pool_pad[:, place:place + 1], pool_one[:], pool_one[:], ALU.add)

            def gather(i, k):
                e = 2 * i + k
                if isinstance(e, int) and e >= E:
                    return
                need(pool, gathered[k], 16 * QT * i)
                need(pool, xT_ready, e - 1)
                hold(k)
                pool.tensor_copy(gather_rows[:, k], slot_rows[:, bass.ts(e, 1)].rearrange("p o q -> p (o q)")).then_inc(gather_rows_ready, 1)
                pool.wait_ge(gather_rows_ready, e + 1)
                hold(2 + k)
                for q in range(QT):
                    pool.indirect_dma_start(xe[:, k, q], None, rows_all, bass.IndirectOffsetOnAxis(ap=gather_rows[:, k, q:q + 1], axis=0)
                                            ).then_inc(gathered[k], 16)

            def scatter(i, k):
                e = 2 * i + k
                need(pool, scattered[k], 16 * QT * i)
                hold(4 + k)
                pool.tensor_copy(scatter_rows[:, k], slot_rows[:, bass.ts(e, 1)].rearrange("p o q -> p (o q)")).then_inc(scatter_rows_ready, 1)
                need(pool, y_ready, QT * (e + 1))
                need(pool, scattered[1 - k], 16 * QT * (i + k))
                need(pool, scatter_rows_ready, e + 1)
                hold(6 + k)
                for q in range(QT):
                    pool.indirect_dma_start(acc_all, bass.IndirectOffsetOnAxis(ap=scatter_rows[:, k, q:q + 1], axis=0), y[:, k, q], None,
                                            compute_op=ALU.add).then_inc(scattered[k], 16)

            def pair(i):
                for k in range(2):
                    e = 2 * i + k
                    gather(i + k, 1 - k)
                    need(pool, w_high, 2 * e + 2)
                    pool.tensor_tensor(w2[:, k, 1].rearrange("p c n -> p (c n)"), w2_raw[:], w2[:, k, 0].rearrange("p c n -> p (c n)").bitcast(F32),
                                       ALU.subtract).then_inc(w2_ready, 1)
                    if k == 1:
                        scatter(i, 0)
                    elif not (isinstance(i, int) and i == 0):
                        scatter(i - 1, 1)
            gather(0, 0)
            pair(0)
            with pool.Fori(1, E // 2 - 1) as i:
                pair(i)
            pair(E // 2 - 1)
            scatter(E // 2 - 1, 1)
            for k in range(2):
                pool.wait_ge(scattered[k], 16 * QT * (E // 2))

        @block.tensor
        def _(pe):
            pe.wait_ge(ident_loaded, 16)

            def transpose_rows(i, k):
                e = 2 * i + k
                need(pe, gathered[k], 16 * QT * (i + 1))
                need(pe, xT_ready, e)
                last = None
                for c in range(DC):
                    for q in range(QT):
                        last = pe.transpose(bank[3 + c][:, q * P:(q + 1) * P], xe[:, k, q, c * P:(c + 1) * P], ident[:])
                last.then_inc(xT_done, 1)

            def fc1(i, k):
                e = 2 * i + k
                need(pe, xT_ready, e + 1)
                need(pe, w1_ready, e + 1)
                for m in range(FC):
                    u = FC * e + m
                    need(pe, gelu_ready, u - 1)
                    last = None
                    for s, (a, b) in enumerate(PASSES):
                        for c in range(DC):
                            last = pe.matmul(bank[m % 2][:], w1[:, k, a, c, m * P:(m + 1) * P], xeT[:, b, c, :],
                                             start=(s == 0 and c == 0), stop=(s == 2 and c == DC - 1))
                    last.then_inc(fc1_done, 1)

            def fc2(i, k):
                e = 2 * i + k
                need(pe, h_ready, FC * (e + 1))
                need(pe, w2_ready, e + 1)
                for q in range(QT):
                    u = QT * e + q
                    need(pe, y_step, u - 1)
                    last = None
                    for s, (a, b) in enumerate(PASSES):
                        for m in range(FC):
                            last = pe.matmul(bank[5 + q % 2][:, 0:D], h[:, k, a, m, q * P:(q + 1) * P], w2[:, k, b, m, :],
                                             start=(s == 0 and m == 0), stop=(s == 2 and m == FC - 1))
                    last.then_inc(fc2_done, 1)

            def pair(i):
                for k in range(2):
                    transpose_rows(i, k)
                    if k == 1:
                        fc2(i, 0)
                    elif not isinstance(i, int):
                        fc2(i - 1, 1)
                    fc1(i, k)
            loop(pe, pair)
            fc2(E // 2 - 1, 1)

        @block.scalar
        def _(act):
            def pair(i):
                for k in range(2):
                    e = 2 * i + k
                    need(act, w_loaded, 32 * e + 32)
                    need(act, fc1_done, FC * (e - 1))
                    act.activation(w1[:, k, 0].rearrange("p c n -> p (c n)"), w1_raw[:], ACT.Copy).then_inc(w_high, 1)
                    need(act, fc2_done, QT * (e - 1))
                    act.activation(w2[:, k, 0].rearrange("p c n -> p (c n)"), w2_raw[:], ACT.Copy).then_inc(w_high, 1)
                    need(act, xT_done, e + 1)
                    need(act, fc1_done, FC * e)
                    last = None
                    for c in range(DC):
                        last = act.activation(xeT[:, 0, c], bank[3 + c][:], ACT.Copy)
                    last.then_inc(xT_high, 1)
                    need(act, b_loaded[k], 32 * (i + 1))
                    for m in range(FC):
                        u = FC * e + m
                        need(act, fc1_done, u + 1)
                        need(act, h_ready, u - 1)
                        act.activation(h_full[:, m % 2], bank[m % 2][:], ACT.Gelu, bias=b1[:, k, m:m + 1]).then_inc(gelu_ready, 1)
            loop(act, pair)

        @block.vector
        def _(dve):
            def outputs(i, k):
                e = 2 * i + k
                need(dve, b_loaded[k], 32 * (i + 1))
                need(dve, scattered[k], 16 * QT * i)
                need(dve, gates_ready, e + 1)
                for q in range(QT):
                    u = QT * e + q
                    need(dve, fc2_done, u + 1)
                    dve.tensor_tensor(y[:, k, q], bank[5 + q % 2][:, 0:D], b2[:, k], ALU.add).then_inc(y_step, 1)
                    need(dve, y_step, u + 1)
                    dve.tensor_scalar(y[:, k, q], y[:, k, q], gates[:, k, q:q + 1], None, ALU.mult).then_inc(y_ready, 1)

            def pair(i):
                for k in range(2):
                    e = 2 * i + k
                    need(dve, w_high, 2 * e + 1)
                    dve.tensor_tensor(w1[:, k, 1].rearrange("p c n -> p (c n)"), w1_raw[:], w1[:, k, 0].rearrange("p c n -> p (c n)").bitcast(F32),
                                      ALU.subtract).then_inc(w1_ready, 1)
                    need(dve, xT_high, e + 1)
                    dve.tensor_copy(gates[:, k].unsqueeze(2), xe[:, k, :, bass.ds(D + e, 1)]).then_inc(gates_ready, 1)
                    last = None
                    for c in range(DC):
                        last = dve.tensor_tensor(xeT[:, 1, c], bank[3 + c][:], xeT[:, 0, c].bitcast(F32), ALU.subtract)
                    last.then_inc(xT_ready, 1)
                    if k == 1:
                        outputs(i, 0)
                    elif not isinstance(i, int):
                        outputs(i - 1, 1)
                    need(dve, fc2_done, QT * (e - 1))
                    for m in range(FC):
                        u = FC * e + m
                        need(dve, gelu_ready, u + 1)
                        dve.tensor_copy(h[:, k, 0, m], h_full[:, m % 2]).then_inc(h_high, 1)
                        need(dve, h_high, u + 1)
                        dve.tensor_tensor(h[:, k, 1, m], h_full[:, m % 2], h[:, k, 0, m].bitcast(F32), ALU.subtract).then_inc(h_ready, 1)
            loop(dve, pair)
            outputs(E // 2 - 1, 1)


def finish(nc, x2_dram, acc_dram, out_dram, gate_scale):
    with ExitStack() as ctx:
        def sb(name, shape, dt=F32):
            return ctx.enter_context(nc.sbuf_tensor(name, shape, dt))

        def sem(name):
            return ctx.enter_context(nc.semaphore(name))

        S = 4
        BUFS = 4
        x2 = sb("x2_d", [P, BUFS, S, D])
        acc = sb("acc_d", [P, BUFS, S, D])
        res = sb("res_d", [P, BUFS, S, D])
        stats = sb("stats_d", [P, BUFS, S, 6])
        mv = sb("mv_d", [P, BUFS, S, 2])
        rstd = sb("rstd_d", [P, BUFS, S, 1])
        eps_col = sb("eps_d", [P, S, 1])
        minus_half = sb("minus_half_d", [P, S, 1])
        pad = sb("pad_d", [1, 1])
        loaded = [sem(f"d_loaded{k}") for k in range(BUFS)]
        consts = sem("d_consts")
        summed = sem("d_summed")
        stats_made = sem("d_stats")
        var_ready = sem("d_var")
        var_eps = sem("d_var_eps")
        rstd_ready = sem("d_rstd")
        res_ready = sem("d_res")
        stored = [sem(f"d_stored{k}") for k in range(BUFS)]
        STEPS = B // S

        def loop(engine, round_of_buffers):
            round_of_buffers(0)
            with engine.Fori(1, STEPS // BUFS) as i:
                round_of_buffers(i)

        block = ctx.enter_context(nc.Block())

        @block.sync
        def _(sp):
            def round_of_buffers(i):
                for k in range(BUFS):
                    n = BUFS * i + k
                    need(sp, res_ready, S * (n - BUFS + 1))
                    sp.dma_start(x2[:, k], x2_dram[:, bass.ts(n, S), :]).then_inc(loaded[k], 16)
                    sp.dma_start(acc[:, k], acc_dram[:, bass.ts(n, S), :]).then_inc(loaded[k], 16)
            loop(sp, round_of_buffers)

        @block.gpsimd
        def _(pool):
            pool.memset(eps_col[:], EPS).then_inc(consts, 1)
            pool.memset(minus_half[:], -0.5).then_inc(consts, 1)
            pool.wait_ge(consts, 2)

            def round_of_buffers(i):
                for k in range(BUFS):
                    n = BUFS * i + k
                    need(pool, var_ready, S * (n + 1))
                    pool.tensor_tensor(rstd[:, k], mv[:, k, :, 1:2], eps_col[:], ALU.add).then_inc(var_eps, 1)
                    pool.wait_ge(var_eps, n + 1)
                    pool.tensor_tensor(rstd[:, k], rstd[:, k], minus_half[:], ALU.pow).then_inc(rstd_ready, 1)
            loop(pool, round_of_buffers)

        @block.scalar
        def _(act):
            def round_of_buffers(i):
                for k in range(BUFS):
                    n = BUFS * i + k
                    need(act, res_ready, S * (n + 1))
                    act.dma_start(out_dram[:, bass.ts(n, S), :], res[:, k]).then_inc(stored[k], 16)
            loop(act, round_of_buffers)
            for k in range(BUFS):
                act.wait_ge(stored[k], 16 * (STEPS // BUFS))

        @block.vector
        def _(dve):
            def normalise(i, k):
                n = BUFS * i + k
                need(dve, rstd_ready, n + 1)
                need(dve, stored[k], 16 * i)
                for s in range(S):
                    dve.tensor_scalar(res[:, k, s], acc[:, k, s], mv[:, k, s, 0:1], rstd[:, k, s], ALU.subtract, ALU.mult).then_inc(res_ready, 1)

            def round_of_buffers(i):
                for k in range(BUFS):
                    n = BUFS * i + k
                    need(dve, loaded[k], 32 * (i + 1))
                    for s in range(S):
                        u = S * n + s
                        dve.scalar_tensor_tensor(acc[:, k, s], acc[:, k, s], gate_scale[:, bass.ts(u, 1)], x2[:, k, s],
                                                 ALU.mult, ALU.add).then_inc(summed, 1)
                    for s in range(S):
                        u = S * n + s
                        need(dve, summed, u + 1)
                        dve.bn_stats(stats[:, k, s], acc[:, k, s]).then_inc(stats_made, 1)
                    need(dve, stats_made, S * (n + 1))
                    dve.memset(pad[:], 0.0)
                    for s in range(S):
                        dve.bn_aggr(mv[:, k, s], stats[:, k, s]).then_inc(var_ready, 1)
                    if k > 0:
                        normalise(i, k - 1)
                    elif not isinstance(i, int):
                        normalise(i - 1, BUFS - 1)
            loop(dve, round_of_buffers)
            normalise(STEPS // BUFS - 1, BUFS - 1)


def decoder_layer(nc, d, x2_dram, rows_dram, logits_dram, acc_dram, slots_dram, out_dram):
    with ExitStack() as ctx:
        probs = ctx.enter_context(nc.sbuf_tensor("probs", [P, B, E], F32))
        slot_rows = ctx.enter_context(nc.sbuf_tensor("slot_rows", [P, E, QT], I32))
        gate_scale = ctx.enter_context(nc.sbuf_tensor("gate_scale", [P, B], F32))
        decoder_attention(nc, d, x2_dram, rows_dram, logits_dram, acc_dram, probs)
        choose_tokens(nc, d, logits_dram, slots_dram, probs, slot_rows, gate_scale)
        run_experts(nc, d, rows_dram, acc_dram, slot_rows)
        finish(nc, x2_dram, acc_dram, out_dram, gate_scale)


def _by_row_chunk(w):
    import numpy as np
    rows, cols = w.shape
    return np.ascontiguousarray(w.reshape(rows // P, P, cols).transpose(1, 0, 2))


def _in_every_partition(v):
    import numpy as np
    return np.ascontiguousarray(np.broadcast_to(v, (P, v.shape[-1])))


def _rope_tables():
    import numpy as np
    half = HD // 2
    theta = (1.0 / 10000.0 ** (np.arange(half, dtype=np.float32) / half)).astype(np.float32)
    ang = np.arange(T, dtype=np.float32)[:, None] * theta[None, :]
    scale = np.repeat(np.array([HD ** -0.5, 1.0], np.float32), H)
    return [np.ascontiguousarray(f(ang).astype(np.float32)[:, None, :] * scale[None, :, None]) for f in (np.cos, np.sin)]


def _layout(v):
    import numpy as np

    def flat(a):
        return np.ascontiguousarray(a.reshape(a.shape[0], -1))

    order = np.arange(D).reshape(H, HD // 2, 2).transpose(0, 2, 1).reshape(-1)
    wt = {k: _by_row_chunk(v[k].T) for k in v if "_W" in k and k != "L0_xattn_Wg"}
    cross = ["Wq_c", "Wk_c", "Wk_s", "Wq_s"]
    cos, sin = _rope_tables()
    a = {
        "x": np.ascontiguousarray(v["x"].transpose(1, 0, 2)),
        "xT": _by_row_chunk(v["x"].reshape(-1, D).T),
        "cT": _by_row_chunk(v["ctx_1024"].reshape(-1, D).T),
        "wqk": flat(np.concatenate([wt["L0_attn_W_q"][:, :, order], wt["L0_attn_W_k"][:, :, order]], axis=2)),
        "wv": flat(wt["L0_attn_W_v"]),
        "wo": flat(wt["L0_attn_W_o"]),
        "wx": flat(np.stack([wt["L0_xattn_" + n] for n in cross], axis=1)),
        "wxv": flat(np.stack([wt["L0_xattn_Wv_s"], wt["L0_xattn_Wv_c"]], axis=1)),
        "wg": flat(_by_row_chunk(v["L0_xattn_Wg"].T)),
        "wr": _by_row_chunk(v["L0_ffn_router_weight"].T),
        "bqkv": _in_every_partition(np.concatenate([v["L0_attn_b_q"][order], v["L0_attn_b_k"][order], v["L0_attn_b_v"]])),
        "bo": _in_every_partition(v["L0_attn_b_o"]),
        "bx": np.ascontiguousarray(np.stack([v["L0_xattn_b" + n[1:]].reshape(DC, P).T for n in cross], axis=1)),
        "bxv": _in_every_partition(np.concatenate([v["L0_xattn_bv_s"], v["L0_xattn_bv_c"]])),
        "bg": _in_every_partition(v["L0_xattn_bg"]),
        "nw": _in_every_partition(v["L0_ffn_norm_weight"]),
        "br": _in_every_partition(v["L0_ffn_router_bias"]),
        "br_col": np.ascontiguousarray(v["L0_ffn_router_bias"].reshape(E, 1)),
        "rope_cos": cos,
        "rope_sin": sin,
        "w1": np.stack([flat(_by_row_chunk(w.T)) for w in v["L0_ffn_fc1_weight"]]),
        "w2": np.stack([flat(_by_row_chunk(w.T)) for w in v["L0_ffn_fc2_weight"]]),
        "b1": np.ascontiguousarray(v["L0_ffn_fc1_bias"].reshape(E, FC, P).transpose(0, 2, 1)),
        "b2": np.ascontiguousarray(v["L0_ffn_fc2_bias"]),
    }
    expert, chunk = np.divmod(np.arange(P), CHUNKS)
    like = expert[:, None] == expert[None, :]
    a["ident"] = np.eye(P, dtype=np.float32)
    a["same_expert"] = like.astype(np.float32)
    a["earlier_chunk"] = (like & (chunk[:, None] < chunk[None, :])).astype(np.float32)
    a["digits_hi"] = _in_every_partition(np.arange(SLOT_HI, dtype=np.float32))
    a["digits_lo"] = _in_every_partition(np.arange(SLOT_LO, dtype=np.float32))
    a["token_no"] = np.arange(P, dtype=np.float32)[:, None]
    a["batch_no"] = _in_every_partition(np.arange(B, dtype=np.float32))
    a["combine"] = np.concatenate([B * np.eye(SLOT_HI), np.eye(SLOT_HI)]).astype(np.float32)
    return a


def kernel(**inputs):
    import numpy as np
    import concourse.bacc as bacc
    from concourse.bass_utils import run_bass_kernel_spmd as run

    arrays = _layout({name: np.asarray(a) for name, a in inputs.items()})
    nc = bacc.Bacc("TRN2", target_bir_lowering=False, num_devices=1)
    d = {name: nc.dram_tensor(f"in_{name}", a.shape, mybir.dt.from_np(a.dtype), kind="ExternalInput").ap()
         for name, a in arrays.items()}
    x2 = nc.dram_tensor("x2_rows", (P, B, D), F32).ap()
    rows = nc.dram_tensor("normed_rows", (P, B, ROW), F32).ap()
    logits = nc.dram_tensor("logits", (E, N), F32).ap()
    acc = nc.dram_tensor("expert_sum", (P, B, D), F32).ap()
    slots = nc.dram_tensor("slots", (E, CAP), I32).ap()
    out = nc.dram_tensor("out_0", (P, B, D), F32, kind="ExternalOutput").ap()
    decoder_layer(nc, d, x2, rows, logits, acc, slots, out)
    r = run(nc, [{f"in_{name}": a for name, a in arrays.items()}], core_ids=[0])
    return np.ascontiguousarray(r.results[0]["out_0"].transpose(1, 0, 2))
```

```python
from contextlib import ExitStack

import concourse.bass as bass
from concourse import mybir

F32 = mybir.dt.float32
F32R = mybir.dt.float32r
BF16 = mybir.dt.bfloat16
I32 = mybir.dt.int32
ALU = mybir.AluOpType
ACT = mybir.ActivationFunctionType
AX_X = mybir.AxisListType.X

P = 128
B = 64
T = 128
D = 256
DC = D // P
H = 16
HD = D // H
N = B * T
G = 2
NG = B // G
GT = G * T
E = 16
F = 1024
FC = F // P
CAP = N // E
ROW = D + E
EPS = 1e-5
QT = CAP // P
SLOT_LO = 32
SLOT_HI = CAP // SLOT_LO
MASKED = -1e30
UNITS = 4
HU = H // UNITS
CHUNKS = P // E
CHUNK = N // CHUNKS
PASSES = ((0, 0), (0, 1), (1, 0))

QC, KC, KS, QS = 0, 1, 2, 3


def need(engine, semaphore, value):
    if isinstance(value, int) and value <= 0:
        return
    engine.wait_ge(semaphore, value)


def decoder_attention(nc, d, x2_dram, rows_dram, logits_dram, probs):
    with ExitStack() as ctx:
        def sb(name, shape, dt=F32):
            return ctx.enter_context(nc.sbuf_tensor(name, shape, dt))

        def sem(name):
            return ctx.enter_context(nc.semaphore(name))

        wqk = sb("wqk", [P, 2, DC, 2 * D], F32R)
        wv = sb("wv", [P, 2, DC, D], F32R)
        wo = sb("wo", [P, 2, DC, D], F32R)
        wx = sb("wx", [P, 2, 4, DC, D], F32R)
        wxv = sb("wxv", [P, 2, 2, DC, D], F32R)
        wg = sb("wg", [P, 2, 2 * DC, D], F32R)
        wr = sb("wr", [P, DC, E])
        WCOLS = DC * (2 * D + D + D + 4 * D + 2 * D + 2 * D)
        shared = sb("shared", [P, WCOLS])
        feat = shared[:, 0:8 * GT].rearrange("p (k c t) -> p k c t", k=4, c=DC)
        values = shared[:, 8 * GT:8 * GT + G * 2 * D].rearrange("p (g n) -> p g n", g=G)
        bqkv = sb("bqkv", [P, 3 * D])
        bo = sb("bo", [P, D])
        bxv = sb("bxv", [P, 2 * D])
        bg = sb("bg", [P, D])
        nw = sb("nw", [P, D])
        br = sb("br", [P, E])
        bx = sb("bx", [P, 4, DC])
        rope_cos = sb("rope_cos", [P, 2 * H, HD // 2])
        rope_sin = sb("rope_sin", [P, 2 * H, HD // 2])
        ident = sb("ident", [P, P])
        ident_bf = sb("ident_bf", [P, P], BF16)
        mask = sb("mask", [P, HU, T], BF16)
        minus_half = sb("minus_half", [P, 1])
        eps_col = sb("eps_col", [P, 1])
        pool_pad = sb("pool_pad", [1, 1])
        dve_pad = sb("dve_pad", [1, 1])
        xT_raw = sb("xT_raw", [P, DC, GT])
        cT_raw = sb("cT_raw", [P, DC, GT])
        xT = sb("xT", [P, 2, DC, GT], F32R)
        cT = sb("cT", [P, 2, DC, GT], F32R)
        xb = sb("xb", [P, G, D])
        qkb = sb("qkb", [P, 2, 2 * D])
        by_cos = sb("by_cos", [P, 2 * H, 2, HD // 2])
        by_sin = sb("by_sin", [P, 2 * H, 2, HD // 2])
        roped = sb("roped", [P, 2, 2 * D])
        qkT = sb("qkT", [P, 2, 2, 2 * DC, T], F32R)
        kblock = sb("kblock", [P, 2, DC, H // DC, T], F32R)
        v_aug = sb("v_aug", [P, G, H, 2 * HD])
        nmax = sb("nmax", [P, 8, HU])
        probs_a = sb("probs_a", [P, 4, HU, T])
        probs_T = sb("probs_T", [P, 2, HU, T])
        outT = sb("outT", [P, 2, UNITS, T])
        rec = sb("rec", [P, 2, H])
        heads = sb("heads", [P, 2, D])
        headsT = sb("headsT", [P, 2, 2, DC, T], F32R)
        pre1 = sb("pre1", [P, 2, D])
        stats = sb("stats", [P, 2, 6])
        mv1 = sb("mv1", [P, 2, 2])
        rstd1 = sb("rstd1", [P, 2, 1])
        x1 = sb("x1", [P, G, D])
        x1T = sb("x1T", [P, 2, DC, GT], F32R)
        xnmax = sb("xnmax", [P, 2, 2])
        xbias = sb("xbias", [P, 2, 2])
        xsum = sb("xsum", [P, 2, 2])
        xrec = sb("xrec", [P, 2, 2])
        xprobs = sb("xprobs", [P, 2, 2, T])
        xprobs_T = sb("xprobs_T", [P, 2, 2, T])
        mixed = sb("mixed", [P, 2, 2, D])
        mixedT = sb("mixedT", [P, 2, 2, 2 * DC, T], F32R)
        diff = sb("diff", [P, 2, D])
        base = sb("base", [P, 2, D])
        gate_z = sb("gate_z", [P, 2, D])
        pre2 = sb("pre2", [P, 2, D])
        mv2 = sb("mv2", [P, 2, 2])
        rstd2 = sb("rstd2", [P, 2, 1])
        rrms2 = sb("rrms2", [P, 2, 1])
        x2 = sb("x2", [P, 2, D])
        row = sb("row", [P, 2, ROW])
        xnT = sb("xnT", [P, DC, GT])
        lg = sb("lg", [P, 2, E])
        lmax = sb("lmax", [P, 2, 1])
        lexp = sb("lexp", [P, 2, E])
        lsum = sb("lsum", [P, 2, 1])
        lrec = sb("lrec", [P, 2, 1])
        lgT = sb("lgT", [E, GT])

        bank = [ctx.enter_context(nc.psum_tensor(f"bank{k}", [P, 512], F32)) for k in range(8)]

        w_loaded = [sem(f"w_loaded{k}") for k in range(6)]
        first_loaded = sem("first_loaded")
        later_loaded = sem("later_loaded")
        w_high = sem("w_high")
        w_ready = sem("w_ready")
        consts = sem("consts")
        pool_step = sem("pool_step")
        xT_loaded = [sem(f"xT_loaded{j}") for j in range(G)]
        cT_loaded = sem("cT_loaded")
        x_loaded = sem("x_loaded")
        xT_high = sem("xT_high")
        cT_high = sem("cT_high")
        xT_ready = sem("xT_ready")
        cT_ready = sem("cT_ready")
        xb_ready = sem("xb_ready")
        qk_done = sem("qk_done")
        v_done = sem("v_done")
        qkb_ready = sem("qkb_ready")
        v_ready = sem("v_ready")
        rope_products = sem("rope_products")
        rope_ready = sem("rope_ready")
        qkT_done = sem("qkT_done")
        qkT_high = sem("qkT_high")
        qkT_ready = sem("qkT_ready")
        kblock_ready = [sem(f"kblock_ready{c}") for c in range(DC)]
        scores_ready = sem("scores_ready")
        max_ready = sem("max_ready")
        probs_ready = sem("probs_ready")
        probsT_done = sem("probsT_done")
        probsT_ready = sem("probsT_ready")
        av_done = sem("av_done")
        outT_ready = sem("outT_ready")
        out_done = sem("out_done")
        rec_ready = sem("rec_ready")
        heads_ready = sem("heads_ready")
        headsT_done = sem("headsT_done")
        headsT_high = sem("headsT_high")
        headsT_ready = sem("headsT_ready")
        wo_done = sem("wo_done")
        pre1_ready = sem("pre1_ready")
        stats1 = sem("stats1")
        var1_ready = sem("var1_ready")
        pool1 = sem("pool1")
        rstd1_ready = sem("rstd1_ready")
        x1_ready = sem("x1_ready")
        x1T_done = sem("x1T_done")
        x1T_high = sem("x1T_high")
        x1T_ready = sem("x1T_ready")
        feat_done = sem("feat_done")
        feat_act = sem("feat_act")
        feat_dve = sem("feat_dve")
        xv_done = sem("xv_done")
        xv_ready = sem("xv_ready")
        xscores_done = sem("xscores_done")
        xmax_made = sem("xmax_made")
        xmax_ready = sem("xmax_ready")
        xprobs_ready = sem("xprobs_ready")
        xrec_ready = sem("xrec_ready")
        xprobsT_done = sem("xprobsT_done")
        xprobsT_ready = sem("xprobsT_ready")
        xav_done = sem("xav_done")
        mixed_ready = sem("mixed_ready")
        mixedT_done = sem("mixedT_done")
        mixedT_high = sem("mixedT_high")
        mixedT_ready = sem("mixedT_ready")
        base_ready = sem("base_ready")
        gate_done = sem("gate_done")
        gate_z_ready = sem("gate_z_ready")
        gate_t_ready = sem("gate_t_ready")
        dve_step = sem("dve_step")
        var2_ready = sem("var2_ready")
        pool2 = sem("pool2")
        rstd2_ready = sem("rstd2_ready")
        rrms_ready = sem("rrms_ready")
        x2_ready = sem("x2_ready")
        xn_ready = sem("xn_ready")
        xnT_done = sem("xnT_done")
        xnT_ready = sem("xnT_ready")
        lg_done = sem("lg_done")
        lg_step = sem("lg_step")
        lmax_ready = sem("lmax_ready")
        lrec_ready = sem("lrec_ready")
        lexp_ready = sem("lexp_ready")
        row_ready = sem("row_ready")
        lgT_done = sem("lgT_done")
        lgT_ready = sem("lgT_ready")
        x2_stored = [sem(f"x2_stored{j}") for j in range(G)]
        row_stored = [sem(f"row_stored{j}") for j in range(G)]
        lgT_stored = sem("lgT_stored")

        def hold_dve(dve):
            dve.memset(dve_pad[:], 0.0)

        def hold_pool(pool):
            pool.tensor_tensor(pool_pad[:], eps_col[0:1, :], eps_col[0:1, :], ALU.add)

        block = ctx.enter_context(nc.Block())

        W_PARTS = ((wqk, d["wqk"]), (wv, d["wv"]), (wo, d["wo"]), (wx, d["wx"]), (wxv, d["wxv"]), (wg, d["wg"]))
        FIRST_LOADS = ((bqkv, "bqkv"), (rope_cos, "rope_cos"), (rope_sin, "rope_sin"))
        LATER_LOADS = ((bo, "bo"), (bxv, "bxv"), (bg, "bg"), (nw, "nw"), (br, "br"), (bx, "bx"), (wr, "wr"))
        N_FIXED = 7
        FIRST_PARTS = 2

        def weight_pieces():
            at = 0
            for tile, src in W_PARTS:
                cols = tile.shape
                width = 1
                for s in cols[2:]:
                    width *= s
                yield tile, src, at, width
                at += width

        def flat(ap):
            names = "abcd"[:len(ap.shape) - 1]
            if len(names) == 1:
                return ap
            return ap.rearrange(f"p {' '.join(names)} -> p ({' '.join(names)})")

        FIRST_FULL, LAST_FULL = 3, NG - 3

        def exists(g):
            return not isinstance(g, int) or 0 <= g < NG

        def passes(engine, body):
            for i in range(-1, FIRST_FULL):
                body(i)
            with engine.Fori(FIRST_FULL, LAST_FULL + 1) as i:
                body(i)
            for i in range(LAST_FULL + 1, NG + 2):
                body(i)

        def units(i):
            for s in range(G * UNITS):
                ahead = (i, (s + 1) // UNITS, (s + 1) % UNITS) if s + 1 < G * UNITS else (i + 1, 0, 0)
                yield s, (i, s // UNITS, s % UNITS), ahead

        @block.sync
        def _(sp):
            def load_x(sp, g, j):
                if not exists(g):
                    return
                n = G * g + j
                need(sp, xT_ready, n - 1)
                sp.dma_start(xT_raw[:, :, j * T:(j + 1) * T], d["xT"][:, :, bass.ts(n, T)]).then_inc(xT_loaded[j], 16)

            def load_weights(parts):
                for k, (tile, src, at, width) in enumerate(weight_pieces()):
                    if k in parts:
                        sp.dma_start(shared[:, at:at + width], src).then_inc(w_loaded[k], 16)

            load_x(sp, 0, 0)
            load_weights(range(1))
            for tile, name in FIRST_LOADS:
                sp.dma_start(tile[:], d[name]).then_inc(first_loaded, 16)
            load_x(sp, 0, 1)
            load_weights(range(1, len(W_PARTS)))
            for tile, name in LATER_LOADS:
                sp.dma_start(tile[:], d[name]).then_inc(later_loaded, 16)

            def kblocks(g, j):
                if not exists(g):
                    return
                n = G * g + j
                need(sp, qkT_ready, n + 1)
                for c in range(DC):
                    need(sp, scores_ready, UNITS * (n - 1) + UNITS // DC * (c + 1))
                    for h in range(H // DC):
                        rows = slice(HD * h, HD * (h + 1))
                        sp.dma_start(kblock[rows, :, c, h, :].bitcast(F32), qkT[rows, j, :, DC + c, :].bitcast(F32)).then_inc(kblock_ready[c], 16)

            def body(i):
                load_x(sp, i + 2, 0)
                kblocks(i, 1)
                if exists(i):
                    need(sp, cT_ready, i)
                    sp.dma_start(cT_raw[:], d["cT"][:, :, bass.ts(i, GT)]).then_inc(cT_loaded, 16)
                    need(sp, pre1_ready, G * i)
                    sp.dma_start(xb[:], d["x"][:, bass.ts(i, G), :]).then_inc(x_loaded, 16)
                load_x(sp, i + 2, 1)
                kblocks(i + 1, 0)
                if exists(i - 2):
                    for j in range(G):
                        n = G * (i - 2) + j
                        need(sp, x2_ready, n + 1)
                        sp.dma_start(x2_dram[:, bass.ts(n, 1), :], x2[:, j:j + 1, :]).then_inc(x2_stored[j], 16)
                    for j in range(G):
                        n = G * (i - 2) + j
                        need(sp, row_ready, n + 1)
                        sp.dma_start(rows_dram[:, bass.ts(n, 1), :], row[:, j:j + 1, :]).then_inc(row_stored[j], 16)
                    need(sp, lgT_ready, i - 1)
                    sp.dma_start(logits_dram[:, bass.ts(i - 2, GT)], lgT[:]).then_inc(lgT_stored, 16)
            passes(sp, body)
            sp.wait_ge(lgT_stored, 16 * NG)
            for j in range(G):
                sp.wait_ge(x2_stored[j], 16 * NG)
                sp.wait_ge(row_stored[j], 16 * NG)

        @block.gpsimd
        def _(pool):
            pool.memset(minus_half[:], -0.5).then_inc(consts, 1)
            pool.memset(eps_col[:], EPS).then_inc(consts, 1)
            pool.memset(ident[:], 0.0).then_inc(pool_step, 1)
            pool.memset(ident_bf[:], 0.0).then_inc(pool_step, 1)
            pool.memset(mask[:], 0.0).then_inc(pool_step, 1)
            pool.memset(v_aug[:], 0.0).then_inc(pool_step, 1)
            pool.wait_ge(pool_step, 4)
            for t in (ident, ident_bf):
                pool.affine_select(out=t[:], in_=t[:], compare_op=ALU.not_equal, fill=1.0, base=0,
                                   pattern=[[-1, P]], channel_multiplier=1).then_inc(consts, 1)
            pool.affine_select(out=mask[:], in_=mask[:], compare_op=ALU.is_ge, fill=MASKED, base=0,
                               pattern=[[0, HU], [-1, T]], channel_multiplier=1).then_inc(consts, 1)
            pool.memset(v_aug[:, :, :, HD:HD + 1], 1.0).then_inc(consts, 1)
            pool.memset(kblock[:].bitcast(F32), 0.0).then_inc(consts, 1)
            pool.wait_ge(first_loaded, 16 * len(FIRST_LOADS))

            def split_x(g, j):
                if not exists(g):
                    return
                n = G * g + j
                tok = slice(j * T, (j + 1) * T)
                need(pool, xT_loaded[j], 16 * (g + 1))
                need(pool, v_done, n - 1)
                hold_pool(pool)
                pool.tensor_copy(xT[:, 0, :, tok], xT_raw[:, :, tok]).then_inc(xT_high, 1)
                need(pool, xT_high, n + 1)
                pool.tensor_tensor(xT[:, 1, :, tok], xT_raw[:, :, tok], xT[:, 0, :, tok].bitcast(F32), ALU.subtract).then_inc(xT_ready, 1)

            def split_context(g):
                if not exists(g):
                    return
                need(pool, cT_loaded, 16 * (g + 1))
                need(pool, xv_done, G * g)
                hold_pool(pool)
                pool.tensor_copy(cT[:, 0], cT_raw[:]).then_inc(cT_high, 1)
                pool.wait_ge(cT_high, g + 1)
                pool.tensor_tensor(cT[:, 1], cT_raw[:], cT[:, 0].bitcast(F32), ALU.subtract).then_inc(cT_ready, 1)

            def rope_products_of(g, j):
                if not exists(g):
                    return
                n = G * g + j
                v = qkb[:, j].rearrange("p (h two k) -> p h two k", two=2, k=HD // 2)
                both = [P, 2 * H, 2, HD // 2]
                need(pool, rope_ready, n)
                need(pool, qkb_ready, n + 1)
                pool.tensor_tensor(by_cos[:], v, rope_cos[:].unsqueeze(2).to_broadcast(both), ALU.mult).then_inc(rope_products, 1)
                pool.tensor_tensor(by_sin[:], v, rope_sin[:].unsqueeze(2).to_broadcast(both), ALU.mult).then_inc(rope_products, 1)

            def rope_sums(g, j):
                if not exists(g):
                    return
                n = G * g + j
                need(pool, qkT_done, n - 1)
                need(pool, rope_products, 2 * n + 2)
                r = roped[:, j].rearrange("p (h two k) -> p h two k", two=2, k=HD // 2)
                pool.tensor_tensor(r[:, :, 0], by_cos[:, :, 0], by_sin[:, :, 1], ALU.subtract)
                pool.tensor_tensor(r[:, :, 1], by_sin[:, :, 0], by_cos[:, :, 1], ALU.add).then_inc(rope_ready, 1)

            def gate_ends(g, j):
                if not exists(g):
                    return
                n = G * g + j
                need(pool, var2_ready, n - 1)
                need(pool, mixed_ready, n + 1)
                pool.tensor_tensor(diff[:, j], mixed[:, j, 0], mixed[:, j, 1], ALU.subtract)
                pool.tensor_tensor(base[:, j], x1[:, j], mixed[:, j, 1], ALU.add).then_inc(base_ready, 1)

            def norm1_root(g, j):
                if not exists(g):
                    return
                n = G * g + j
                need(pool, x1_ready, n - 1)
                need(pool, var1_ready, n + 1)
                pool.tensor_tensor(rstd1[:, j], mv1[:, j, 1:2], eps_col[:], ALU.add).then_inc(pool1, 1)
                need(pool, pool1, n + 1)
                pool.tensor_tensor(rstd1[:, j], rstd1[:, j], minus_half[:], ALU.pow).then_inc(rstd1_ready, 1)

            def norm2_roots(g, j):
                if not exists(g):
                    return
                n = G * g + j
                var, rstd, rrms = mv2[:, j, 1:2], rstd2[:, j], rrms2[:, j]
                need(pool, xn_ready, n - 1)
                need(pool, var2_ready, n + 1)
                pool.tensor_tensor(rrms, var, eps_col[:], ALU.add).then_inc(pool2, 1)
                need(pool, pool2, 4 * n + 1)
                pool.tensor_tensor(rstd, rrms, minus_half[:], ALU.pow).then_inc(rstd2_ready, 1)
                need(pool, rstd2_ready, n + 1)
                pool.tensor_tensor(rrms, var, rstd, ALU.mult).then_inc(pool2, 1)
                need(pool, pool2, 4 * n + 2)
                pool.tensor_tensor(rrms, rrms, rstd, ALU.mult).then_inc(pool2, 1)
                need(pool, pool2, 4 * n + 3)
                pool.tensor_tensor(rrms, rrms, eps_col[:], ALU.add).then_inc(pool2, 1)
                need(pool, pool2, 4 * n + 4)
                pool.tensor_tensor(rrms, rrms, minus_half[:], ALU.pow).then_inc(rrms_ready, 1)

            def add_bias(g):
                if not exists(g):
                    return
                need(pool, x_loaded, 16 * (g + 1))
                for j in range(G):
                    pool.tensor_tensor(xb[:, j], xb[:, j], bo[:], ALU.add).then_inc(xb_ready, 1)

            def body(i):
                if isinstance(i, int) and i == 0:
                    pool.wait_ge(later_loaded, 16 * len(LATER_LOADS))
                for j in range(G):
                    gate_ends(i - 2, j)
                split_x(i + 1, 1)
                norm1_root(i - 1, 1)
                rope_products_of(i + 1, 0)
                rope_sums(i + 1, 0)
                for j in range(G):
                    norm2_roots(i - 2, j)
                add_bias(i)
                split_x(i + 2, 0)
                rope_products_of(i + 1, 1)
                rope_sums(i + 1, 1)
                norm1_root(i, 0)
                split_context(i)
            split_x(0, 0)
            passes(pool, body)

        @block.tensor
        def _(pe):
            pe.wait_ge(w_ready, FIRST_PARTS)
            pe.wait_ge(consts, N_FIXED)

            def split_product(out, stationary, moving, chunks):
                last = None
                for k, (a, b) in enumerate(PASSES):
                    for c in range(chunks):
                        last = pe.matmul(out, stationary(a, c), moving(b, c), start=(k == 0 and c == 0),
                                         stop=(k == len(PASSES) - 1 and c == chunks - 1))
                return last


            def project_qk(g, j):
                if not exists(g):
                    return
                tok = slice(j * T, (j + 1) * T)
                need(pe, xT_ready, G * g + j + 1)
                need(pe, v_ready, G * g + j)
                split_product(bank[5][:], lambda a, c: xT[:, a, c, tok], lambda b, c: wqk[:, b, c, :], DC).then_inc(qk_done, 1)

            def project_v(g, j):
                if not exists(g):
                    return
                tok = slice(j * T, (j + 1) * T)
                need(pe, qkT_ready, G * g + j + 1)
                split_product(bank[5][:, 0:D], lambda a, c: xT[:, a, c, tok], lambda b, c: wv[:, b, c, :], DC).then_inc(v_done, 1)

            def transpose_qk(g, j):
                if not exists(g):
                    return
                n = G * g + j
                if j == 0:
                    need(pe, x1T_ready, g - 1)
                need(pe, rope_ready, n + 1)
                last = None
                for k in range(2 * DC):
                    last = pe.transpose(bank[5][:, k * P:(k + 1) * P], roped[:, j, k * P:(k + 1) * P], ident[:])
                last.then_inc(qkT_done, 1)

            def scores(g, j, t):
                if not exists(g):
                    return
                n = G * g + j
                u = UNITS * n + t
                c = t // (UNITS // DC)
                h0 = HU * (t % (UNITS // DC))
                need(pe, probs_ready, u - 1)
                if t % (UNITS // DC) == 0:
                    need(pe, kblock_ready[c], 16 * (H // DC) * (n + 1))
                pe.matmul(bank[t % 2][:], ident_bf[:], mask[:].rearrange("p h k -> p (h k)"), start=True, stop=False)
                last = None
                for k, (a, b) in enumerate(PASSES):
                    last = pe.matmul(bank[t % 2][:], qkT[:, j, a, c, :], kblock[:, b, c, h0:h0 + HU, :].rearrange("p h k -> p (h k)"),
                                     start=False, stop=(k == len(PASSES) - 1))
                last.then_inc(scores_ready, 1)

            def transpose_probs(g, j, t):
                if not exists(g):
                    return
                u = UNITS * (G * g + j) + t
                if (j, t) == (1, UNITS - 2):
                    need(pe, xnT_ready, G * (g - 1))
                elif (j, t) == (1, UNITS - 1):
                    need(pe, lg_step, G * (g - 1))
                elif (j, t) == (0, 0):
                    need(pe, lgT_ready, g - 2)
                need(pe, probsT_ready, u)
                need(pe, probs_ready, u + 1)
                last = None
                for h in range(HU):
                    last = pe.transpose(bank[2][:, h * T:(h + 1) * T], probs_a[:, t, h], ident[:])
                last.then_inc(probsT_done, 1)

            def weigh_values(g, j, t):
                if not exists(g):
                    return
                n = G * g + j
                if t == 0:
                    need(pe, v_ready, n + 1)
                    need(pe, pre1_ready, n - 1)
                need(pe, probsT_ready, UNITS * n + t + 1)
                last = None
                for h in range(HU):
                    last = pe.matmul(bank[3 + j][2 * HD * h:2 * HD * (h + 1), t * T:(t + 1) * T], v_aug[:, j, HU * t + h, :],
                                     probs_T[:, t % 2, h], start=True, stop=True)
                last.then_inc(av_done, 1)

            def transpose_out(g, j):
                if not exists(g):
                    return
                need(pe, outT_ready, G * g + j + 1)
                last = None
                for t in range(UNITS):
                    last = pe.transpose(bank[3 + j][:, t * P:(t + 1) * P], outT[:, j, t], ident[:])
                last.then_inc(out_done, 1)

            def transpose_heads(g, j):
                if not exists(g):
                    return
                need(pe, heads_ready, G * g + j + 1)
                last = None
                for c in range(DC):
                    last = pe.transpose(bank[3 + j][:, c * P:(c + 1) * P], heads[:, j, c * P:(c + 1) * P], ident[:])
                last.then_inc(headsT_done, 1)

            def project_out(g, j):
                if not exists(g):
                    return
                need(pe, headsT_ready, G * g + j + 1)
                split_product(bank[3 + j][:, 0:D], lambda a, c: headsT[:, j, a, c, :], lambda b, c: wo[:, b, c, :], DC).then_inc(wo_done, 1)

            def transpose_x1(g):
                if not exists(g):
                    return
                need(pe, x1_ready, G * (g + 1))
                if exists(g + 2):
                    need(pe, qkb_ready, G * (g + 2) + 1)
                elif exists(g + 1):
                    need(pe, v_ready, G * (g + 2))
                last = None
                for j in range(G):
                    for c in range(DC):
                        last = pe.transpose(bank[5][:, (DC * j + c) * P:(DC * j + c + 1) * P], x1[:, j, c * P:(c + 1) * P], ident[:])
                last.then_inc(x1T_done, 1)

            def features(g, k):
                if not exists(g):
                    return
                kind = (KS, QS, QC, KC)[k]
                src = cT if k < 2 else x1T
                if k == 0:
                    need(pe, cT_ready, g + 1)
                    need(pe, gate_z_ready, G * g - 1)
                elif k == 1:
                    need(pe, gate_z_ready, G * g)
                elif k == 2:
                    need(pe, x1T_ready, g + 1)
                    need(pe, feat_act, 2 * g + 1)
                else:
                    need(pe, feat_dve, 2 * g + 1)
                last = None
                for m in range(DC):
                    last = split_product(bank[6 + k % 2][:, m * GT:(m + 1) * GT], lambda a, c: wx[:, a, kind, c, m * P:(m + 1) * P],
                                         lambda b, c: src[:, b, c, :], DC)
                last.then_inc(feat_done, 1)

            def cross_values(g, j):
                if not exists(g):
                    return
                tok = slice(j * T, (j + 1) * T)
                need(pe, (feat_act, feat_dve)[j], 2 * g + 2)
                split_product(bank[6 + j][:, 0:D], lambda a, c: cT[:, a, c, tok], lambda b, c: wxv[:, b, 0, c, :], DC)
                split_product(bank[6 + j][:, D:2 * D], lambda a, c: x1T[:, a, c, tok], lambda b, c: wxv[:, b, 1, c, :], DC).then_inc(xv_done, 1)

            def cross_scores(g, j):
                if not exists(g):
                    return
                tok = slice(j * T, (j + 1) * T)
                if j == 0:
                    need(pe, feat_dve, 2 * g + 2)
                need(pe, xv_ready, G * g + j + 1)
                last = None
                for s, (q, k) in enumerate(((QC, KS), (QS, KC))):
                    for c in range(DC):
                        last = pe.matmul(bank[6 + j][:, s * T:(s + 1) * T], feat[:, q, c, tok], feat[:, k, c, tok],
                                         start=(c == 0), stop=(c == DC - 1))
                last.then_inc(xscores_done, 1)

            def transpose_cross(g, j):
                if not exists(g):
                    return
                need(pe, xprobs_ready, G * g + j + 1)
                last = None
                for s in range(2):
                    last = pe.transpose(bank[6 + j][:, s * T:(s + 1) * T], xprobs[:, j, s], ident[:])
                last.then_inc(xprobsT_done, 1)

            def cross_weigh(g, j):
                if not exists(g):
                    return
                need(pe, xprobsT_ready, G * g + j + 1)
                last = None
                for s in range(2):
                    last = pe.matmul(bank[6 + j][:, s * D:(s + 1) * D], xprobs_T[:, j, s], values[:, j, s * D:(s + 1) * D],
                                     start=True, stop=True)
                last.then_inc(xav_done, 1)

            def transpose_mixed(g, j):
                if not exists(g):
                    return
                need(pe, mixed_ready, G * g + j + 1)
                last = None
                for k in range(2 * DC):
                    last = pe.transpose(bank[6 + j][:, k * P:(k + 1) * P], mixed[:, j, k // DC, (k % DC) * P:(k % DC + 1) * P], ident[:])
                last.then_inc(mixedT_done, 1)

            def gate(g, j):
                if not exists(g):
                    return
                need(pe, mixedT_ready, G * g + j + 1)
                split_product(bank[6 + j][:, 0:D], lambda a, c: mixedT[:, j, a, c, :], lambda b, c: wg[:, b, c, :], 2 * DC).then_inc(gate_done, 1)


            def transpose_xn(g, j):
                if not exists(g):
                    return
                need(pe, lgT_ready, g)
                need(pe, xn_ready, G * g + j + 1)
                last = None
                for c in range(DC):
                    last = pe.transpose(bank[2][:, (j * DC + c) * P:(j * DC + c + 1) * P], row[:, j, c * P:(c + 1) * P], ident[:])
                last.then_inc(xnT_done, 1)

            def router(g, j):
                if not exists(g):
                    return
                tok = slice(j * T, (j + 1) * T)
                need(pe, xnT_ready, G * (g + 1))
                last = None
                for c in range(DC):
                    last = pe.matmul(bank[2][:, j * E:(j + 1) * E], xnT[:, c, tok], wr[:, c, :], start=(c == 0), stop=(c == DC - 1))
                last.then_inc(lg_done, 1)

            def router_T(g):
                if not exists(g):
                    return
                need(pe, lg_step, G * (g + 1))
                last = None
                for j in range(G):
                    last = pe.transpose(bank[2][0:E, j * T:(j + 1) * T], lg[:, j], ident[:])
                last.then_inc(lgT_done, 1)

            def body(i):
                if isinstance(i, int) and i == 0:
                    pe.wait_ge(w_ready, len(W_PARTS))
                    pe.wait_ge(later_loaded, 16 * len(LATER_LOADS))
                for s, unit, ahead in units(i):
                    if s == 1:
                        transpose_heads(i - 1, 1)
                    if s == 5:
                        transpose_heads(i, 0)
                    scores(*ahead)
                    transpose_probs(*unit)
                    if s == 0:
                        transpose_mixed(i - 2, 0)
                        transpose_mixed(i - 2, 1)
                        transpose_out(i - 1, 1)
                        transpose_qk(i, 1)
                    if s == 1:
                        gate(i - 2, 0)
                        project_v(i, 1)
                        gate(i - 2, 1)
                    if s == 2:
                        project_out(i - 1, 1)
                        project_qk(i + 1, 0)
                    if s == 3:
                        features(i - 1, 0)
                    if s == 4:
                        transpose_out(i, 0)
                        features(i - 1, 1)
                        transpose_qk(i + 1, 0)
                    if s == 5:
                        project_v(i + 1, 0)
                        features(i - 1, 3)
                    if s == 6:
                        cross_values(i - 1, 1)
                        project_qk(i + 1, 1)
                    if s == 7:
                        project_out(i, 0)
                        transpose_cross(i - 1, 0)
                        transpose_cross(i - 1, 1)
                    weigh_values(*unit)
                    if s == 3:
                        transpose_x1(i - 1)
                    if s == 4:
                        features(i - 1, 2)
                    if s == 5:
                        transpose_xn(i - 2, 0)
                        transpose_xn(i - 2, 1)
                        cross_values(i - 1, 0)
                    if s == 6:
                        router(i - 2, 0)
                        router(i - 2, 1)
                        cross_scores(i - 1, 0)
                        cross_scores(i - 1, 1)
                    if s == 7:
                        router_T(i - 2)
                        cross_weigh(i - 1, 0)
                        cross_weigh(i - 1, 1)
            passes(pe, body)

        @block.scalar
        def _(act):
            def high_parts(parts):
                for k, (tile, src, at, width) in enumerate(weight_pieces()):
                    if k in parts:
                        act.wait_ge(w_loaded[k], 16)
                        act.activation(flat(tile[:, 0]), shared[:, at:at + width], ACT.Copy).then_inc(w_high, 1)

            def exponentials(g, j, t):
                if not exists(g):
                    return
                u = UNITS * (G * g + j) + t
                need(act, probsT_done, u - 3)
                need(act, max_ready, u + 1)
                last = None
                for h in range(HU):
                    last = act.activation(probs_a[:, t, h], bank[t % 2][:, h * T:(h + 1) * T], ACT.Exp,
                                          bias=nmax[:, UNITS * j + t, h:h + 1])
                last.then_inc(probs_ready, 1)

            def qkT_out(g, j):
                if not exists(g):
                    return
                n = G * g + j
                need(act, scores_ready, UNITS * (n - 1))
                need(act, qkT_done, n + 1)
                act.activation(qkT[:, j, 0].rearrange("p c t -> p (c t)"), bank[5][:], ACT.Copy).then_inc(qkT_high, 1)

            def out_evacuate(g, j):
                if not exists(g):
                    return
                n = G * g + j
                need(act, out_done, n - 1)
                need(act, av_done, UNITS * (n + 1))
                act.activation(outT[:, j].rearrange("p u t -> p (u t)"), bank[3 + j][:], ACT.Copy).then_inc(outT_ready, 1)

            def heads_out(g, j):
                if not exists(g):
                    return
                n = G * g + j
                need(act, wo_done, n - 1)
                need(act, headsT_done, n + 1)
                act.activation(headsT[:, j, 0].rearrange("p c t -> p (c t)"), bank[3 + j][:, 0:D], ACT.Copy).then_inc(headsT_high, 1)

            def x1T_out(g):
                if not exists(g):
                    return
                need(act, xv_done, G * g)
                need(act, x1T_done, g + 1)
                act.activation(x1T[:, 0].rearrange("p c (j t) -> p j c t", j=G), bank[5][:].rearrange("p (j c t) -> p j c t", j=G, c=DC),
                               ACT.Copy).then_inc(x1T_high, 1)

            def features_out(g, k):
                if not exists(g):
                    return
                kind = (KS, QS, QC, KC)[k]
                need(act, xscores_done, G * g)
                need(act, feat_done, 4 * g + k + 1)
                last = None
                for m in range(DC):
                    last = act.activation(feat[:, kind, m, :], bank[6 + k % 2][:, m * GT:(m + 1) * GT], ACT.Identity, bias=bx[:, kind, m:m + 1])
                last.then_inc(feat_act, 1)

            def cross_exponentials(g, j):
                if not exists(g):
                    return
                n = G * g + j
                need(act, xprobsT_done, n - 1)
                need(act, xmax_ready, n + 1)
                last = None
                for s in range(2):
                    last = act.activation(xprobs[:, j, s], bank[6 + j][:, s * T:(s + 1) * T], ACT.Exp, scale=float(D) ** -0.5,
                                          bias=xbias[:, j, s:s + 1], accum_out=xsum[:, j, s:s + 1])
                last.then_inc(xprobs_ready, 1)

            def cross_probs_out(g, j):
                if not exists(g):
                    return
                n = G * g + j
                need(act, xav_done, n - 1)
                need(act, xprobsT_done, n + 1)
                act.activation(xprobs_T[:, j].rearrange("p s t -> p (s t)"), bank[6 + j][:, 0:2 * T], ACT.Copy).then_inc(xprobsT_ready, 1)

            def mixed_out(g, j):
                if not exists(g):
                    return
                n = G * g + j
                need(act, base_ready, n - 1)
                need(act, mixedT_done, n - 1)
                need(act, xrec_ready, n + 1)
                need(act, xav_done, n + 1)
                last = None
                for s in range(2):
                    last = act.activation(mixed[:, j, s], bank[6 + j][:, s * D:(s + 1) * D], ACT.Copy, scale=xrec[:, j, s:s + 1])
                last.then_inc(mixed_ready, 1)

            def mixedT_out(g, j):
                if not exists(g):
                    return
                n = G * g + j
                need(act, gate_done, n - 1)
                need(act, mixedT_done, n + 1)
                act.activation(mixedT[:, j, 0].rearrange("p c t -> p (c t)"), bank[6 + j][:], ACT.Copy).then_inc(mixedT_high, 1)

            def gate_tanh(g, j):
                if not exists(g):
                    return
                n = G * g + j
                need(act, gate_z_ready, n + 1)
                act.activation(gate_z[:, j], gate_z[:, j], ACT.Tanh, scale=0.5).then_inc(gate_t_ready, 1)

            def xnT_out(g, j):
                if not exists(g):
                    return
                need(act, lgT_done, g)
                need(act, xnT_done, G * (g + 1))
                act.activation(xnT[:, :, j * T:(j + 1) * T], bank[2][:, j * D:(j + 1) * D].rearrange("p (c t) -> p c t", c=DC), ACT.Copy).then_inc(xnT_ready, 1)

            def router_exponentials(g, j):
                if not exists(g):
                    return
                n = G * g + j
                need(act, row_ready, n - 1)
                need(act, lmax_ready, n + 1)
                act.activation(lexp[:, j], lg[:, j], ACT.Exp, bias=lmax[:, j], accum_out=lsum[:, j]).then_inc(lexp_ready, 1)

            def logitsT_out(g):
                if not exists(g):
                    return
                need(act, lgT_stored, 16 * g)
                need(act, lgT_done, g + 1)
                act.activation(lgT[:], bank[2][0:E, 0:GT], ACT.Copy).then_inc(lgT_ready, 1)

            def body(i):
                for s, unit, ahead in units(i):
                    if s == 0:
                        mixed_out(i - 2, 0)
                        mixed_out(i - 2, 1)
                        out_evacuate(i - 1, 1)
                    if s == 1:
                        heads_out(i - 1, 1)
                    if s == 4:
                        out_evacuate(i, 0)
                        features_out(i - 1, 0)
                    if s == 5:
                        heads_out(i, 0)
                        features_out(i - 1, 2)
                    if isinstance(i, int) and i == -1 and s == 7:
                        high_parts(range(FIRST_PARTS, len(W_PARTS)))
                        act.wait_ge(later_loaded, 16 * len(LATER_LOADS))
                    exponentials(*ahead)
                    if s == 0:
                        mixedT_out(i - 2, 0)
                        mixedT_out(i - 2, 1)
                        qkT_out(i, 1)
                    if s == 2:
                        gate_tanh(i - 2, 0)
                        gate_tanh(i - 2, 1)
                    if s == 3:
                        x1T_out(i - 1)
                    if s == 4:
                        qkT_out(i + 1, 0)
                    if s == 5:
                        xnT_out(i - 2, 0)
                        xnT_out(i - 2, 1)
                    if s == 6:
                        cross_exponentials(i - 1, 0)
                        cross_exponentials(i - 1, 1)
                    if s == 7:
                        cross_probs_out(i - 1, 0)
                        cross_probs_out(i - 1, 1)
                        logitsT_out(i - 2)
                        router_exponentials(i - 2, 0)
                        router_exponentials(i - 2, 1)
            high_parts(range(FIRST_PARTS))
            passes(act, body)

        @block.vector
        def _(dve):
            def low_parts(parts):
                for k, (tile, src, at, width) in enumerate(weight_pieces()):
                    if k in parts:
                        dve.wait_ge(w_high, k + 1)
                        dve.tensor_tensor(flat(tile[:, 1]), shared[:, at:at + width], flat(tile[:, 0]).bitcast(F32), ALU.subtract).then_inc(w_ready, 1)

            def qk_out(g, j):
                if not exists(g):
                    return
                n = G * g + j
                need(dve, rope_ready, n - 1)
                need(dve, qk_done, n + 1)
                dve.tensor_tensor(qkb[:, j], bank[5][:], bqkv[:, 0:2 * D], ALU.add).then_inc(qkb_ready, 1)

            def v_out(g, j):
                if not exists(g):
                    return
                n = G * g + j
                need(dve, av_done, UNITS * (n - 1))
                need(dve, v_done, n + 1)
                dve.tensor_tensor(v_aug[:, j, :, 0:HD], bank[5][:, 0:D].rearrange("p (h k) -> p h k", h=H),
                                  bqkv[:, 2 * D:3 * D].rearrange("p (h k) -> p h k", h=H), ALU.add).then_inc(v_ready, 1)

            def qkT_low(g, j):
                if not exists(g):
                    return
                need(dve, qkT_high, G * g + j + 1)
                dve.tensor_tensor(qkT[:, j, 1].rearrange("p c t -> p (c t)"), bank[5][:],
                                  qkT[:, j, 0].rearrange("p c t -> p (c t)").bitcast(F32), ALU.subtract).then_inc(qkT_ready, 1)

            def maxima(g, j, t):
                if not exists(g):
                    return
                u = UNITS * (G * g + j) + t
                need(dve, probs_ready, u - 7)
                need(dve, scores_ready, u + 1)
                dve.tensor_reduce(out=nmax[:, UNITS * j + t], in_=bank[t % 2][:].rearrange("p (h k) -> p h k", h=HU),
                                  axis=AX_X, op=ALU.max, negate=True).then_inc(max_ready, 1)

            def probs_out(g, j, t):
                if not exists(g):
                    return
                u = UNITS * (G * g + j) + t
                need(dve, av_done, u - 1)
                need(dve, probsT_done, u + 1)
                dve.tensor_copy(probs_T[:, t % 2].rearrange("p h t -> p (h t)"), bank[2][:]).then_inc(probsT_ready, 1)

            def normalise_heads(g, j):
                if not exists(g):
                    return
                n = G * g + j
                need(dve, headsT_done, n - 1)
                need(dve, out_done, n + 1)
                o = bank[3 + j][:].rearrange("p (h k) -> p h k", h=H)
                dve.reciprocal(rec[:, j].unsqueeze(2), o[:, :, HD:HD + 1]).then_inc(rec_ready, 1)
                need(dve, rec_ready, n + 1)
                dve.tensor_tensor(heads[:, j].rearrange("p (h k) -> p h k", h=H), o[:, :, 0:HD],
                                  rec[:, j].unsqueeze(2).to_broadcast([P, H, HD]), ALU.mult).then_inc(heads_ready, 1)

            def heads_low(g, j):
                if not exists(g):
                    return
                need(dve, headsT_high, G * g + j + 1)
                dve.tensor_tensor(headsT[:, j, 1].rearrange("p c t -> p (c t)"), bank[3 + j][:, 0:D],
                                  headsT[:, j, 0].rearrange("p c t -> p (c t)").bitcast(F32), ALU.subtract).then_inc(headsT_ready, 1)

            def norm1_stats(g, j):
                if not exists(g):
                    return
                n = G * g + j
                need(dve, x1_ready, n - 1)
                need(dve, xb_ready, n + 1)
                need(dve, wo_done, n + 1)
                dve.tensor_tensor(pre1[:, j], bank[3 + j][:, 0:D], xb[:, j], ALU.add).then_inc(pre1_ready, 1)
                need(dve, pre1_ready, n + 1)
                dve.bn_stats(stats[:, 0], pre1[:, j]).then_inc(stats1, 1)
                need(dve, rstd1_ready, n - 1)
                need(dve, stats1, n + 1)
                hold_dve(dve)
                dve.bn_aggr(mv1[:, j], stats[:, 0]).then_inc(var1_ready, 1)

            def norm1(g, j):
                if not exists(g):
                    return
                n = G * g + j
                need(dve, base_ready, n - 1)
                need(dve, x1T_done, g)
                need(dve, rstd1_ready, n + 1)
                dve.tensor_scalar(x1[:, j], pre1[:, j], mv1[:, j, 0:1], rstd1[:, j], ALU.subtract, ALU.mult).then_inc(x1_ready, 1)

            def x1T_low(g):
                if not exists(g):
                    return
                need(dve, x1T_high, g + 1)
                for j in range(G):
                    last = dve.tensor_tensor(x1T[:, 1, :, j * T:(j + 1) * T], bank[5][:, j * D:(j + 1) * D].rearrange("p (c t) -> p c t", c=DC),
                                             x1T[:, 0, :, j * T:(j + 1) * T].bitcast(F32), ALU.subtract)
                last.then_inc(x1T_ready, 1)

            def features_out(g, k):
                if not exists(g):
                    return
                kind = (KS, QS, QC, KC)[k]
                need(dve, xscores_done, G * g)
                need(dve, feat_done, 4 * g + k + 1)
                last = None
                for m in range(DC):
                    last = dve.tensor_scalar(feat[:, kind, m, :], bank[6 + k % 2][:, m * GT:(m + 1) * GT], bx[:, kind, m:m + 1], None, ALU.add)
                last.then_inc(feat_dve, 1)

            def values_out(g, j):
                if not exists(g):
                    return
                n = G * g + j
                need(dve, xav_done, n - 1)
                need(dve, xv_done, n + 1)
                dve.tensor_tensor(values[:, j], bank[6 + j][:], bxv[:], ALU.add).then_inc(xv_ready, 1)

            def cross_maxima(g, j):
                if not exists(g):
                    return
                n = G * g + j
                need(dve, xscores_done, n + 1)
                dve.tensor_reduce(out=xnmax[:, j], in_=bank[6 + j][:, 0:2 * T].rearrange("p (s k) -> p s k", s=2),
                                  axis=AX_X, op=ALU.max, negate=True).then_inc(xmax_made, 1)
                need(dve, xprobs_ready, n - 1)
                need(dve, xmax_made, n + 1)
                dve.tensor_scalar(xbias[:, j], xnmax[:, j], float(D) ** -0.5, None, ALU.mult).then_inc(xmax_ready, 1)

            def cross_reciprocal(g, j):
                if not exists(g):
                    return
                n = G * g + j
                need(dve, mixed_ready, n - 1)
                need(dve, xprobs_ready, n + 1)
                dve.reciprocal(xrec[:, j], xsum[:, j]).then_inc(xrec_ready, 1)

            def mixedT_low(g, j):
                if not exists(g):
                    return
                need(dve, mixedT_high, G * g + j + 1)
                dve.tensor_tensor(mixedT[:, j, 1].rearrange("p c t -> p (c t)"), bank[6 + j][:],
                                  mixedT[:, j, 0].rearrange("p c t -> p (c t)").bitcast(F32), ALU.subtract).then_inc(mixedT_ready, 1)

            def gate_out(g, j):
                if not exists(g):
                    return
                n = G * g + j
                need(dve, gate_done, n + 1)
                dve.tensor_tensor(gate_z[:, j], bank[6 + j][:, 0:D], bg[:], ALU.add).then_inc(gate_z_ready, 1)

            def gate_and_stats(g, j):
                if not exists(g):
                    return
                n = G * g + j
                need(dve, base_ready, n + 1)
                need(dve, gate_t_ready, n + 1)
                dve.scalar_tensor_tensor(diff[:, j], gate_z[:, j], 1.0, diff[:, j], ALU.add, ALU.mult).then_inc(dve_step, 1)
                need(dve, x2_ready, n - 1)
                need(dve, dve_step, 3 * n + 1)
                dve.scalar_tensor_tensor(pre2[:, j], diff[:, j], 0.5, base[:, j], ALU.mult, ALU.add).then_inc(dve_step, 1)
                need(dve, dve_step, 3 * n + 2)
                dve.bn_stats(stats[:, 1], pre2[:, j]).then_inc(dve_step, 1)
                need(dve, rrms_ready, n - 1)
                need(dve, dve_step, 3 * n + 3)
                hold_dve(dve)
                dve.bn_aggr(mv2[:, j], stats[:, 1]).then_inc(var2_ready, 1)

            def norm2(g, j):
                if not exists(g):
                    return
                n = G * g + j
                need(dve, x2_stored[j], 16 * g)
                need(dve, rstd2_ready, n + 1)
                dve.tensor_scalar(x2[:, j], pre2[:, j], mv2[:, j, 0:1], rstd2[:, j], ALU.subtract, ALU.mult).then_inc(x2_ready, 1)

            def rms_norm(g, j):
                if not exists(g):
                    return
                n = G * g + j
                need(dve, row_stored[j], 16 * g)
                need(dve, x2_ready, n + 1)
                need(dve, rrms_ready, n + 1)
                dve.scalar_tensor_tensor(row[:, j, 0:D], x2[:, j], rrms2[:, j], nw[:], ALU.mult, ALU.mult).then_inc(xn_ready, 1)

            def router_maximum(g, j):
                if not exists(g):
                    return
                n = G * g + j
                need(dve, lexp_ready, n - 1)
                need(dve, lgT_done, g)
                need(dve, lg_done, G * (g + 1))
                dve.tensor_tensor(lg[:, j], bank[2][:, j * E:(j + 1) * E], br[:], ALU.add).then_inc(lg_step, 1)
                need(dve, lg_step, n + 1)
                dve.tensor_reduce(out=lmax[:, j], in_=lg[:, j], axis=AX_X, op=ALU.max, negate=True).then_inc(lmax_ready, 1)

            def router_probs(g, j):
                if not exists(g):
                    return
                n = G * g + j
                need(dve, lexp_ready, n + 1)
                dve.reciprocal(lrec[:, j], lsum[:, j]).then_inc(lrec_ready, 1)
                need(dve, lrec_ready, n + 1)
                dve.tensor_scalar(row[:, j, D:ROW], lexp[:, j], lrec[:, j], None, ALU.mult)
                dve.tensor_scalar(probs[:, bass.ts(n, 1), :].rearrange("p o e -> p (o e)"), lexp[:, j], lrec[:, j], None, ALU.mult).then_inc(row_ready, 1)

            def body(i):
                for s, unit, ahead in units(i):
                    if s == 1:
                        heads_low(i - 1, 1)
                    if s == 5:
                        heads_low(i, 0)
                    if s == 6:
                        values_out(i - 1, 0)
                    if isinstance(i, int) and i == -1 and s == 7:
                        low_parts(range(FIRST_PARTS, len(W_PARTS)))
                        dve.wait_ge(later_loaded, 16 * len(LATER_LOADS))
                    maxima(*ahead)
                    probs_out(*unit)
                    if s == 0:
                        normalise_heads(i - 1, 1)
                        mixedT_low(i - 2, 0)
                        mixedT_low(i - 2, 1)
                        qkT_low(i, 1)
                    if s == 1:
                        norm1(i - 1, 0)
                        gate_out(i - 2, 0)
                        v_out(i, 1)
                        gate_out(i - 2, 1)
                    if s == 2:
                        norm1_stats(i - 1, 1)
                        qk_out(i + 1, 0)
                    if s == 3:
                        norm1(i - 1, 1)
                        gate_and_stats(i - 2, 0)
                        gate_and_stats(i - 2, 1)
                        x1T_low(i - 1)
                    if s == 4:
                        normalise_heads(i, 0)
                        features_out(i - 1, 1)
                        qkT_low(i + 1, 0)
                        norm2(i - 2, 0)
                        norm2(i - 2, 1)
                        rms_norm(i - 2, 0)
                        rms_norm(i - 2, 1)
                    if s == 5:
                        v_out(i + 1, 0)
                        features_out(i - 1, 3)
                    if s == 6:
                        values_out(i - 1, 1)
                        qk_out(i + 1, 1)
                        router_maximum(i - 2, 0)
                        router_maximum(i - 2, 1)
                        cross_maxima(i - 1, 0)
                        cross_maxima(i - 1, 1)
                    if s == 7:
                        cross_reciprocal(i - 1, 0)
                        cross_reciprocal(i - 1, 1)
                        norm1_stats(i, 0)
                        router_probs(i - 2, 0)
                        router_probs(i - 2, 1)
            low_parts(range(FIRST_PARTS))
            dve.wait_ge(first_loaded, 16 * len(FIRST_LOADS))
            passes(dve, body)


def choose_tokens(nc, d, logits_dram, slots_dram, scale_dram, probs, slot_rows):
    with ExitStack() as ctx:
        def sb(name, shape, dt=F32):
            return ctx.enter_context(nc.sbuf_tensor(name, shape, dt))

        def sem(name):
            return ctx.enter_context(nc.semaphore(name))

        keys = sb("keys", [P, CHUNK])
        ones = sb("ones_bf", [P, CHUNK], BF16)
        hits = sb("hits", [P, CHUNK])
        same = sb("same", [P, CHUNK])
        place = sb("place", [P, CHUNK])
        same_expert = sb("same_expert", [P, P])
        earlier_chunk = sb("earlier_chunk", [P, P])
        ident = sb("ident_b", [P, P])
        token_no = sb("token_no", [P, 1])
        batch_no = sb("batch_no", [P, B])
        combine = sb("combine", [2 * SLOT_HI, SLOT_HI])
        zeros = sb("zeros_bf", [P, E * SLOT_LO], BF16)
        thr = sb("thr", [P, 1], I32)
        high_pos = sb("high_pos", [P, 1], I32)
        high_neg = sb("high_neg", [P, 1], I32)
        thr_low = sb("thr_low", [P, 1], I32)
        cand = sb("cand", [P, 3], I32)
        cand_base = sb("cand_base", [P, 3], I32)
        patterns = sb("patterns", [P, 3], I32)
        weights = sb("weights", [P, 3])
        weighed = sb("weighed", [P, 3])
        digit = sb("digit", [P, 1])
        digit_i = sb("digit_i", [P, 1], I32)
        sign = sb("sign", [P, 1])
        signed_cap = sb("signed_cap", [P, 1])
        signed_expert = sb("signed_expert", [P, P])
        neg = sb("neg", [P, 1])
        neg_i = sb("neg_i", [P, 1], I32)
        count = sb("count", [P, 3])
        counts = sb("counts", [P, 2])
        left = sb("left", [P, 1])
        before = sb("before", [P, 2])
        slot = sb("slot", [P, CHUNKS, CHUNK // P, E], I32)
        digit_hi = sb("digit_hi", [P, B * E], I32)
        digit_lo = sb("digit_lo", [P, B * E], I32)
        slot_hi = sb("slot_hi", [P, B * E], BF16)
        slot_lo = sb("slot_lo", [P, B * E], BF16)
        gated = sb("gated", [P, B, E])
        gate_sum = sb("gate_sum", [P, B])
        empty = sb("empty", [P, B])
        gate_scale = sb("gate_scale", [P, B])
        KB = CHUNK // P
        DIGITS = 15
        QUARTERS = 4
        QB = B // QUARTERS
        ACT_B = QB - 4
        hot_hi = sb("hot_hi", [P, 2, SLOT_HI, QB * E], BF16)
        hot_ids = sb("hot_ids", [P, 2, 2, SLOT_HI, QB * E], BF16)
        hot_lo = sb("hot_lo", [P, 2, SLOT_LO, QB * E], BF16)
        ids_two = sb("ids_two", [2 * SLOT_HI, E * SLOT_LO])
        ids = sb("ids", [SLOT_HI, E * SLOT_LO], I32)
        total = ctx.enter_context(nc.psum_tensor("total", [P, 512], F32))
        placeT = ctx.enter_context(nc.psum_tensor("placeT", [P, KB, P], F32))
        table = ctx.enter_context(nc.psum_tensor("table", [P, 512], F32))
        table2 = ctx.enter_context(nc.psum_tensor("table2", [P, 512], F32))

        keys_loaded = sem("keys_loaded")
        loaded = sem("b_loaded")
        ready = sem("b_consts")
        counted = sem("counted")
        totalled = sem("totalled")
        step = sem("b_step")
        placed = sem("placed")
        transposed = sem("transposed")
        hi_ready = sem("hi_ready")
        lo_ready = sem("lo_ready")
        act_numbers = sem("act_numbers")
        pool_numbers = sem("pool_numbers")
        scale_ready = sem("scale_ready")
        table_used = sem("table_used")
        table_done = sem("table_done")
        ids_two_ready = sem("ids_two_ready")
        ids_done = sem("ids_done")
        ids_ready = sem("ids_ready")
        lists_stored = sem("lists_stored")
        slots_loaded = sem("slots_loaded")

        consts = ((earlier_chunk, "earlier_chunk"), (ident, "ident"), 
                  (token_no, "token_no"), (batch_no, "batch_no"), (combine, "combine"))
        block = ctx.enter_context(nc.Block())

        @block.sync
        def _(sp):
            sp.dma_start(keys[:], logits_dram.rearrange("e (c k) -> (e c) k", c=CHUNKS)).then_inc(keys_loaded, 16)
            sp.dma_start(same_expert[:], d["same_expert"]).then_inc(keys_loaded, 16)
            for tile, name in consts:
                sp.dma_start(tile[:], d[name]).then_inc(loaded, 16)
            sp.wait_ge(scale_ready, 1)
            sp.dma_start(scale_dram, gate_scale[:]).then_inc(lists_stored, 16)
            sp.wait_ge(ids_ready, 1)
            sp.dma_start(slots_dram.rearrange("e (h l) -> h e l", h=SLOT_HI), ids[:].rearrange("h (e l) -> h e l", e=E)).then_inc(lists_stored, 16)
            sp.wait_ge(lists_stored, 32)
            sp.dma_start(slot_rows[:], slots_dram.rearrange("e (p q) -> p e q", p=P)).then_inc(slots_loaded, 16)
            sp.wait_ge(slots_loaded, 16)

        @block.tensor
        def _(pe):
            pe.wait_ge(keys_loaded, 32)
            pe.wait_ge(counted, 1)
            pe.matmul(total[:, 0:3], same_expert[:], count[:], start=True, stop=True).then_inc(totalled, 1)
            with pe.Fori(0, DIGITS) as k:
                pe.wait_ge(counted, k + 2)
                pe.matmul(total[:, 0:3], signed_expert[:], count[:], start=True, stop=True).then_inc(totalled, 1)
            pe.wait_ge(loaded, 16 * len(consts))
            pe.wait_ge(counted, DIGITS + 2)
            pe.matmul(total[:, 0:1], same_expert[:], counts[:, 0:1], start=True, stop=True)
            pe.matmul(total[:, 1:2], earlier_chunk[:], counts[:, 1:2], start=True, stop=True).then_inc(totalled, 1)
            pe.wait_ge(counted, DIGITS + 3)
            pe.matmul(total[:, 0:1], earlier_chunk[:], count[:, 0:1], start=True, stop=True).then_inc(totalled, 1)
            pe.wait_ge(placed, 1)
            last = None
            for k in range(KB):
                last = pe.transpose(placeT[:, k], place[:, k * P:(k + 1) * P], ident[:])
            last.then_inc(transposed, 1)
            pe.wait_ge(ready, 2)
            pe.matmul(table[0:2 * SLOT_HI, :], zeros[:, 0:2 * SLOT_HI], zeros[:], start=True, stop=False)

            with pe.Fori(0, QUARTERS // 2) as i:
                for b in range(2):
                    pe.wait_ge(lo_ready, 2 * i + b + 1)
                    pe.wait_ge(act_numbers, 2 * i + b + 1)
                    pe.wait_ge(pool_numbers, 2 * i + b + 1)
                    for column in range(QB * E):
                        e = column % E
                        last = pe.matmul(table[0:2 * SLOT_HI, e * SLOT_LO:(e + 1) * SLOT_LO],
                                         hot_ids[:, b, :, :, column:column + 1].rearrange("p two h o -> p (two h o)"),
                                         hot_lo[:, b, :, column:column + 1].rearrange("p l o -> p (l o)"),
                                         start=False, stop=False, skip_group_check=True)
                    last.then_inc(table_used, 1)
            pe.matmul(table[0:2 * SLOT_HI, :], zeros[:, 0:2 * SLOT_HI], zeros[:], start=False, stop=True).then_inc(table_done, 1)
            pe.wait_ge(ids_two_ready, 1)
            pe.matmul(table2[0:SLOT_HI, :], combine[:], ids_two[:], start=True, stop=True).then_inc(ids_done, 1)

        @block.vector
        def _(dve):
            dve.memset(ones[:], 1.0).then_inc(ready, 1)
            dve.memset(zeros[:], 0.0).then_inc(ready, 1)
            for j, pattern in enumerate((0, 1 << 30, -1 << 30)):
                dve.memset(cand[:, j:j + 1], pattern).then_inc(step, 1)
            dve.memset(weights[:], float(1 << 28)).then_inc(step, 1)
            for j in range(3):
                dve.memset(patterns[:, j:j + 1], (j + 1) << 28).then_inc(step, 1)
            dve.wait_ge(keys_loaded, 32)
            dve.wait_ge(step, 7)
            cand_f = cand[:].bitcast(F32)
            three = [P, 3]

            def count_at_least(j, where):
                return dve.tensor_scalar(where[:], keys[:], cand_f[:, j:j + 1], None, ALU.is_ge, ALU.add, accum_out=count[:, j:j + 1])

            def count_all():
                count_at_least(0, hits)
                count_at_least(1, same)
                count_at_least(2, place).then_inc(counted, 1)

            count_all()
            dve.wait_ge(totalled, 1)
            dve.tensor_scalar(neg[:], total[:, 0:1], float(CAP), None, ALU.is_lt).then_inc(step, 1)
            dve.tensor_scalar(neg_i[:], total[:, 0:1], float(CAP), None, ALU.is_lt).then_inc(step, 1)
            dve.tensor_scalar(high_pos[:], total[:, 1:2], float(CAP), None, ALU.is_ge).then_inc(step, 1)
            dve.tensor_scalar(high_neg[:], total[:, 2:3], float(CAP), None, ALU.is_lt).then_inc(step, 1)
            dve.wait_ge(step, 11)
            dve.tensor_scalar(sign[:], neg[:], -2.0, 1.0, ALU.mult, ALU.add).then_inc(step, 1)
            dve.tensor_scalar(signed_cap[:], neg[:], float(1 - 2 * CAP), float(CAP), ALU.mult, ALU.add).then_inc(step, 1)
            dve.tensor_scalar(thr[:], neg_i[:], 31, None, ALU.logical_shift_left).then_inc(step, 1)
            dve.tensor_tensor(high_pos[:], high_pos[:], high_neg[:], ALU.bitwise_or).then_inc(step, 1)
            dve.wait_ge(step, 15)
            dve.tensor_scalar(signed_expert[:], same_expert[:], sign[:], None, ALU.mult).then_inc(step, 1)
            dve.tensor_scalar(high_pos[:], high_pos[:], 30, None, ALU.logical_shift_left).then_inc(step, 1)
            dve.wait_ge(step, 17)
            dve.tensor_tensor(thr[:], thr[:], high_pos[:], ALU.bitwise_or).then_inc(step, 1)
            dve.wait_ge(step, 18)
            dve.tensor_tensor(cand[:], patterns[:], thr[:].to_broadcast(three), ALU.bitwise_or).then_inc(step, 1)
            with dve.Fori(0, DIGITS) as k:
                dve.wait_ge(step, 7 * k + 19)
                count_all()
                dve.tensor_scalar(patterns[:], patterns[:], 2, None, ALU.logical_shift_right).then_inc(step, 1)
                dve.wait_ge(step, 7 * k + 20)
                dve.tensor_tensor(cand_base[:], patterns[:], thr[:].to_broadcast(three), ALU.bitwise_or).then_inc(step, 1)
                dve.wait_ge(totalled, k + 2)
                dve.scalar_tensor_tensor(weighed[:], total[:, 0:3], signed_cap[:], weights[:], ALU.is_ge, ALU.mult,
                                         accum_out=digit[:]).then_inc(step, 1)
                dve.wait_ge(step, 7 * k + 22)
                dve.tensor_copy(digit_i[:], digit[:]).then_inc(step, 1)
                dve.tensor_scalar(weights[:], weights[:], 0.25, None, ALU.mult).then_inc(step, 1)
                dve.wait_ge(step, 7 * k + 23)
                dve.tensor_tensor(thr[:], thr[:], digit_i[:], ALU.bitwise_or).then_inc(step, 1)
                dve.tensor_tensor(cand[:], cand_base[:], digit_i[:].to_broadcast(three), ALU.bitwise_or).then_inc(step, 1)
            dve.wait_ge(loaded, 16 * len(consts))
            s = 7 * DIGITS + 19
            dve.wait_ge(step, s)
            dve.tensor_scalar(thr_low[:], thr[:], 0xffff, None, ALU.bitwise_and).then_inc(step, 1)
            dve.tensor_scalar(thr[:], thr[:], 16, None, ALU.logical_shift_right).then_inc(step, 1)
            dve.wait_ge(step, s + 1)
            dve.tensor_tensor(thr_low[:], thr_low[:], neg_i[:], ALU.add).then_inc(step, 1)
            dve.wait_ge(step, s + 3)
            dve.tensor_scalar(digit_i[:], thr_low[:], 16, None, ALU.logical_shift_right).then_inc(step, 1)
            dve.tensor_scalar(thr_low[:], thr_low[:], 0xffff, None, ALU.bitwise_and).then_inc(step, 1)
            dve.wait_ge(step, s + 4)
            dve.tensor_tensor(thr[:], thr[:], digit_i[:], ALU.add).then_inc(step, 1)
            dve.wait_ge(step, s + 6)
            dve.tensor_scalar(thr[:], thr[:], 16, None, ALU.logical_shift_left).then_inc(step, 1)
            dve.wait_ge(step, s + 7)
            dve.tensor_tensor(thr[:], thr[:], thr_low[:], ALU.bitwise_or).then_inc(step, 1)
            s += 7
            dve.wait_ge(step, s + 1)
            thr_f = thr[:].bitcast(F32)
            dve.tensor_scalar(hits[:], keys[:], thr_f, None, ALU.is_gt, ALU.add, accum_out=counts[:, 0:1])
            dve.tensor_scalar(same[:], keys[:], thr_f, None, ALU.is_equal, ALU.add, accum_out=counts[:, 1:2]).then_inc(counted, 1)
            dve.wait_ge(totalled, DIGITS + 2)
            dve.tensor_scalar(left[:], total[:, 0:1], -1.0, float(CAP), ALU.mult, ALU.add).then_inc(step, 1)
            dve.tensor_copy(before[:, 0:1], total[:, 1:2]).then_inc(step, 1)
            dve.wait_ge(step, s + 3)
            dve.tensor_tensor_scan(place[:], ones[:], same[:], before[:, 0:1], ALU.mult, ALU.add).then_inc(step, 1)
            dve.wait_ge(step, s + 4)
            dve.scalar_tensor_tensor(same[:], place[:], left[:], same[:], ALU.is_le, ALU.mult).then_inc(step, 1)
            dve.wait_ge(step, s + 5)
            dve.scalar_tensor_tensor(hits[:], same[:], 1.0, hits[:], ALU.mult, ALU.add, accum_out=count[:, 0:1]).then_inc(counted, 1)
            dve.wait_ge(totalled, DIGITS + 3)
            dve.tensor_copy(before[:, 1:2], total[:, 0:1]).then_inc(step, 1)
            dve.wait_ge(step, s + 6)
            dve.tensor_tensor_scan(place[:], ones[:], hits[:], before[:, 1:2], ALU.mult, ALU.add).then_inc(step, 1)
            dve.wait_ge(step, s + 7)
            dve.tensor_tensor(place[:], place[:], hits[:], ALU.mult).then_inc(placed, 1)
            dve.wait_ge(transposed, 1)
            for k in range(KB):
                last = dve.tensor_scalar(slot[:, :, k, :], placeT[:, k].rearrange("p (e c) -> p c e", e=E), -1.0, None, ALU.add)
            last.then_inc(step, 1)
            dve.wait_ge(step, s + 8)
            flat = slot[:].rearrange("p c k e -> p (c k e)")
            dve.tensor_scalar(digit_hi[:], flat, SLOT_LO.bit_length() - 1, None, ALU.arith_shift_right).then_inc(step, 1)
            dve.tensor_scalar(digit_lo[:], flat, SLOT_LO - 1, None, ALU.bitwise_and).then_inc(step, 1)
            dve.wait_ge(step, s + 10)
            dve.tensor_copy(slot_hi[:], digit_hi[:]).then_inc(step, 1)
            dve.tensor_copy(slot_lo[:], digit_lo[:]).then_inc(step, 1)
            dve.wait_ge(step, s + 12)

            def digits(quarter):
                b = quarter % 2
                columns = slice(quarter * QB * E, (quarter + 1) * QB * E)
                need(dve, act_numbers, quarter - 1)
                need(dve, pool_numbers, quarter - 1)
                last = None
                for n in range(SLOT_HI):
                    last = dve.tensor_scalar(hot_hi[:, b, n], slot_hi[:, columns], float(n), None, ALU.is_equal)
                last.then_inc(hi_ready, 1)
                need(dve, table_used, quarter - 1)
                for n in range(SLOT_HI):
                    last = dve.tensor_scalar(hot_ids[:, b, 0, n], slot_hi[:, columns], float(n), token_no[:], ALU.is_equal, ALU.mult)
                for n in range(SLOT_LO):
                    last = dve.tensor_scalar(hot_lo[:, b, n], slot_lo[:, columns], float(n), None, ALU.is_equal)
                last.then_inc(lo_ready, 1)
            for quarter in range(QUARTERS):
                digits(quarter)
            dve.scalar_tensor_tensor(gated[:].rearrange("p b e -> p (b e)"), slot[:].rearrange("p c k e -> p (c k e)"), 0.0,
                                     probs[:].rearrange("p b e -> p (b e)"), ALU.is_ge, ALU.mult).then_inc(step, 1)
            dve.wait_ge(step, s + 13)
            dve.tensor_reduce(out=gate_sum[:], in_=gated[:], axis=AX_X, op=ALU.add).then_inc(step, 1)
            dve.wait_ge(step, s + 14)
            dve.tensor_scalar(empty[:], gate_sum[:], 0.0, None, ALU.is_le).then_inc(step, 1)
            dve.wait_ge(step, s + 15)
            dve.tensor_tensor(gate_sum[:], gate_sum[:], empty[:], ALU.add).then_inc(step, 1)
            dve.wait_ge(step, s + 16)
            dve.reciprocal(gate_scale[:], gate_sum[:]).then_inc(scale_ready, 1)
            dve.wait_ge(table_done, 1)
            dve.tensor_copy(ids_two[:], table[0:2 * SLOT_HI, :]).then_inc(ids_two_ready, 1)
            dve.wait_ge(ids_done, 1)
            dve.tensor_copy(ids[:], table2[0:SLOT_HI, :]).then_inc(ids_ready, 1)

        @block.scalar
        def _(act):
            act.wait_ge(loaded, 16 * len(consts))
            for quarter in range(QUARTERS):
                b = quarter % 2
                need(act, table_used, quarter - 1)
                act.wait_ge(hi_ready, quarter + 1)
                last = None
                for n in range(ACT_B):
                    columns = slice(n * E, (n + 1) * E)
                    last = act.activation(hot_ids[:, b, 1, :, columns], hot_hi[:, b, :, columns], ACT.Copy,
                                          scale=batch_no[:, quarter * QB + n:quarter * QB + n + 1])
                last.then_inc(act_numbers, 1)

        @block.gpsimd
        def _(pool):
            pool.wait_ge(loaded, 16 * len(consts))
            for quarter in range(QUARTERS):
                b = quarter % 2
                need(pool, table_used, quarter - 1)
                pool.wait_ge(hi_ready, quarter + 1)
                columns = slice(ACT_B * E, QB * E)
                first = quarter * QB + ACT_B
                pool.tensor_tensor(hot_ids[:, b, 1, :, columns].rearrange("p h (k e) -> p h k e", e=E),
                                   hot_hi[:, b, :, columns].rearrange("p h (k e) -> p h k e", e=E),
                                   batch_no[:, first:first + QB - ACT_B].unsqueeze(1).unsqueeze(3).to_broadcast([P, SLOT_HI, QB - ACT_B, E]),
                                   ALU.mult).then_inc(pool_numbers, 1)


def run_experts(nc, d, rows_dram, scale_dram, sum_dram, slot_rows):
    with ExitStack() as ctx:
        def sb(name, shape, dt=F32):
            return ctx.enter_context(nc.sbuf_tensor(name, shape, dt))

        def sem(name):
            return ctx.enter_context(nc.semaphore(name))

        ident = sb("ident_c", [P, P])
        w1_raw = sb("w1_raw", [P, DC * F])
        w2_raw = sb("w2_raw", [P, FC * D])
        w1 = sb("w1", [P, 2, 2, DC, F], F32R)
        w2 = sb("w2", [P, 2, 2, FC, D], F32R)
        b1 = sb("b1", [P, 2, FC])
        b2 = sb("b2", [P, 2, D])
        gather_rows = sb("gather_rows", [P, 2, QT], I32)
        scatter_rows = sb("scatter_rows", [P, 2, QT], I32)
        scales = sb("scales", [P, 2, QT, 1])
        gates = sb("gates", [P, 2, QT])
        xe = sb("xe", [P, 2, QT, ROW])
        xeT = sb("xeT", [P, 2, DC, CAP], F32R)
        h_full = sb("h_full", [P, 2, CAP])
        h = sb("h", [P, 2, 2, FC, CAP], F32R)
        y = sb("y", [P, 2, QT, D])
        pool_pad = sb("pool_pad_c", [1, 10])
        pool_one = sb("pool_one_c", [1, 1])
        bank = [ctx.enter_context(nc.psum_tensor(f"cbank{k}", [P, 512], F32)) for k in range(7)]

        ident_loaded = sem("ident_loaded")
        w_loaded = sem("ew_loaded")
        w_high = sem("ew_high")
        w1_ready = sem("w1_ready")
        w2_ready = sem("w2_ready")
        b_loaded = [sem(f"eb_loaded{k}") for k in range(2)]
        one_ready = sem("one_ready")
        gather_rows_ready = sem("gather_rows_ready")
        scatter_rows_ready = sem("scatter_rows_ready")
        gathered = [sem(f"gathered{k}") for k in range(2)]
        xT_done = sem("exT_done")
        xT_high = sem("exT_high")
        xT_ready = sem("exT_ready")
        fc1_done = sem("fc1_done")
        gelu_ready = sem("gelu_ready")
        h_high = sem("h_high")
        h_ready = sem("h_ready")
        fc2_done = sem("fc2_done")
        y_step = sem("y_step")
        gates_ready = sem("gates_ready")
        y_ready = sem("y_ready")
        scattered = [sem(f"scattered{k}") for k in range(2)]

        def loop(engine, pair):
            pair(0)
            with engine.Fori(1, E // 2) as i:
                pair(i)

        block = ctx.enter_context(nc.Block())

        @block.sync
        def _(sp):
            sp.dma_start(ident[:], d["ident"]).then_inc(ident_loaded, 16)

            def pair(i):
                experts = [sp.snap(2 * i + k) if not isinstance(i, int) else 2 * i + k for k in range(2)]
                for k, e in enumerate(experts):
                    need(sp, w1_ready, e)
                    sp.dma_start(w1_raw[:], d["w1"][bass.ts(e, 1)].rearrange("o p n -> p (o n)")).then_inc(w_loaded, 16)
                    need(sp, w2_ready, e)
                    sp.dma_start(w2_raw[:], d["w2"][bass.ts(e, 1)].rearrange("o p n -> p (o n)")).then_inc(w_loaded, 16)
                    need(sp, y_step, QT * (e - 1))
                    sp.dma_start(b1[:, k], d["b1"][bass.ts(e, 1)].rearrange("o p n -> p (o n)")).then_inc(b_loaded[k], 16)
                    sp.dma_start(b2[:, k], d["b2"][bass.ts(e, 1)].rearrange("o n -> (o n)").partition_broadcast(P)).then_inc(b_loaded[k], 16)
            loop(sp, pair)

        @block.gpsimd
        def _(pool):
            pool.memset(pool_one[:], 1.0).then_inc(one_ready, 1)
            pool.wait_ge(one_ready, 1)
            rows_all = rows_dram.rearrange("p b n -> (p b) n")
            sum_all = sum_dram.rearrange("p b n -> (p b) n")
            scale_all = scale_dram.rearrange("p (b o) -> (p b) o", o=1)

            def hold(place):
                pool.tensor_tensor(pool_pad[:, place:place + 1], pool_one[:], pool_one[:], ALU.add)

            def gather(i, k):
                e = 2 * i + k
                if isinstance(e, int) and e >= E:
                    return
                need(pool, gathered[k], 2 * 16 * QT * i)
                need(pool, xT_ready, e - 1)
                hold(k)
                pool.tensor_copy(gather_rows[:, k], slot_rows[:, bass.ts(e, 1)].rearrange("p o q -> p (o q)")).then_inc(gather_rows_ready, 1)
                pool.wait_ge(gather_rows_ready, e + 1)
                hold(2 + k)
                for q in range(QT):
                    pool.indirect_dma_start(xe[:, k, q], None, rows_all, bass.IndirectOffsetOnAxis(ap=gather_rows[:, k, q:q + 1], axis=0)
                                            ).then_inc(gathered[k], 16)
                    pool.indirect_dma_start(scales[:, k, q], None, scale_all, bass.IndirectOffsetOnAxis(ap=gather_rows[:, k, q:q + 1], axis=0)
                                            ).then_inc(gathered[k], 16)

            def scatter(i, k):
                e = 2 * i + k
                need(pool, scattered[k], 16 * QT * i)
                hold(4 + k)
                pool.tensor_copy(scatter_rows[:, k], slot_rows[:, bass.ts(e, 1)].rearrange("p o q -> p (o q)")).then_inc(scatter_rows_ready, 1)
                need(pool, y_ready, QT * (e + 1))
                need(pool, scattered[1 - k], 16 * QT * (i + k))
                need(pool, scatter_rows_ready, e + 1)
                hold(6 + k)
                for q in range(QT):
                    pool.indirect_dma_start(sum_all, bass.IndirectOffsetOnAxis(ap=scatter_rows[:, k, q:q + 1], axis=0), y[:, k, q], None,
                                            compute_op=ALU.add).then_inc(scattered[k], 16)

            def pair(i):
                for k in range(2):
                    e = 2 * i + k
                    gather(i + k, 1 - k)
                    need(pool, w_high, 2 * e + 2)
                    pool.tensor_tensor(w2[:, k, 1].rearrange("p c n -> p (c n)"), w2_raw[:], w2[:, k, 0].rearrange("p c n -> p (c n)").bitcast(F32),
                                       ALU.subtract).then_inc(w2_ready, 1)
                    if k == 1:
                        scatter(i, 0)
                    elif not (isinstance(i, int) and i == 0):
                        scatter(i - 1, 1)
            gather(0, 0)
            pair(0)
            with pool.Fori(1, E // 2 - 1) as i:
                pair(i)
            pair(E // 2 - 1)
            scatter(E // 2 - 1, 1)
            for k in range(2):
                pool.wait_ge(scattered[k], 16 * QT * (E // 2))

        @block.tensor
        def _(pe):
            pe.wait_ge(ident_loaded, 16)

            def transpose_rows(i, k):
                e = 2 * i + k
                need(pe, gathered[k], 2 * 16 * QT * (i + 1))
                need(pe, xT_ready, e)
                last = None
                for c in range(DC):
                    for q in range(QT):
                        last = pe.transpose(bank[3 + c][:, q * P:(q + 1) * P], xe[:, k, q, c * P:(c + 1) * P], ident[:])
                last.then_inc(xT_done, 1)

            def fc1(i, k):
                e = 2 * i + k
                need(pe, xT_ready, e + 1)
                need(pe, w1_ready, e + 1)
                for m in range(FC):
                    u = FC * e + m
                    need(pe, gelu_ready, u - 1)
                    last = None
                    for s, (a, b) in enumerate(PASSES):
                        for c in range(DC):
                            last = pe.matmul(bank[m % 2][:], w1[:, k, a, c, m * P:(m + 1) * P], xeT[:, b, c, :],
                                             start=(s == 0 and c == 0), stop=(s == 2 and c == DC - 1))
                    last.then_inc(fc1_done, 1)

            def fc2(i, k):
                e = 2 * i + k
                need(pe, h_ready, FC * e + FC - 1)
                need(pe, w2_ready, e + 1)
                for q in range(QT):
                    u = QT * e + q
                    need(pe, y_step, u - 1)
                    last = None
                    for m in range(FC):
                        if q == 0 and m == FC - 1:
                            need(pe, h_ready, FC * (e + 1))
                        for s, (a, b) in enumerate(PASSES):
                            last = pe.matmul(bank[5 + q % 2][:, 0:D], h[:, k, a, m, q * P:(q + 1) * P], w2[:, k, b, m, :],
                                             start=(s == 0 and m == 0), stop=(s == 2 and m == FC - 1))
                    last.then_inc(fc2_done, 1)

            def pair(i):
                for k in range(2):
                    transpose_rows(i, k)
                    if k == 1:
                        fc2(i, 0)
                    elif not isinstance(i, int):
                        fc2(i - 1, 1)
                    fc1(i, k)
            loop(pe, pair)
            fc2(E // 2 - 1, 1)

        @block.scalar
        def _(act):
            def pair(i):
                for k in range(2):
                    e = 2 * i + k
                    need(act, xT_done, e + 1)
                    need(act, fc1_done, FC * e)
                    last = None
                    for c in range(DC):
                        last = act.activation(xeT[:, 0, c], bank[3 + c][:], ACT.Copy)
                    last.then_inc(xT_high, 1)
                    need(act, w_loaded, 32 * e + 32)
                    need(act, fc1_done, FC * (e - 1))
                    act.activation(w1[:, k, 0].rearrange("p c n -> p (c n)"), w1_raw[:], ACT.Copy).then_inc(w_high, 1)
                    need(act, fc2_done, QT * (e - 1))
                    act.activation(w2[:, k, 0].rearrange("p c n -> p (c n)"), w2_raw[:], ACT.Copy).then_inc(w_high, 1)
                    need(act, b_loaded[k], 32 * (i + 1))
                    for m in range(FC):
                        u = FC * e + m
                        need(act, fc1_done, u + 1)
                        need(act, h_ready, u - 1)
                        act.activation(h_full[:, m % 2], bank[m % 2][:], ACT.Gelu, bias=b1[:, k, m:m + 1]).then_inc(gelu_ready, 1)
            loop(act, pair)

        @block.vector
        def _(dve):
            def outputs(i, k, tiles):
                e = 2 * i + k
                need(dve, b_loaded[k], 32 * (i + 1))
                need(dve, scattered[k], 16 * QT * i)
                need(dve, gates_ready, e + 1)
                for q in tiles:
                    u = QT * e + q
                    need(dve, fc2_done, u + 1)
                    dve.tensor_tensor(y[:, k, q], bank[5 + q % 2][:, 0:D], b2[:, k], ALU.add).then_inc(y_step, 1)
                    need(dve, y_step, u + 1)
                    dve.tensor_scalar(y[:, k, q], y[:, k, q], gates[:, k, q:q + 1], None, ALU.mult).then_inc(y_ready, 1)

            def pair(i):
                for k in range(2):
                    e = 2 * i + k
                    need(dve, xT_high, e + 1)
                    dve.tensor_tensor(gates[:, k].unsqueeze(2), xe[:, k, :, bass.ds(D + e, 1)], scales[:, k], ALU.mult).then_inc(gates_ready, 1)
                    last = None
                    for c in range(DC):
                        last = dve.tensor_tensor(xeT[:, 1, c], bank[3 + c][:], xeT[:, 0, c].bitcast(F32), ALU.subtract)
                    last.then_inc(xT_ready, 1)
                    previous = (i, 0) if k == 1 else (i - 1, 1) if not isinstance(i, int) else None
                    if previous is not None:
                        outputs(*previous, range(1))
                    need(dve, w_high, 2 * e + 1)
                    dve.tensor_tensor(w1[:, k, 1].rearrange("p c n -> p (c n)"), w1_raw[:], w1[:, k, 0].rearrange("p c n -> p (c n)").bitcast(F32),
                                      ALU.subtract).then_inc(w1_ready, 1)
                    if previous is not None:
                        outputs(*previous, range(1, QT))
                    need(dve, fc2_done, QT * (e - 1))
                    for m in range(FC):
                        u = FC * e + m
                        need(dve, gelu_ready, u + 1)
                        dve.tensor_copy(h[:, k, 0, m], h_full[:, m % 2]).then_inc(h_high, 1)
                        need(dve, h_high, u + 1)
                        dve.tensor_tensor(h[:, k, 1, m], h_full[:, m % 2], h[:, k, 0, m].bitcast(F32), ALU.subtract).then_inc(h_ready, 1)
            loop(dve, pair)
            outputs(E // 2 - 1, 1, range(QT))


def finish(nc, sum_dram, out_dram):
    with ExitStack() as ctx:
        def sb(name, shape, dt=F32):
            return ctx.enter_context(nc.sbuf_tensor(name, shape, dt))

        def sem(name):
            return ctx.enter_context(nc.semaphore(name))

        S = 4
        BUFS = 4
        total = sb("total_d", [P, BUFS, S, D])
        res = sb("res_d", [P, BUFS, S, D])
        stats = sb("stats_d", [P, BUFS, S, 6])
        mv = sb("mv_d", [P, BUFS, S, 2])
        rstd = sb("rstd_d", [P, BUFS, S, 1])
        eps_col = sb("eps_d", [P, S, 1])
        minus_half = sb("minus_half_d", [P, S, 1])
        pad = sb("pad_d", [1, 1])
        loaded = [sem(f"d_loaded{k}") for k in range(BUFS)]
        consts = sem("d_consts")
        stats_made = sem("d_stats")
        var_ready = sem("d_var")
        var_eps = sem("d_var_eps")
        rstd_ready = sem("d_rstd")
        res_ready = sem("d_res")
        stored = [sem(f"d_stored{k}") for k in range(BUFS)]
        STEPS = B // S

        def loop(engine, round_of_buffers):
            round_of_buffers(0)
            with engine.Fori(1, STEPS // BUFS) as i:
                round_of_buffers(i)

        block = ctx.enter_context(nc.Block())

        @block.sync
        def _(sp):
            def round_of_buffers(i):
                for k in range(BUFS):
                    n = BUFS * i + k
                    need(sp, res_ready, S * (n - BUFS + 1))
                    sp.dma_start(total[:, k], sum_dram[:, bass.ts(n, S), :]).then_inc(loaded[k], 16)
            loop(sp, round_of_buffers)

        @block.gpsimd
        def _(pool):
            pool.memset(eps_col[:], EPS).then_inc(consts, 1)
            pool.memset(minus_half[:], -0.5).then_inc(consts, 1)
            pool.wait_ge(consts, 2)

            def round_of_buffers(i):
                for k in range(BUFS):
                    n = BUFS * i + k
                    need(pool, var_ready, S * (n + 1))
                    pool.tensor_tensor(rstd[:, k], mv[:, k, :, 1:2], eps_col[:], ALU.add).then_inc(var_eps, 1)
                    pool.wait_ge(var_eps, n + 1)
                    pool.tensor_tensor(rstd[:, k], rstd[:, k], minus_half[:], ALU.pow).then_inc(rstd_ready, 1)
            loop(pool, round_of_buffers)

        @block.scalar
        def _(act):
            def round_of_buffers(i):
                for k in range(BUFS):
                    n = BUFS * i + k
                    need(act, res_ready, S * (n + 1))
                    act.dma_start(out_dram[:, bass.ts(n, S), :], res[:, k]).then_inc(stored[k], 16)
            loop(act, round_of_buffers)
            for k in range(BUFS):
                act.wait_ge(stored[k], 16 * (STEPS // BUFS))

        @block.vector
        def _(dve):
            def normalise(i, k):
                n = BUFS * i + k
                need(dve, rstd_ready, n + 1)
                need(dve, stored[k], 16 * i)
                for s in range(S):
                    dve.tensor_scalar(res[:, k, s], total[:, k, s], mv[:, k, s, 0:1], rstd[:, k, s], ALU.subtract, ALU.mult).then_inc(res_ready, 1)

            def round_of_buffers(i):
                for k in range(BUFS):
                    n = BUFS * i + k
                    need(dve, loaded[k], 16 * (i + 1))
                    for s in range(S):
                        dve.bn_stats(stats[:, k, s], total[:, k, s]).then_inc(stats_made, 1)
                    need(dve, stats_made, S * (n + 1))
                    dve.memset(pad[:], 0.0)
                    for s in range(S):
                        dve.bn_aggr(mv[:, k, s], stats[:, k, s]).then_inc(var_ready, 1)
                    if k > 0:
                        normalise(i, k - 1)
                    elif not isinstance(i, int):
                        normalise(i - 1, BUFS - 1)
            loop(dve, round_of_buffers)
            normalise(STEPS // BUFS - 1, BUFS - 1)


def decoder_layer(nc, d, x2_dram, rows_dram, logits_dram, scale_dram, slots_dram, out_dram):
    with ExitStack() as ctx:
        probs = ctx.enter_context(nc.sbuf_tensor("probs", [P, B, E], F32))
        slot_rows = ctx.enter_context(nc.sbuf_tensor("slot_rows", [P, E, QT], I32))
        decoder_attention(nc, d, x2_dram, rows_dram, logits_dram, probs)
        choose_tokens(nc, d, logits_dram, slots_dram, scale_dram, probs, slot_rows)
        run_experts(nc, d, rows_dram, scale_dram, x2_dram, slot_rows)
        finish(nc, x2_dram, out_dram)


def _by_row_chunk(w):
    import numpy as np
    rows, cols = w.shape
    return np.ascontiguousarray(w.reshape(rows // P, P, cols).transpose(1, 0, 2))


def _in_every_partition(v):
    import numpy as np
    return np.ascontiguousarray(np.broadcast_to(v, (P, v.shape[-1])))


def _rope_tables():
    import numpy as np
    half = HD // 2
    theta = (1.0 / 10000.0 ** (np.arange(half, dtype=np.float32) / half)).astype(np.float32)
    ang = np.arange(T, dtype=np.float32)[:, None] * theta[None, :]
    scale = np.repeat(np.array([HD ** -0.5, 1.0], np.float32), H)
    return [np.ascontiguousarray(f(ang).astype(np.float32)[:, None, :] * scale[None, :, None]) for f in (np.cos, np.sin)]


def _layout(v):
    import numpy as np

    def flat(a):
        return np.ascontiguousarray(a.reshape(a.shape[0], -1))

    order = np.arange(D).reshape(H, HD // 2, 2).transpose(0, 2, 1).reshape(-1)
    wt = {k: _by_row_chunk(v[k].T) for k in v if "_W" in k and k != "L0_xattn_Wg"}
    cross = ["Wq_c", "Wk_c", "Wk_s", "Wq_s"]
    cos, sin = _rope_tables()
    a = {
        "x": np.ascontiguousarray(v["x"].transpose(1, 0, 2)),
        "xT": _by_row_chunk(v["x"].reshape(-1, D).T),
        "cT": _by_row_chunk(v["ctx_1024"].reshape(-1, D).T),
        "wqk": flat(np.concatenate([wt["L0_attn_W_q"][:, :, order], wt["L0_attn_W_k"][:, :, order]], axis=2)),
        "wv": flat(wt["L0_attn_W_v"]),
        "wo": flat(wt["L0_attn_W_o"]),
        "wx": flat(np.stack([wt["L0_xattn_" + n] for n in cross], axis=1)),
        "wxv": flat(np.stack([wt["L0_xattn_Wv_s"], wt["L0_xattn_Wv_c"]], axis=1)),
        "wg": flat(_by_row_chunk(v["L0_xattn_Wg"].T)),
        "wr": _by_row_chunk(v["L0_ffn_router_weight"].T),
        "bqkv": _in_every_partition(np.concatenate([v["L0_attn_b_q"][order], v["L0_attn_b_k"][order], v["L0_attn_b_v"]])),
        "bo": _in_every_partition(v["L0_attn_b_o"]),
        "bx": np.ascontiguousarray(np.stack([v["L0_xattn_b" + n[1:]].reshape(DC, P).T for n in cross], axis=1)),
        "bxv": _in_every_partition(np.concatenate([v["L0_xattn_bv_s"], v["L0_xattn_bv_c"]])),
        "bg": _in_every_partition(v["L0_xattn_bg"]),
        "nw": _in_every_partition(v["L0_ffn_norm_weight"]),
        "br": _in_every_partition(v["L0_ffn_router_bias"]),
        "rope_cos": cos,
        "rope_sin": sin,
        "w1": np.stack([flat(_by_row_chunk(w.T)) for w in v["L0_ffn_fc1_weight"]]),
        "w2": np.stack([flat(_by_row_chunk(w.T)) for w in v["L0_ffn_fc2_weight"]]),
        "b1": np.ascontiguousarray(v["L0_ffn_fc1_bias"].reshape(E, FC, P).transpose(0, 2, 1)),
        "b2": np.ascontiguousarray(v["L0_ffn_fc2_bias"]),
    }
    expert, chunk = np.divmod(np.arange(P), CHUNKS)
    like = expert[:, None] == expert[None, :]
    a["ident"] = np.eye(P, dtype=np.float32)
    a["same_expert"] = like.astype(np.float32)
    a["earlier_chunk"] = (like & (chunk[:, None] < chunk[None, :])).astype(np.float32)
    a["token_no"] = np.arange(P, dtype=np.float32)[:, None]
    a["batch_no"] = _in_every_partition(np.arange(B, dtype=np.float32))
    a["combine"] = np.concatenate([B * np.eye(SLOT_HI), np.eye(SLOT_HI)]).astype(np.float32)
    return a


def kernel(**inputs):
    import numpy as np
    import concourse.bacc as bacc
    from concourse.bass_utils import run_bass_kernel_spmd as run

    arrays = _layout({name: np.asarray(a) for name, a in inputs.items()})
    nc = bacc.Bacc("TRN2", target_bir_lowering=False, num_devices=1)
    d = {name: nc.dram_tensor(f"in_{name}", a.shape, mybir.dt.from_np(a.dtype), kind="ExternalInput").ap()
         for name, a in arrays.items()}
    x2 = nc.dram_tensor("x2_rows", (P, B, D), F32).ap()
    rows = nc.dram_tensor("normed_rows", (P, B, ROW), F32).ap()
    logits = nc.dram_tensor("logits", (E, N), F32).ap()
    scale = nc.dram_tensor("gate_scale_rows", (P, B), F32).ap()
    slots = nc.dram_tensor("slots", (E, CAP), I32).ap()
    out = nc.dram_tensor("out_0", (P, B, D), F32, kind="ExternalOutput").ap()
    decoder_layer(nc, d, x2, rows, logits, scale, slots, out)
    r = run(nc, [{f"in_{name}": a for name, a in arrays.items()}], core_ids=[0])
    return np.ascontiguousarray(r.results[0]["out_0"].transpose(1, 0, 2))
```
